# Optimizing a Trainium2 kernel written in Bass

```python
import numpy as np
import jax
import jax.numpy as jnp

def _softmax(x, axis=-1):
    return jax.nn.softmax(x, axis=axis)

def _gelu(x):
    return jax.nn.gelu(x, approximate=True)

def _silu(x):
    return jax.nn.silu(x)

def _sigmoid(x):
    return jax.nn.sigmoid(x)

def _layernorm(x, axis=-1, eps=1e-05):
    m = jnp.mean(x, axis=axis, keepdims=True)
    v = jnp.var(x, axis=axis, keepdims=True)
    return (x - m) / jnp.sqrt(v + eps)

def _scatter_add(tgt, idx, src, axis=0):
    return tgt.at[idx].add(src)

def _segment_sum(src, seg, n):
    return jax.ops.segment_sum(src, seg, n)
kernel_name = 'mk_gnn_resnorm_d4_gnn_r16_9bc49c'

def setup_inputs(seed: int=0):
    np.random.seed(seed)
    _w = jnp.asarray

    def _rec_inputs():
        import jax
        import jax.numpy as jnp
        _gk = jax.random.key(seed)
        x = -0.0003713 + 1 * jax.random.normal(jax.random.fold_in(_gk, 1), (3125, 128), jnp.float32)
        src = jax.random.randint(jax.random.fold_in(_gk, 2), (50000,), 0, 3125, jnp.int32)
        dst = jax.random.randint(jax.random.fold_in(_gk, 3), (50000,), 0, 3125, jnp.int32)
        _o = jnp.argsort(dst, stable=True)
        src = src[_o]
        dst = dst[_o]
        edge_attr_128 = -5.16925e-05 + 1.00005 * jax.random.normal(jax.random.fold_in(_gk, 11), (50000, 128), jnp.float32)
        edge_weight = jax.random.uniform(jax.random.fold_in(_gk, 13), (50000,), jnp.float32, 0.0, 0.999999)
        return (x, src, dst, edge_attr_128, edge_weight)
    x, src, dst, edge_attr_128, edge_weight = _rec_inputs()

    def _L0_gnn_setup():
        import jax, jax.numpy as jnp
        import numpy as np
        N = 6250
        E = 100000
        D = 128

        def _gcn_layer(x, src, dst, ew, W, b):
            n = x.shape[0]
            loop = jnp.arange(n)
            s = jnp.concatenate([src, loop])
            d = jnp.concatenate([dst, loop])
            w = jnp.concatenate([ew, jnp.ones((n,), ew.dtype)])
            deg = jax.ops.segment_sum(w, d, num_segments=n)
            dinv = jnp.where(deg > 0, jax.lax.rsqrt(deg), 0.0)
            norm = dinv[s] * w * dinv[d]
            h = x @ W
            out = jax.ops.segment_sum(h[s] * norm[:, None], d, num_segments=n)
            return out + b
        key = jax.random.key(seed)
        ks = jax.random.split(key, 10)
        s = 1.0 / np.sqrt(D)
        inp = {'x': jax.random.normal(ks[0], (N, D), jnp.float32), 'edge_index': jax.random.randint(ks[1], (2, E), 0, N, dtype=jnp.int64), 'edge_weight': jax.random.uniform(ks[2], (E,), jnp.float32), 'W1': jax.random.normal(ks[3], (D, D), jnp.float32) * s, 'b1': jnp.zeros((D,), jnp.float32), 'W2': jax.random.normal(ks[4], (D, D), jnp.float32) * s, 'b2': jnp.zeros((D,), jnp.float32), 'W3': jax.random.normal(ks[5], (D, D), jnp.float32) * s, 'b3': jnp.zeros((D,), jnp.float32)}
        return inp
    _L0_gnn_all = _L0_gnn_setup()
    _L0_gnn_in = {k: v for k, v in _L0_gnn_all.items() if k in ('W1', 'b1', 'W2', 'b2', 'W3', 'b3')}
    del _L0_gnn_all

    def _L1_gnn_setup():
        import jax, jax.numpy as jnp
        import numpy as np
        N_NODES = 6250
        N_EDGES = 100000
        IN_F = 128
        HEADS = 4
        OUT_F = 32
        NEG_SLOPE = 0.2

        def _xavier(key, shape):
            fan_in, fan_out = (shape[0], shape[-1])
            if len(shape) == 3:
                fan_in, fan_out = (1, shape[1] * shape[2])
            limit = float(np.sqrt(6.0 / (fan_in + fan_out)))
            return jax.random.uniform(key, shape, jnp.float32, -limit, limit)
        key = jax.random.key(seed)
        k_feat, k_ei, k_wl, k_wr, k_att = jax.random.split(key, 5)
        features = jax.random.normal(k_feat, (N_NODES, IN_F), jnp.float32)
        edge_index = jax.random.randint(k_ei, (2, N_EDGES), 0, N_NODES, jnp.int64)
        weight_l = _xavier(k_wl, (IN_F, HEADS * OUT_F))
        weight_r = _xavier(k_wr, (IN_F, HEADS * OUT_F))
        att = _xavier(k_att, (1, HEADS, OUT_F))
        bias = jnp.zeros((HEADS * OUT_F,), jnp.float32)
        return {'features': features, 'edge_index': edge_index, 'weight_l': weight_l, 'weight_r': weight_r, 'att': att, 'bias': bias}
    _L1_gnn_all = _L1_gnn_setup()
    _L1_gnn_in = {k: v for k, v in _L1_gnn_all.items() if k in ('weight_l', 'weight_r', 'att', 'bias')}
    del _L1_gnn_all

    def _L2_gnn_setup():
        import jax, jax.numpy as jnp
        import numpy as np
        N_NODES = 3125
        N_EDGES = 50000
        C = 128
        D = 128
        Z = 2 * C + D
        key = jax.random.key(seed)
        ks = jax.random.split(key, 7)
        x = jax.random.normal(ks[0], (N_NODES, C), dtype=jnp.float32)
        edge_index = jax.random.randint(ks[1], (2, N_EDGES), 0, N_NODES, dtype=jnp.int64)
        edge_attr = jax.random.normal(ks[2], (N_EDGES, D), dtype=jnp.float32)
        s = 1.0 / np.sqrt(Z)
        W_f = jax.random.uniform(ks[3], (Z, C), dtype=jnp.float32, minval=-s, maxval=s)
        b_f = jax.random.uniform(ks[4], (C,), dtype=jnp.float32, minval=-s, maxval=s)
        W_s = jax.random.uniform(ks[5], (Z, C), dtype=jnp.float32, minval=-s, maxval=s)
        b_s = jax.random.uniform(ks[6], (C,), dtype=jnp.float32, minval=-s, maxval=s)
        return {'x': x, 'edge_index': edge_index, 'edge_attr': edge_attr, 'W_f': W_f, 'b_f': b_f, 'W_s': W_s, 'b_s': b_s}
    _L2_gnn_all = _L2_gnn_setup()
    _L2_gnn_in = {k: v for k, v in _L2_gnn_all.items() if k in ('W_f', 'b_f', 'W_s', 'b_s')}
    del _L2_gnn_all

    def _L3_gnn_setup():
        import jax, jax.numpy as jnp
        import numpy as np
        LN_EPS = 1e-05

        def _layernorm(h, g, b):
            mu = jnp.mean(h, axis=-1, keepdims=True)
            var = jnp.mean(jnp.square(h - mu), axis=-1, keepdims=True)
            return (h - mu) * jax.lax.rsqrt(var + LN_EPS) * g + b
        key = jax.random.key(seed)
        ks = jax.random.split(key, 8)
        N, E, D, L = (6250, 100000, 128, 10)
        x = jax.random.normal(ks[0], (N, D), dtype=jnp.float32)
        edge_index = jax.random.randint(ks[1], (2, E), 0, N, dtype=jnp.int32)
        edge_weight = jax.random.uniform(ks[2], (E,), dtype=jnp.float32)
        s = 1.0 / np.sqrt(D)
        conv_W = jax.random.normal(ks[3], (L, D, D), dtype=jnp.float32) * s
        conv_b = jnp.zeros((L, D), jnp.float32)
        ln_g = jnp.ones((L, D), jnp.float32)
        ln_b = jnp.zeros((L, D), jnp.float32)
        res_W = jax.random.normal(ks[4], (D, D), dtype=jnp.float32) * s
        res_b = jnp.zeros((D,), jnp.float32)
        res_g = jnp.ones((D,), jnp.float32)
        res_beta = jnp.zeros((D,), jnp.float32)
        return dict(x=x, edge_index=edge_index, edge_weight=edge_weight, conv_W=conv_W, conv_b=conv_b, ln_g=ln_g, ln_b=ln_b, res_W=res_W, res_b=res_b, res_g=res_g, res_beta=res_beta)
    _L3_gnn_all = _L3_gnn_setup()
    _L3_gnn_in = {k: v for k, v in _L3_gnn_all.items() if k in ('conv_W', 'conv_b', 'ln_g', 'ln_b', 'res_W', 'res_b', 'res_g', 'res_beta')}
    del _L3_gnn_all
    return {'x': x, 'src': src, 'dst': dst, 'edge_attr_128': edge_attr_128, 'edge_weight': edge_weight, 'L0_gnn_W1': _L0_gnn_in['W1'], 'L0_gnn_b1': _L0_gnn_in['b1'], 'L0_gnn_W2': _L0_gnn_in['W2'], 'L0_gnn_b2': _L0_gnn_in['b2'], 'L0_gnn_W3': _L0_gnn_in['W3'], 'L0_gnn_b3': _L0_gnn_in['b3'], 'L1_gnn_weight_l': _L1_gnn_in['weight_l'], 'L1_gnn_weight_r': _L1_gnn_in['weight_r'], 'L1_gnn_att': _L1_gnn_in['att'], 'L1_gnn_bias': _L1_gnn_in['bias'], 'L2_gnn_W_f': _L2_gnn_in['W_f'], 'L2_gnn_b_f': _L2_gnn_in['b_f'], 'L2_gnn_W_s': _L2_gnn_in['W_s'], 'L2_gnn_b_s': _L2_gnn_in['b_s'], 'L3_gnn_conv_W': _L3_gnn_in['conv_W'], 'L3_gnn_conv_b': _L3_gnn_in['conv_b'], 'L3_gnn_ln_g': _L3_gnn_in['ln_g'], 'L3_gnn_ln_b': _L3_gnn_in['ln_b'], 'L3_gnn_res_W': _L3_gnn_in['res_W'], 'L3_gnn_res_b': _L3_gnn_in['res_b'], 'L3_gnn_res_g': _L3_gnn_in['res_g'], 'L3_gnn_res_beta': _L3_gnn_in['res_beta']}

def reference(x, src, dst, edge_attr_128, edge_weight, L0_gnn_W1, L0_gnn_b1, L0_gnn_W2, L0_gnn_b2, L0_gnn_W3, L0_gnn_b3, L1_gnn_weight_l, L1_gnn_weight_r, L1_gnn_att, L1_gnn_bias, L2_gnn_W_f, L2_gnn_b_f, L2_gnn_W_s, L2_gnn_b_s, L3_gnn_conv_W, L3_gnn_conv_b, L3_gnn_ln_g, L3_gnn_ln_b, L3_gnn_res_W, L3_gnn_res_b, L3_gnn_res_g, L3_gnn_res_beta):
    import jax
    import jax.numpy as jnp

    def _L0_gnn_ref(x, edge_index, edge_weight, W1, b1, W2, b2, W3, b3):
        import jax, jax.numpy as jnp
        import numpy as np
        N = 6250
        E = 100000
        D = 128

        def _gcn_layer(x, src, dst, ew, W, b):
            n = x.shape[0]
            loop = jnp.arange(n)
            s = jnp.concatenate([src, loop])
            d = jnp.concatenate([dst, loop])
            w = jnp.concatenate([ew, jnp.ones((n,), ew.dtype)])
            deg = jax.ops.segment_sum(w, d, num_segments=n)
            dinv = jnp.where(deg > 0, jax.lax.rsqrt(deg), 0.0)
            norm = dinv[s] * w * dinv[d]
            h = x @ W
            out = jax.ops.segment_sum(h[s] * norm[:, None], d, num_segments=n)
            return out + b
        src, dst = (edge_index[0], edge_index[1])
        for W, b in ((W1, b1), (W2, b2), (W3, b3)):
            x = jax.nn.relu(_gcn_layer(x, src, dst, edge_weight, W, b))
        return x

    def _L1_gnn_ref(features, edge_index, weight_l, weight_r, att, bias):
        import jax, jax.numpy as jnp
        import numpy as np
        N_NODES = 6250
        N_EDGES = 100000
        IN_F = 128
        HEADS = 4
        OUT_F = 32
        NEG_SLOPE = 0.2

        def _xavier(key, shape):
            fan_in, fan_out = (shape[0], shape[-1])
            if len(shape) == 3:
                fan_in, fan_out = (1, shape[1] * shape[2])
            limit = float(np.sqrt(6.0 / (fan_in + fan_out)))
            return jax.random.uniform(key, shape, jnp.float32, -limit, limit)
        num_nodes = features.shape[0]
        src, tgt = (edge_index[0], edge_index[1])
        h_l = (features @ weight_l).reshape(num_nodes, HEADS, OUT_F)
        h_r = (features @ weight_r).reshape(num_nodes, HEADS, OUT_F)
        x_i = h_l[tgt]
        x_j = h_r[src]
        e = jnp.sum(jax.nn.leaky_relu(x_i + x_j, NEG_SLOPE) * att, axis=-1)
        seg_max = jax.ops.segment_max(e, tgt, num_segments=num_nodes)
        exp_e = jnp.exp(e - seg_max[tgt])
        seg_sum = jax.ops.segment_sum(exp_e, tgt, num_segments=num_nodes)
        alpha = exp_e / jnp.clip(seg_sum[tgt], 1e-16)
        messages = x_j * alpha[..., None]
        out = jax.ops.segment_sum(messages, tgt, num_segments=num_nodes)
        out = out.reshape(num_nodes, HEADS * OUT_F) + bias
        return out

    def _L2_gnn_ref(x, edge_index, edge_attr, W_f, b_f, W_s, b_s):
        import jax, jax.numpy as jnp
        import numpy as np
        N_NODES = 3125
        N_EDGES = 50000
        C = 128
        D = 128
        Z = 2 * C + D
        src = edge_index[0]
        dst = edge_index[1]
        z = jnp.concatenate([x[dst], x[src], edge_attr], axis=-1)
        gate = jax.nn.sigmoid(z @ W_f + b_f)
        core = jax.nn.softplus(z @ W_s + b_s)
        msg = gate * core
        agg = jax.ops.segment_sum(msg, dst, num_segments=x.shape[0])
        return x + agg

    def _L3_gnn_ref(x, edge_index, edge_weight, conv_W, conv_b, ln_g, ln_b, res_W, res_b, res_g, res_beta):
        import jax, jax.numpy as jnp
        import numpy as np
        LN_EPS = 1e-05

        def _layernorm(h, g, b):
            mu = jnp.mean(h, axis=-1, keepdims=True)
            var = jnp.mean(jnp.square(h - mu), axis=-1, keepdims=True)
            return (h - mu) * jax.lax.rsqrt(var + LN_EPS) * g + b
        N = x.shape[0]
        identity = jax.nn.gelu(_layernorm(x @ res_W + res_b, res_g, res_beta), approximate=False)
        loop = jnp.arange(N, dtype=edge_index.dtype)
        row = jnp.concatenate([edge_index[0], loop])
        col = jnp.concatenate([edge_index[1], loop])
        w = jnp.concatenate([edge_weight, jnp.ones((N,), edge_weight.dtype)])
        deg = jax.ops.segment_sum(w, col, num_segments=N)
        dis = jnp.where(deg > 0, jax.lax.rsqrt(jnp.maximum(deg, 1e-30)), 0.0)
        norm = dis[row] * w * dis[col]

        def layer(out, params):
            W, b, g, beta = params
            h = out @ W
            msg = h[row] * norm[:, None]
            agg = jax.ops.segment_sum(msg, col, num_segments=N) + b
            out = jax.nn.gelu(_layernorm(agg, g, beta), approximate=False)
            return (out, None)
        out, _ = jax.lax.scan(layer, x, (conv_W, conv_b, ln_g, ln_b))
        return out + identity
    edge_index = jnp.stack([src, dst])
    x = _layernorm(x + _L0_gnn_ref(x, edge_index, edge_weight, L0_gnn_W1, L0_gnn_b1, L0_gnn_W2, L0_gnn_b2, L0_gnn_W3, L0_gnn_b3), axis=-1)
    x = _layernorm(x + _L1_gnn_ref(x, edge_index, L1_gnn_weight_l, L1_gnn_weight_r, L1_gnn_att, L1_gnn_bias), axis=-1)
    x = _layernorm(x + _L2_gnn_ref(x, edge_index, edge_attr_128, L2_gnn_W_f, L2_gnn_b_f, L2_gnn_W_s, L2_gnn_b_s), axis=-1)
    x = _layernorm(x + _L3_gnn_ref(x, edge_index, edge_weight, L3_gnn_conv_W, L3_gnn_conv_b, L3_gnn_ln_g, L3_gnn_ln_b, L3_gnn_res_W, L3_gnn_res_b, L3_gnn_res_g, L3_gnn_res_beta), axis=-1)
    return x

_drawn_inputs = setup_inputs


def setup_inputs(seed=0):
    import zlib

    import numpy as np

    out = dict(_drawn_inputs(seed))
    spreads = {'L0_gnn_b1': (0.0, 0.1),
     'L0_gnn_b2': (0.0, 0.1),
     'L0_gnn_b3': (0.0, 0.1),
     'L1_gnn_bias': (0.0, 0.1),
     'L3_gnn_conv_b': (0.0, 0.1),
     'L3_gnn_ln_g': (1.0, 0.2),
     'L3_gnn_ln_b': (0.0, 0.1),
     'L3_gnn_res_b': (0.0, 0.1),
     'L3_gnn_res_g': (1.0, 0.2),
     'L3_gnn_res_beta': (0.0, 0.1)}
    factors = {}
    for name, (base, spread) in spreads.items():
        noise = np.random.default_rng([zlib.crc32(name.encode()), seed]).standard_normal(out[name].shape)
        drawn = base * np.exp(spread * noise) if base else spread * noise
        out[name] = jnp.asarray(drawn.astype(out[name].dtype))
    for name, factor in factors.items():
        out[name] = (out[name] * factor).astype(out[name].dtype)
    return out
```

```python
import numpy as np
import concourse.bass as bass
from concourse import mybir

F32 = mybir.dt.float32
I32 = mybir.dt.int32
ALU = mybir.AluOpType
ACT = mybir.ActivationFunctionType
AX = mybir.AxisListType

N = 3125
E = 50000
D = 128
T = 125
NS = N // T
G = 25
NG = N // G
Q = 4
EB = 128 * Q
UM = -(-E // EB) + NG
UM += UM % 2
UT = UM + 2
ER = T
EC = E // ER
BIG = 1.0e6


def wait_alone(eng, c, sem, value):
    eng.wait_ge(sem, value)
    eng.sem_inc(c["ticks"], 1)


class Order:

    def __init__(self, eng, sem):
        self.eng, self.sem, self.n, self.base = eng, sem, 0, 0

    def link(self, ins):
        ins.then_inc(self.sem, 1)
        self.n += 1
        self.eng.wait_ge(self.sem, self.base + self.n)


class Semaphores:

    def __init__(self, nc):
        self.nc, self.taken, self.c, self.stages = nc, [], {}, 0

    def take(self, name):
        self.taken.append(self.nc.alloc_semaphore(name))
        return self.taken[-1]

    def begin(self, c):
        self.c = c
        self.stages += 1
        c["ticks"] = self.take(f"ticks_{self.stages}")

    def end(self):
        self.nc.clear_and_free_semaphores(self.taken)
        self.nc.all_engine_barrier()
        self.taken = []
        self.begin(self.c)


def dram_scratch(nc):
    return {
        "edges": nc.dram_tensor("edge_list", [E + EB, 4], I32).ap(),
        "adj": nc.dram_tensor("adjacency", [NG, 128, NS * G], F32).ap(),
        "dinv": nc.dram_tensor("dinv_row", [N], F32).ap(),
        "h_l": nc.dram_tensor("gat_target_rows", [N, D], F32).ap(),
        "h_r": nc.dram_tensor("gat_source_rows", [N, D], F32).ap(),
        "gat": nc.dram_tensor("gat_out", [N, D], F32).ap(),
        "p_dst": nc.dram_tensor("gate_target_rows", [N, 2 * D], F32).ap(),
        "p_src": nc.dram_tensor("gate_source_rows", [N, 2 * D], F32).ap(),
        "agg_t": nc.dram_tensor("gate_sum_t", [128, N], F32).ap(),
    }


def constants(nc, c):
    s_c = c["sems"].take("constants_step")
    with nc.Block() as block:
        @block.gpsimd
        def _(pool):
            o = Order(pool, s_c)
            nc.gpsimd.iota(c["ramp_i"][:, :], [[1, 640]], base=0, channel_multiplier=0)
            nc.gpsimd.iota(c["lane_i"][:, :], [[0, 1]], base=0, channel_multiplier=1)
            nc.gpsimd.memset(c["ones"][:, :], 1.0)
            nc.gpsimd.memset(c["ident"][:, :], 0.0)
            o.link(nc.gpsimd.memset(c["mean_w"][:, :], 1.0 / D))
            o.link(nc.gpsimd.tensor_copy(c["ramp"][:, :], c["ramp_i"][:, :]))
            o.link(nc.gpsimd.tensor_copy(c["lane"][:, :], c["lane_i"][:, :]))
            o.link(nc.gpsimd.affine_select(out=c["ident"][:, :], in_=c["ident"][:, :], compare_op=ALU.not_equal,
                                           fill=1.0, base=0, pattern=[[-1, 128]], channel_multiplier=1))


def prepare(nc, c, d, x_src, x_dst, x_w):
    s_ld = c["sems"].take("edge_inputs_loaded")
    s_st = c["sems"].take("edge_list_stored")
    s_v = c["sems"].take("prepare_vector_step")
    s_p = c["sems"].take("prepare_pool_step")
    s_il = c["sems"].take("edge_list_interleaved")
    s_row = c["sems"].take("search_rows_gathered")
    s_ask = c["sems"].take("search_rows_known")
    s_in = c["sems"].take("prepare_matmul_operand")
    s_mm = c["sems"].take("prepare_matmul_done")
    s_tab = c["sems"].take("block_tables_ready")
    s_blk = [c["sems"].take(f"edge_blocks_loaded_{k}") for k in range(2)]

    def sb(name, shape, dt=F32):
        return ctx.enter_context(nc.sbuf_tensor(name, shape, dt))

    from contextlib import ExitStack
    with ExitStack() as ctx:
        ei = sb("edge_in", [ER, 3, EC], I32)
        el = sb("edge_rows", [ER, EC, 4], I32)
        pad = sb("edge_pad", [128, Q, 4], I32)
        thr = sb("group_threshold", [128, NG + 1])
        first = sb("row_first", [ER, 1])
        below = sb("rows_below", [ER, NG + 1])
        rowf = sb("search_row_f", [NG + 1, 1])
        rowi = sb("search_row_i", [NG + 1, 1], I32)
        found = sb("search_rows", [NG + 1, EC], I32)
        foundf = sb("search_rows_f", [NG + 1, EC])
        thrp = sb("own_threshold", [NG + 1, 1])
        cnt = sb("below_in_row", [NG + 1, 1])
        start = sb("group_start", [NG + 1, 1])
        up = sb("next_minus_own", [NG + 1, NG])
        down = sb("own_minus_previous", [NG, NG])
        before = sb("earlier_groups", [NG, NG])
        ramp512 = sb("block_sizes", [NG, UM])
        size = sb("group_size", [NG, 1])
        nblk = sb("group_blocks", [NG, 1])
        hits = sb("threshold_hits", [128, EC])
        base = sb("group_first_block", [NG, 1])
        v = sb("block_edge_offset", [NG, 1])
        dv = sb("block_edge_step", [NG, 1])
        begun = sb("group_begun", [NG, UT])
        begun_v = sb("group_begun_edges", [NG, UT])
        gof = sb("block_group", [128, UT])
        e0f = sb("block_first_edge_f", [128, UT])
        e0r = sb("block_ramp_edges", [128, UT])
        e0i = c["first_i"]
        prs = sb("pairs_f", [1, 2])
        ps = ctx.enter_context(nc.psum_tensor("prep_psum", [128, 2, 512], F32))
        meta = sb("edge_blocks", [128, UT * Q, 4], I32)
        tmp = sb("edge_tmp", [128, UT * Q])
        tmpi = sb("edge_tmp_i", [128, UT * Q], I32)
        sq = sb("edge_src_tile", [128, UT * Q])

        block = ctx.enter_context(nc.Block())

        def load_blocks(eng, k):
            eng.wait_ge(s_tab, 1)
            eng.wait_ge(s_st, 32)
            pairs = eng.value_load(c["pairs_i"][0:1, 0:1], min_val=1, max_val=UM // 2)
            with eng.Fori(0, pairs) as i:
                e0 = eng.value_load(e0i[0:1, bass.ds(2 * i + k, 1)], min_val=0, max_val=E)
                eng.dma_start(meta[:, bass.ds((2 * i + k) * Q, Q), :],
                              d["edges"][bass.ds(e0, EB), :].rearrange("(p q) w -> p q w", q=Q)).then_inc(s_blk[k], 16)
            wait_alone(eng, c, s_blk[k], pairs * 16)

        @block.sync
        def _(sp):
            sp.dma_start(ei[:, 0, :], x_src.rearrange("(p c) -> p c", p=ER)).then_inc(s_ld, 16)
            sp.dma_start(ei[:, 1, :], x_dst.rearrange("(p c) -> p c", p=ER)).then_inc(s_ld, 16)
            sp.dma_start(ei[:, 2, :], x_w.bitcast(I32).rearrange("(p c) -> p c", p=ER)).then_inc(s_ld, 16)
            sp.wait_ge(s_il, 1)
            sp.dma_start(d["edges"][0:E, :].rearrange("(p c) w -> p (c w)", p=ER), el[:, :, :].rearrange("p c w -> p (c w)")).then_inc(s_st, 16)
            sp.dma_start(d["edges"][E:E + EB, :].rearrange("(p c) w -> p (c w)", p=128), pad[:, :, :].rearrange("p c w -> p (c w)")).then_inc(s_st, 16)
            load_blocks(sp, 0)

        @block.scalar
        def _(act):
            load_blocks(act, 1)

        @block.gpsimd
        def _(pool):
            o = Order(pool, s_p)
            nc.gpsimd.memset(meta[:, :, :], 0)
            nc.gpsimd.memset(up[:, :], 0.0)
            nc.gpsimd.memset(down[:, :], 0.0)
            nc.gpsimd.memset(before[:, :], 1.0)
            nc.gpsimd.memset(pad[:, :, :], 0)
            nc.gpsimd.iota(tmpi[:, 0:NG + 1], [[G, NG + 1]], base=0, channel_multiplier=0)
            nc.gpsimd.iota(tmpi[0:NG, 256:256 + UM], [[EB, UM]], base=EB, channel_multiplier=0)
            o.link(nc.gpsimd.iota(tmpi[:, 512:512 + UT], [[EB, UT]], base=0, channel_multiplier=0))
            nc.gpsimd.tensor_copy(thr[:, :], tmpi[:, 0:NG + 1])
            nc.gpsimd.tensor_copy(ramp512[:, :], tmpi[0:NG, 256:256 + UM])
            nc.gpsimd.tensor_copy(e0r[:, :], tmpi[:, 512:512 + UT])
            nc.gpsimd.memset(pad[:, :, 1:2], N + G)
            o.link(nc.gpsimd.tensor_scalar(thrp[:, :], c["lane"][0:NG + 1, :], float(G), 0.0, ALU.mult, ALU.add))
            o.link(nc.gpsimd.affine_select(out=up[:, :], in_=up[:, :], compare_op=ALU.not_equal, fill=1.0,
                                           base=-1, pattern=[[-1, NG]], channel_multiplier=1))
            o.link(nc.gpsimd.affine_select(out=up[:, :], in_=up[:, :], compare_op=ALU.not_equal, fill=-1.0,
                                           base=0, pattern=[[-1, NG]], channel_multiplier=1))
            o.link(nc.gpsimd.affine_select(out=down[:, :], in_=down[:, :], compare_op=ALU.not_equal, fill=1.0,
                                           base=0, pattern=[[-1, NG]], channel_multiplier=1))
            o.link(nc.gpsimd.affine_select(out=down[:, :], in_=down[:, :], compare_op=ALU.not_equal, fill=-1.0,
                                           base=1, pattern=[[-1, NG]], channel_multiplier=1))
            o.link(nc.gpsimd.affine_select(out=before[:, :], in_=before[:, :], compare_op=ALU.is_gt, fill=0.0,
                                           base=0, pattern=[[1, NG]], channel_multiplier=-1))
            pool.wait_ge(s_ask, 1)
            pool.indirect_dma_start(found[:, :], None, x_dst.rearrange("(p c) -> p c", p=ER),
                                    bass.IndirectOffsetOnAxis(ap=rowi[:, 0:1], axis=0)).then_inc(s_row, 16)
            pool.wait_ge(s_row, 16)

        @block.tensor
        def _(pe):
            steps = [(ps[0:NG + 1, 0, 0:1], below[:, :], c["ones"][0:ER, 0:1]),
                     (ps[0:NG, 1, 0:1], up[:, :], start[:, :]),
                     (ps[0:NG, 0, 0:1], before[:, :], nblk[:, :]),
                     (ps[0:1, 1, 0:1], nblk[:, :], c["ones"][0:NG, 0:1]),
                     (ps[0:NG, 0, 0:1], down[:, :], v[:, :]),
                     (ps[:, 1, 0:UT], c["ones"][0:NG, :], begun[:, :]),
                     (ps[:, 0, 0:UT], c["ones"][0:NG, :], begun_v[:, :])]
            pe.wait_ge(s_p, 7)
            for n, (out, lhs, rhs) in enumerate(steps):
                pe.wait_ge(s_in, n + 1)
                nc.tensor.matmul(out, lhs, rhs, start=True, stop=True).then_inc(s_mm, 1)

        @block.vector
        def _(dve):
            o = Order(dve, s_v)
            vec = nc.vector
            dve.wait_ge(s_ld, 48)
            dve.wait_ge(s_p, 2)
            for w in range(3):
                vec.tensor_copy(el[:, :, w], ei[:, w, :])
            vec.memset(el[:, :, 3:4], 0).then_inc(s_il, 1)
            vec.memset(hits[:, :], 0.0)
            o.link(vec.tensor_copy(first[:, :], ei[:, 1, 0:1]))
            vec.tensor_scalar(below[:, :], thr[0:ER, :], first[:, 0:1], None, ALU.is_gt).then_inc(s_in, 1)
            dve.wait_ge(s_mm, 1)
            o.link(vec.tensor_scalar(rowf[:, :], ps[0:NG + 1, 0, 0:1], -1.0, 0.0, ALU.add, ALU.max))
            vec.tensor_copy(rowi[:, :], rowf[:, :]).then_inc(s_ask, 1)
            dve.wait_ge(s_row, 16)
            o.link(vec.tensor_copy(foundf[:, :], found[:, :]))
            o.link(vec.tensor_scalar(hits[0:NG + 1, :], foundf[:, :], thrp[:, 0:1], 0.0, ALU.is_lt, ALU.add, accum_out=cnt[:, :]))
            vec.scalar_tensor_tensor(start[:, :], rowf[:, :], float(EC), cnt[:, :], ALU.mult, ALU.add).then_inc(s_in, 1)
            dve.wait_ge(s_mm, 2)
            o.link(vec.tensor_copy(size[:, :], ps[0:NG, 1, 0:1]))
            o.link(vec.tensor_scalar(hits[0:NG, 0:UM], ramp512[:, :], size[:, 0:1], 1.0, ALU.is_lt, ALU.add, accum_out=nblk[:, :]))
            vec.tensor_copy(size[:, :], nblk[:, :]).then_inc(s_in, 1)
            dve.wait_ge(s_mm, 3)
            vec.tensor_copy(base[:, :], ps[0:NG, 0, 0:1]).then_inc(s_in, 1)
            dve.wait_ge(s_in, 4)
            dve.wait_ge(s_mm, 4)
            o.link(vec.tensor_scalar(prs[:, 0:1], ps[0:1, 1, 0:1], 0.5, None, ALU.mult))
            o.link(vec.tensor_scalar(hits[0:1, 0:UM], c["ramp"][0:1, 0:UM], prs[:, 0:1], 0.0, ALU.is_lt, ALU.add, accum_out=prs[:, 1:2]))
            o.link(vec.tensor_copy(c["pairs_i"][:, :], prs[:, 1:2]))
            vec.scalar_tensor_tensor(v[:, :], base[:, :], -float(EB), start[0:NG, :], ALU.mult, ALU.add).then_inc(s_in, 1)
            dve.wait_ge(s_mm, 5)
            o.link(vec.tensor_copy(dv[:, :], ps[0:NG, 0, 0:1]))
            vec.tensor_scalar(begun[:, :], c["ramp"][0:NG, 0:UT], base[:, 0:1], None, ALU.is_ge).then_inc(s_in, 1)
            dve.wait_ge(s_in, 6)
            vec.tensor_scalar(begun_v[:, :], begun[:, :], dv[:, 0:1], None, ALU.mult).then_inc(s_in, 1)
            dve.wait_ge(s_mm, 6)
            o.link(vec.tensor_scalar(gof[:, :], ps[:, 1, 0:UT], -1.0, None, ALU.add))
            dve.wait_ge(s_mm, 7)
            o.link(vec.tensor_tensor(e0f[:, :], ps[:, 0, 0:UT], e0r[:, :], ALU.add))
            o.link(vec.tensor_scalar(e0f[:, :], e0f[:, :], float(E), None, ALU.min))
            o.link(vec.tensor_copy(c["group_i"][:, :], gof[0:1, :]))
            vec.tensor_copy(e0i[:, :], e0f[0:1, :]).then_inc(s_tab, 1)
            vec.memset(c["goes_on"][:, 0:1], 0.0)
            o.link(vec.tensor_tensor(c["goes_on"][:, 1:UT], gof[:, 1:UT], gof[:, 0:UT - 1], ALU.is_equal))
            o.link(vec.tensor_scalar(gof[:, :], gof[:, :], float(G), None, ALU.mult))
            o.link(vec.scalar_tensor_tensor(c["self_at"][:, :], c["goes_on"][:, :], -BIG, gof[:, :], ALU.mult, ALU.add))
            np_ = dve.value_load(c["pairs_i"][0:1, 0:1], min_val=1, max_val=UM // 2)
            for k in range(2):
                dve.wait_ge(s_blk[k], np_ * 16)
            vec.tensor_copy(c["e_idx"][:, :], meta[:, :, 0])
            vec.tensor_copy(c["e_w"][:, :].bitcast(I32), meta[:, :, 2])
            vec.tensor_copy(tmp[:, :], meta[:, :, 0])
            o.link(vec.tensor_copy(c["e_dst"][:, :], meta[:, :, 1]))
            o.link(vec.tensor_scalar(sq[:, :], tmp[:, :], 1.0 / T, None, ALU.mult))
            o.link(vec.tensor_copy(tmpi[:, :], sq[:, :]))
            o.link(vec.tensor_copy(sq[:, :], tmpi[:, :]))
            r = c["e_row"]
            o.link(vec.scalar_tensor_tensor(r[:, :], sq[:, :], -float(T), tmp[:, :], ALU.mult, ALU.add))
            o.link(vec.tensor_scalar(tmp[:, :], r[:, :], 0.0, None, ALU.is_lt))
            o.link(vec.tensor_tensor(sq[:, :], sq[:, :], tmp[:, :], ALU.subtract))
            o.link(vec.scalar_tensor_tensor(r[:, :], tmp[:, :], float(T), r[:, :], ALU.mult, ALU.add))
            o.link(vec.tensor_scalar(tmp[:, :], r[:, :], float(T), None, ALU.is_ge))
            o.link(vec.tensor_tensor(sq[:, :], sq[:, :], tmp[:, :], ALU.add))
            o.link(vec.scalar_tensor_tensor(r[:, :], tmp[:, :], -float(T), r[:, :], ALU.mult, ALU.add))
            dl = c["e_dst"]
            o.link(vec.tensor_tensor(dl[:, :].rearrange("p (u q) -> p u q", q=Q), dl[:, :].rearrange("p (u q) -> p u q", q=Q),
                                     gof[:, :].unsqueeze(2).to_broadcast([128, UT, Q]), ALU.subtract))
            o.link(vec.tensor_scalar(tmp[:, :], dl[:, :], 0.0, None, ALU.is_ge))
            o.link(vec.scalar_tensor_tensor(tmp[:, :], dl[:, :], float(G), tmp[:, :], ALU.is_lt, ALU.mult))
            qq = c["e_cell"]
            o.link(vec.scalar_tensor_tensor(qq[:, :], sq[:, :], float(G), dl[:, :], ALU.mult, ALU.add))
            o.link(vec.scalar_tensor_tensor(qq[:, :], qq[:, :], 1.0, tmp[:, :], ALU.add, ALU.mult))
            o.link(vec.tensor_scalar(qq[:, :], qq[:, :], -1.0, None, ALU.add))


def build_adjacency(nc, c, d):
    from contextlib import ExitStack
    with ExitStack() as ctx:
        def sb(name, shape, dt=F32):
            return ctx.enter_context(nc.sbuf_tensor(name, shape, dt))
        H1 = 13 * G
        H2 = NS * G - H1
        ohr = sb("source_onehot", [128, 2, Q, 128])
        cell = sb("weighted_cell", [128, 2, Q, NS * G])
        selfd = sb("self_loop_distance", [128, NS * G])
        selfi = sb("self_loop_distance_i", [128, NS * G], I32)
        part = sb("adjacency_part", [128, 2, NS * G])
        cur = sb("adjacency_tile", [128, 2, NS * G])
        acc = [ctx.enter_context(nc.psum_tensor(f"adjacency_sum_{k}", [128, 2, 512], F32)) for k in range(2)]
        s_p = c["sems"].take("build_pool_step")
        s_oh = [c["sems"].take(f"onehots_ready_{k}") for k in range(2)]
        s_mm = [c["sems"].take(f"adjacency_summed_{k}") for k in range(2)]
        s_pf = [c["sems"].take(f"adjacency_sum_read_{k}") for k in range(2)]
        s_cur = [c["sems"].take(f"adjacency_tile_ready_{k}") for k in range(2)]
        s_st = [c["sems"].take(f"adjacency_tile_stored_{k}") for k in range(2)]
        block = ctx.enter_context(nc.Block())

        def pair_count(eng):
            return eng.value_load(c["pairs_i"][0:1, 0:1], min_val=1, max_val=UM // 2)

        @block.gpsimd
        def _(pool):
            o = Order(pool, s_p)
            nc.gpsimd.iota(selfi[:, :], [[T, NS], [-1, G]], base=0, channel_multiplier=1)
            nc.gpsimd.memset(ohr[:, :, :, :], 0.0)
            nc.gpsimd.memset(cur[:, :, :], 0.0)
            o.link(nc.gpsimd.memset(part[:, :, :], 0.0))
            nc.gpsimd.memset(ohr[:, :, :, T:T + 1], 1.0)
            o.link(nc.gpsimd.tensor_copy(selfd[:, :], selfi[:, :]))
            o.link(nc.gpsimd.affine_select(out=selfd[:, :], in_=selfd[:, :], compare_op=ALU.is_gt, fill=-3 * BIG,
                                           base=T, pattern=[[0, NS * G]], channel_multiplier=-1))

        @block.vector
        def _(dve):
            vec = nc.vector

            def onehots(u, k):
                for q in range(Q):
                    col = bass.ds(u * Q + q, 1)
                    vec.tensor_scalar(ohr[:, k, q, 0:T], c["ramp"][:, 0:T], c["e_row"][:, col], None, ALU.is_equal)
                    last = vec.tensor_scalar(cell[:, k, q, :], c["ramp"][:, 0:NS * G], c["e_cell"][:, col],
                                             c["e_w"][:, col], ALU.is_equal, ALU.mult)
                last.then_inc(s_oh[k], 1)

            def finish(i, u, k):
                dve.wait_ge(s_mm[k], i + 1)
                vec.scalar_tensor_tensor(part[:, k, 0:H1], selfd[:, 0:H1], c["self_at"][:, bass.ds(u, 1)],
                                         acc[k][:, 0, 0:H1], ALU.is_equal, ALU.add)
                vec.scalar_tensor_tensor(part[:, k, H1:], selfd[:, H1:], c["self_at"][:, bass.ds(u, 1)],
                                         acc[k][:, 1, 0:H2], ALU.is_equal, ALU.add).then_inc(s_pf[k], 1)
                dve.wait_ge(s_pf[k], i + 1)
                dve.wait_ge(s_st[k], i * 16)
                dve.wait_ge(s_cur[1 - k], i + k)
                vec.scalar_tensor_tensor(cur[:, k, :], cur[:, 1 - k, :], c["goes_on"][:, bass.ds(u, 1)],
                                         part[:, k, :], ALU.mult, ALU.add).then_inc(s_cur[k], 1)

            dve.wait_ge(s_p, 3)
            pairs = pair_count(dve)
            onehots(0, 0)
            with dve.Fori(0, pairs) as i:
                dve.wait_ge(s_mm[1], i)
                onehots(2 * i + 1, 1)
                finish(i, 2 * i, 0)
                onehots(2 * i + 2, 0)
                finish(i, 2 * i + 1, 1)

        @block.tensor
        def _(pe):
            pe.wait_ge(s_p, 3)
            pairs = pair_count(pe)
            with pe.Fori(0, pairs) as i:
                for k in range(2):
                    pe.wait_ge(s_oh[k], i + 1)
                    pe.wait_ge(s_pf[k], i)
                    for q in range(Q):
                        nc.tensor.matmul(acc[k][:, 0, 0:H1], ohr[:, k, q, :], cell[:, k, q, 0:H1], start=q == 0, stop=q == Q - 1)
                        last = nc.tensor.matmul(acc[k][:, 1, 0:H2], ohr[:, k, q, :], cell[:, k, q, H1:], start=q == 0, stop=q == Q - 1)
                    last.then_inc(s_mm[k], 1)

        @block.sync
        def _(sp):
            pairs = pair_count(sp)
            with sp.Fori(0, pairs) as i:
                for k in range(2):
                    g = sp.value_load(c["group_i"][0:1, bass.ds(2 * i + k, 1)], min_val=0, max_val=NG - 1)
                    wait_alone(sp, c, s_cur[k], i + 1)
                    wait_alone(sp, c, s_st[1 - k], (i + k) * 16)
                    sp.dma_start(d["adj"][bass.ds(g, 1), :, :].rearrange("o p c -> (o p) c"), cur[:, k, :]).then_inc(s_st[k], 16)
            for k in range(2):
                wait_alone(sp, c, s_st[k], pairs * 16)


def degrees(nc, c, d):
    from contextlib import ExitStack
    with ExitStack() as ctx:
        def sb(name, shape, dt=F32):
            return ctx.enter_context(nc.sbuf_tensor(name, shape, dt))
        sums = sb("degree_parts", [NG, NS * G])
        deg = sb("degree", [NG, G])
        safe = sb("degree_guarded", [NG, G])
        y = sb("inverse_root", [NG, G])
        z = sb("inverse_root_step", [NG, G])
        s_ld = c["sems"].take("degree_parts_loaded")
        s_v = c["sems"].take("degree_vector_step")
        s_a = c["sems"].take("degree_root_ready")
        s_o = c["sems"].take("dinv_ready")
        s_st = c["sems"].take("dinv_stored")
        s_bk = c["sems"].take("dinv_loaded")
        s_in = c["sems"].take("degree_guarded_ready")
        block = ctx.enter_context(nc.Block())

        @block.sync
        def _(sp):
            sp.dma_start(sums[:, :], d["adj"][:, T, :]).then_inc(s_ld, 16)
            sp.wait_ge(s_o, 1)
            sp.dma_start(d["dinv"].rearrange("(g j) -> g j", j=G), y[:, :]).then_inc(s_st, 16)
            sp.wait_ge(s_st, 16)
            with nc.allow_non_contiguous_dma(reason="3125 values, once"):
                sp.dma_start(c["dinv_n"][:, :], d["dinv"].rearrange("(s r) -> r s", r=T)).then_inc(s_bk, 16)
            sp.dma_start(c["dinv_b"][:, :], d["dinv"].unsqueeze(0).to_broadcast([128, N])).then_inc(s_bk, 16)
            sp.wait_ge(s_bk, 32)

        @block.scalar
        def _(act):
            act.wait_ge(s_in, 1)
            nc.scalar.activation(y[:, :], safe[:, :], ACT.Sqrt).then_inc(s_a, 1)

        @block.vector
        def _(dve):
            o = Order(dve, s_v)
            vec = nc.vector
            dve.wait_ge(s_ld, 16)
            o.link(vec.tensor_reduce(deg[:, :], sums[:, :].rearrange("g (s j) -> g j s", j=G), AX.X, ALU.add))
            o.link(vec.tensor_scalar(deg[:, :], deg[:, :], 1.0, None, ALU.add))
            vec.tensor_scalar(safe[:, :], deg[:, :], 1e-30, None, ALU.max).then_inc(s_in, 1)
            dve.wait_ge(s_a, 1)
            o.link(vec.reciprocal(y[:, :], y[:, :]))
            o.link(vec.tensor_tensor(z[:, :], y[:, :], y[:, :], ALU.mult))
            o.link(vec.tensor_tensor(z[:, :], z[:, :], safe[:, :], ALU.mult))
            o.link(vec.tensor_scalar(z[:, :], z[:, :], -0.5, 1.5, ALU.mult, ALU.add))
            o.link(vec.tensor_tensor(y[:, :], y[:, :], z[:, :], ALU.mult))
            vec.scalar_tensor_tensor(y[:, :], deg[:, :], 0.0, y[:, :], ALU.is_gt, ALU.mult).then_inc(s_o, 1)


def shared_tensors(nc):
    def sb(name, shape, dt=F32):
        return nc.alloc_sbuf_tensor(name, shape, dt)
    return {
        "sems": Semaphores(nc), 
        "ramp_i": sb("ramp_i", [128, 640], I32), "ramp": sb("ramp", [128, 640]),
        "lane_i": sb("lane_i", [128, 1], I32), "lane": sb("lane", [128, 1]),
        "ones": sb("ones", [128, 128]), "ident": sb("ident", [128, 128]), "mean_w": sb("mean_w", [128, 128]),
        "pairs_i": sb("block_pairs", [1, 1], I32), "group_i": sb("block_group_i", [1, UT], I32),
        "goes_on": sb("block_goes_on", [128, UT]), "self_at": sb("block_self_at", [128, UT]),
        "first_i": sb("block_first_edge", [1, UT], I32),
        "e_idx": sb("edge_src", [128, UT * Q], I32), "e_w": sb("edge_w", [128, UT * Q]),
        "e_row": sb("edge_src_row", [128, UT * Q]), "e_dst": sb("edge_dst_local", [128, UT * Q]),
        "e_cell": sb("edge_cell", [128, UT * Q]),
        "dinv_n": sb("dinv_nodes", [T, NS]), "dinv_b": sb("dinv_all", [128, N]),
        "x_t": sb("x_t", [128, N]), "h_t": sb("h_t", [128, N]),
    }


BLK = 20
NB = NG // BLK
TAIL = NG - NB * BLK
COLS = [(b * BLK * G, BLK * G) for b in range(NB)] + [(NB * BLK * G, TAIL * G)]
EPS = 1e-5
NEG = -float(2 ** 100)
HEADS, HF = 4, 32
SLOPE = 0.2


def scope(nc, stack):
    def sb(name, shape, dt=F32):
        return stack.enter_context(nc.sbuf_tensor(name, shape, dt))

    def pb(name, shape, dt=F32):
        return stack.enter_context(nc.psum_tensor(name, shape, dt))
    return sb, pb


def load_transposed(nc, c, tag, x, out, bias=None):
    from contextlib import ExitStack
    with ExitStack() as ctx:
        sb, pb = scope(nc, ctx)
        xn = sb(tag + "_nodes", [T, NS, D])
        bt = sb(tag + "_bias", [128, 1])
        pt = pb(tag + "_transposed", [128, 2, 4, 128])
        s_ld, s_t, s_c = (c["sems"].take(f"{tag}_{n}") for n in ("loaded", "tiles_transposed", "tiles_copied"))
        block = ctx.enter_context(nc.Block())

        @block.sync
        def _(sp):
            sp.dma_start(xn[:, :, :], x.rearrange("(s r) f -> r s f", r=T)).then_inc(s_ld, 16)
            if bias is not None:
                with nc.allow_non_contiguous_dma(reason="one value to a partition"):
                    sp.dma_start(bt[:, :], bias.unsqueeze(1)).then_inc(s_ld, 16)

        @block.tensor
        def _(pe):
            pe.wait_ge(s_ld, 16 if bias is None else 32)
            for s in range(NS):
                if s % 4 == 0 and s >= 8:
                    pe.wait_ge(s_c, s // 4 - 1)
                t = nc.tensor.transpose(pt[:, s // 4 % 2, s % 4, 0:T], xn[:, s, :], c["ident"][0:T, 0:T])
                if s % 4 == 3 or s == NS - 1:
                    t.then_inc(s_t, 1)

        @block.vector
        def _(dve):
            for q in range(-(-NS // 4)):
                n = min(4, NS - 4 * q)
                dve.wait_ge(s_t, q + 1)
                o, i = out[:, 4 * q * T:(4 * q + n) * T].rearrange("f (s r) -> f s r", r=T), pt[:, q % 2, 0:n, 0:T]
                if bias is None:
                    nc.vector.tensor_copy(o, i).then_inc(s_c, 1)
                else:
                    nc.vector.tensor_scalar(o, i, bt[:, 0:1], None, ALU.add).then_inc(s_c, 1)


def gcn_layers(nc, c, d, tag, weights, bias, norm):
    from contextlib import ExitStack
    L = len(bias)
    with ExitStack() as ctx:
        sb, pb = scope(nc, ctx)
        w = sb(tag + "_weights", [128, L, D])
        vecs = sb(tag + "_vectors", [128, 3, L])
        h = sb(tag + "_scaled_nodes", [T, NS, D])
        ring = sb(tag + "_adjacency", [128, 2, BLK, NS * G])
        tail = sb(tag + "_adjacency_tail", [128, TAIL, NS * G])
        y = sb(tag + "_aggregate", [128, 2, BLK * G])
        eps = sb(tag + "_eps", [128, 1])
        hp = pb(tag + "_node_psum", [128, 2, 4, D])
        op = pb(tag + "_out_psum", [128, 2, 512])
        if norm:
            yb = sb(tag + "_centred", [128, BLK * G])
            sq = sb(tag + "_squares", [128, BLK * G])
            mp = pb(tag + "_moments", [128, 2, 512])
        names = ("weights_loaded", "tail_loaded", "nodes_multiplied", "nodes_scaled", "block_summed",
                 "block_read", "block_biased", "mean_ready", "block_centred", "squares_ready", "variance_ready",
                 "deviation_ready", "block_normed", "vec_step", "block_out", "start_copied")
        (s_w, s_tl, s_hm, s_hs, s_bs, s_br, s_bb, s_mn, s_ct, s_sq, s_vr, s_dv, s_nm, s_v, s_out, s_x0) = (
            c["sems"].take(f"{tag}_{n}") for n in names)
        s_a = [c["sems"].take(f"{tag}_adjacency_loaded_{k}") for k in range(2)]
        NBL = NB + 1
        NHG = -(-NS // 4)
        block = ctx.enter_context(nc.Block())
        HALF = NB // 2
        vec_rows = [bias] + (list(norm) if norm else [])

        @block.sync
        def _(sp):
            for l in range(L):
                sp.dma_start(w[:, l, :], weights[l]).then_inc(s_w, 16)
            with nc.allow_non_contiguous_dma(reason="one value to a partition"):
                for r, rows in enumerate(vec_rows):
                    for l in range(L):
                        sp.dma_start(vecs[:, r, l:l + 1], rows[l].unsqueeze(1)).then_inc(s_w, 16)
            sp.dma_start(tail[:, :, :], d["adj"][NB * BLK:, :, :].rearrange("g p c -> p g c")).then_inc(s_tl, 16)

            def load(b):
                sp.dma_start(ring[:, b % 2, :, :], d["adj"][b * BLK:(b + 1) * BLK, :, :].rearrange("g p c -> p g c")
                             ).then_inc(s_a[b % 2], 16)

            load(0)
            load(1)
            with sp.Fori(0, L - 1) as l:
                for b in range(2, NB + 2):
                    wait_alone(sp, c, s_bs, l * NBL + b - 1)
                    load(b % NB)
            for b in range(2, NB):
                sp.wait_ge(s_bs, (L - 1) * NBL + b - 1)
                load(b)

        LOADS = 16 * L * (1 + len(vec_rows))

        @block.tensor
        def _(pe):
            pe.wait_ge(s_w, LOADS)
            pe.wait_ge(s_tl, 16)

            def moments(l, b, which):
                n = COLS[b][1]
                done = l * NBL + b + 1
                pe.wait_ge(s_bb if which == 0 else s_sq, done)
                src = y[:, b % 2, 0:n] if which == 0 else sq[:, 0:n]
                nc.tensor.matmul(mp[:, which, 0:n], c["mean_w"][:, :], src, start=True, stop=True
                                 ).then_inc(s_mn if which == 0 else s_vr, 1)

            with pe.Fori(0, L) as l:
                pe.wait_ge(s_x0, 1)
                pe.wait_ge(s_out, l * NBL)
                for s in range(NS):
                    q = s // 4
                    if s % 4 == 0:
                        pe.wait_ge(s_hs, l * NHG + q - 1) if q >= 2 else pe.wait_ge(s_hs, l * NHG)
                    m = nc.tensor.matmul(hp[0:T, q % 2, s % 4, :], c["h_t"][:, s * T:(s + 1) * T], w[:, bass.ds(l, 1), :].rearrange("p o f -> p (o f)"),
                                         start=True, stop=True)
                    if s % 4 == 3 or s == NS - 1:
                        m.then_inc(s_hm, 1)
                pe.wait_ge(s_hs, (l + 1) * NHG)
                for b, (_, n) in enumerate(COLS):
                    if b < NB:
                        pe.wait_ge(s_a[b % 2], (l * HALF + b // 2 + 1) * 16)
                    pe.wait_ge(s_br, l * NBL + b - 1) if b >= 1 else pe.wait_ge(s_br, l * NBL)
                    a = ring[:, b % 2, :, :] if b < NB else tail[:, :, :]
                    for s in range(NS):
                        m = nc.tensor.matmul(op[:, b % 2, 0:n], h[:, s, :], a[0:T, :, s * G:(s + 1) * G],
                                             start=s == 0, stop=s == NS - 1)
                        if norm and b >= 1 and s in (8, 17):
                            moments(l, b - 1, 0 if s == 8 else 1)
                    m.then_inc(s_bs, 1)
                if norm:
                    moments(l, NB, 0)
                    moments(l, NB, 1)

        @block.scalar
        def _(act):
            act.wait_ge(s_w, LOADS)
            act.wait_ge(s_x0, 2)
            with act.Fori(0, L) as l:
                for b, (c0, n) in enumerate(COLS):
                    done = l * NBL + b + 1
                    wait_alone(act, c, s_br, done)
                    row = [vecs[:, r, bass.ds(l, 1)] for r in range(3)]
                    yk = y[:, b % 2, 0:n]
                    if not norm:
                        nc.scalar.activation(c["h_t"][:, c0:c0 + n], yk, ACT.Relu, bias=row[0]).then_inc(s_out, 1)
                        continue
                    nc.scalar.activation(yk, yk, ACT.Identity, bias=row[0]).then_inc(s_bb, 1)
                    wait_alone(act, c, s_ct, done)
                    nc.scalar.activation(sq[:, 0:n], yb[:, 0:n], ACT.Square).then_inc(s_sq, 1)
                    wait_alone(act, c, s_vr, done)
                    nc.scalar.activation(sq[:, 0:n], mp[:, 1, 0:n], ACT.Sqrt, bias=eps[:, 0:1]).then_inc(s_dv, 1)
                    wait_alone(act, c, s_nm, done)
                    nc.scalar.activation(c["h_t"][:, c0:c0 + n], yb[:, 0:n], ACT.Gelu, bias=row[2], scale=row[1]
                                         ).then_inc(s_out, 1)

        @block.vector
        def _(dve):
            o = Order(dve, s_v)
            vec = nc.vector
            vec.tensor_copy(c["h_t"][:, :], c["x_t"][:, :]).then_inc(s_x0, 1)
            vec.memset(eps[:, :], EPS).then_inc(s_x0, 1)
            with dve.Fori(0, L) as l:
                for q in range(NHG):
                    n = min(4, NS - 4 * q)
                    dve.wait_ge(s_hm, l * NHG + q + 1)
                    vec.tensor_tensor(h[:, 4 * q:4 * q + n, :], hp[0:T, q % 2, 0:n, :],
                                      c["dinv_n"][:, 4 * q:4 * q + n].unsqueeze(2).to_broadcast([T, n, D]), ALU.mult).then_inc(s_hs, 1)
                for b, (c0, n) in enumerate(COLS):
                    done = l * NBL + b + 1
                    dve.wait_ge(s_bs, done)
                    if b >= 2:
                        dve.wait_ge(s_out, done - 2)
                    yk = y[:, b % 2, 0:n]
                    vec.tensor_tensor(yk, op[:, b % 2, 0:n], c["dinv_b"][:, c0:c0 + n], ALU.mult).then_inc(s_br, 1)
                    if norm:
                        dve.wait_ge(s_mn, done)
                        dve.wait_ge(s_out, done - 1)
                        vec.tensor_tensor(yb[:, 0:n], yk, mp[:, 0, 0:n], ALU.subtract).then_inc(s_ct, 1)
                        dve.wait_ge(s_dv, done)
                        vec.reciprocal(sq[:, 0:n], sq[:, 0:n]).then_inc(s_v, 1)
                        dve.wait_ge(s_v, done)
                        vec.tensor_tensor(yb[:, 0:n], yb[:, 0:n], sq[:, 0:n], ALU.mult).then_inc(s_nm, 1)


def add_and_norm(nc, c, tag, parts):
    from contextlib import ExitStack
    with ExitStack() as ctx:
        sb, pb = scope(nc, ctx)
        t = sb(tag + "_sum", [128, N])
        sq = sb(tag + "_squares", [128, 2, BLK * G])
        eps = sb(tag + "_eps", [128, 1])
        mp = pb(tag + "_moments", [128, 2, 2, 512])
        s_v, s_sum, s_mn, s_ct, s_sq, s_vr, s_dv, s_out, s_e = (c["sems"].take(f"{tag}_{n}") for n in (
            "vec_step", "sum_ready", "mean_ready", "centred", "squares_ready", "variance_ready", "deviation_ready", "out", "eps_ready"))
        block = ctx.enter_context(nc.Block())

        def variance(pe, b):
            n = COLS[b][1]
            pe.wait_ge(s_sq, b + 1)
            if b >= 2:
                pe.wait_ge(s_dv, b - 1)
            nc.tensor.matmul(mp[:, 1, b % 2, 0:n], c["mean_w"][:, :], sq[:, b % 2, 0:n], start=True, stop=True).then_inc(s_vr, 1)

        def deviation(act, b):
            n = COLS[b][1]
            act.wait_ge(s_vr, b + 1)
            nc.scalar.activation(sq[:, b % 2, 0:n], mp[:, 1, b % 2, 0:n], ACT.Sqrt, bias=eps[:, 0:1]).then_inc(s_dv, 1)

        def scale(dve, o, b):
            c0, n = COLS[b]
            dve.wait_ge(s_dv, b + 1)
            o.link(nc.vector.reciprocal(sq[:, b % 2, 0:n], sq[:, b % 2, 0:n]))
            nc.vector.tensor_tensor(c["x_t"][:, c0:c0 + n], t[:, c0:c0 + n], sq[:, b % 2, 0:n], ALU.mult).then_inc(s_out, 1)


        @block.tensor
        def _(pe):
            for b, (c0, n) in enumerate(COLS):
                pe.wait_ge(s_sum, b + 1)
                if b >= 2:
                    pe.wait_ge(s_ct, b - 1)
                nc.tensor.matmul(mp[:, 0, b % 2, 0:n], c["mean_w"][:, :], t[:, c0:c0 + n], start=True, stop=True).then_inc(s_mn, 1)
                if b >= 1:
                    variance(pe, b - 1)
            variance(pe, NB)

        @block.scalar
        def _(act):
            act.wait_ge(s_e, 1)
            for b, (c0, n) in enumerate(COLS):
                act.wait_ge(s_ct, b + 1)
                if b >= 2:
                    act.wait_ge(s_out, b - 1)
                nc.scalar.activation(sq[:, b % 2, 0:n], t[:, c0:c0 + n], ACT.Square).then_inc(s_sq, 1)
                if b >= 1:
                    deviation(act, b - 1)
            deviation(act, NB)

        @block.vector
        def _(dve):
            vec = nc.vector
            o = Order(dve, s_v)
            vec.memset(eps[:, :], EPS).then_inc(s_e, 1)
            for b, (c0, n) in enumerate(COLS):
                cols = slice(c0, c0 + n)
                if len(parts) == 3:
                    o.link(vec.tensor_tensor(t[:, cols], parts[0][:, cols], parts[1][:, cols], ALU.add))
                    vec.tensor_tensor(t[:, cols], t[:, cols], parts[2][:, cols], ALU.add).then_inc(s_sum, 1)
                else:
                    vec.tensor_tensor(t[:, cols], parts[0][:, cols], parts[1][:, cols], ALU.add).then_inc(s_sum, 1)
            for b, (c0, n) in enumerate(COLS):
                cols = slice(c0, c0 + n)
                dve.wait_ge(s_mn, b + 1)
                vec.tensor_tensor(t[:, cols], t[:, cols], mp[:, 0, b % 2, 0:n], ALU.subtract).then_inc(s_ct, 1)
                if b >= 1:
                    scale(dve, o, b - 1)
            scale(dve, o, NB)



def node_tables(nc, c, tag, tables):
    from contextlib import ExitStack
    with ExitStack() as ctx:
        sb, pb = scope(nc, ctx)
        width = sum(b - a for _, (a, b), _ in tables[0][0])
        nt = len(tables)
        w = sb(tag + "_w", [128, nt, width])
        bias = sb(tag + "_bias", [T, nt, width])
        out = sb(tag + "_rows", [T, nt, NS, width])
        ready = sb(tag + "_ready", [1, 1])
        per = 512 // width
        runs = [(t, s, min(per, NS - s)) for t in range(nt) for s in range(0, NS, per)]
        ps = pb(tag + "_psum", [T, 2, per, width])
        s_w, s_v, s_n, s_b, s_mm, s_o, s_st = (c["sems"].take(f"{tag}_{n}") for n in (
            "loaded", "vec_step", "weights_ready", "bias_cleared", "tile_multiplied", "rows_ready", "rows_stored"))
        loads = sum(len(ws) + len(bs) for ws, bs, _ in tables)
        block = ctx.enter_context(nc.Block())

        @block.sync
        def _(sp):
            sp.wait_ge(s_b, 1)
            for t, (ws, bs, _) in enumerate(tables):
                for ap, (a, b), _ in ws:
                    sp.dma_start(w[:, t, a:b], ap).then_inc(s_w, 16)
                for ap, (a, b), _ in bs:
                    sp.dma_start(bias[:, t, a:b], ap.unsqueeze(0).to_broadcast([T, b - a])).then_inc(s_w, 16)
            for t, (_, _, dst) in enumerate(tables):
                sp.wait_ge(s_o, -(-NS // per) * (t + 1))
                sp.dma_start(dst.rearrange("(s r) f -> r s f", r=T), out[:, t, :, :]).then_inc(s_st, 16)
            sp.wait_ge(s_st, 16 * nt)

        @block.vector
        def _(dve):
            o = Order(dve, s_v)
            nc.vector.memset(bias[:, :, :], 0.0).then_inc(s_b, 1)
            dve.wait_ge(s_w, 16 * loads)
            for t, (ws, bs, _) in enumerate(tables):
                for _, (a, b), negate in ws:
                    if negate:
                        o.link(nc.vector.tensor_scalar(w[:, t, a:b], w[:, t, a:b], -1.0, None, ALU.mult))
                for _, (a, b), negate in bs:
                    if negate:
                        o.link(nc.vector.tensor_scalar(bias[:, t, a:b], bias[:, t, a:b], -1.0, None, ALU.mult))
            nc.vector.memset(ready[:, :], 0.0).then_inc(s_n, 1)
            for m, (t, s, n) in enumerate(runs):
                dve.wait_ge(s_mm, m + 1)
                nc.vector.tensor_tensor(out[:, t, s:s + n, :], ps[:, m % 2, 0:n, :],
                                        bias[:, t, :].unsqueeze(1).to_broadcast([T, n, width]), ALU.add).then_inc(s_o, 1)

        @block.tensor
        def _(pe):
            pe.wait_ge(s_n, 1)
            for m, (t, s0, n) in enumerate(runs):
                if m >= 2:
                    pe.wait_ge(s_o, m - 1)
                for s in range(n):
                    i = nc.tensor.matmul(ps[:, m % 2, s, :], c["x_t"][:, (s0 + s) * T:(s0 + s + 1) * T], w[:, t, :], start=True, stop=True)
                i.then_inc(s_mm, 1)


def attention(nc, c, d, att):
    from contextlib import ExitStack
    with ExitStack() as ctx:
        sb, pb = scope(nc, ctx)
        NH = G * HEADS
        HW = HF + 1
        att_b = sb("att_row", [128, D])
        head_of = sb("head_of", [NH, HEADS])
        head_rows = sb("head_rows", [HEADS, NH])
        mask_rows = sb("mask_rows", [G + 1, NH])
        node_of = sb("node_of", [NH, G])
        gone = sb("block_begins", [128, UT])
        idx = sb("gather_rows", [128, 2, Q], I32)
        xj = sb("source_rows", [128, 2, Q, D])
        hl = sb("group_rows", [G, 2, D])
        oh = sb("node_onehot", [128, 2, Q, G + 1])
        oht = sb("node_onehot_t", [G + 1, 2, Q * 128])
        z = sb("score_terms", [128, Q, D])
        zl = sb("score_terms_leaky", [128, Q, D])
        sc = sb("scores", [128, 2, Q * HEADS])
        sct = sb("scores_t", [HEADS, Q * 128])
        mx = sb("block_max", [NH, 1])
        mxh = sb("block_max_by_head", [NH, HEADS])
        mn = sb("block_max_nodes", [G, 2, HEADS])
        df = sb("score_less_max", [128, 2, Q * HEADS])
        msg = sb("messages", [128, 2, Q, HEADS, HW])
        run = sb("running_max", [G, 2, HEADS])
        acc = sb("running_sum", [G, 2, HEADS, HW])
        dab = sb("max_changes", [G, 2, HEADS])
        ab = sb("rescale", [G, 2, HEADS])
        t1 = sb("rescaled_run", [G, HEADS, HW])
        t2 = sb("rescaled_block", [G, HEADS, HW])
        den = sb("weight_sum", [G, HEADS])
        out = sb("group_out", [G, 2, D])
        p_t = pb("onehot_t_psum", [128, 512])
        p_z = pb("score_psum", [128, 2, 512])
        p_e = pb("scores_t_psum", [128, 512])
        p_m = pb("masked_scores", [128, 512])
        p_n = pb("max_nodes_psum", [128, 512])
        p_g = pb("max_edges_psum", [128, 512])
        p_a = pb("block_sum_psum", [128, 512])
        names = ("att_loaded", "pool_step", "index_copied", "vec_step", "constants_ready", "onehot", "onehot_t", "onehot_t_copied", "score_sum",
                 "score_sum_read", "scores", "scores_t", "scores_t_copied", "masked", "max", "max_by_head", "max_nodes_sum", "max_nodes",
                 "max_edges", "less_max", "weights", "messages", "block_sum", "changes", "rescale", "run_updated", "group_out")
        (s_at, s_p, s_ix, s_v, s_c, s_oh, s_T, s_oht, s_z, s_zr, s_ev, s_E, s_eT, s_M, s_mu, s_mh, s_N, s_mN,
         s_G, s_d, s_w, s_msg, s_A, s_ab, s_ex, s_acc, s_O) = (c["sems"].take("att_" + n) for n in names)
        s_g = [c["sems"].take(f"att_sources_gathered_{k}") for k in range(2)]
        s_hl = [c["sems"].take(f"att_group_rows_loaded_{k}") for k in range(2)]
        s_st = [c["sems"].take(f"att_group_out_stored_{k}") for k in range(2)]
        block = ctx.enter_context(nc.Block())

        def steps(eng, step):
            pairs = eng.value_load(c["pairs_i"][0:1, 0:1], min_val=1, max_val=UM // 2)
            step(0, 0, 1, False)
            with eng.Fori(0, pairs) as i:
                step(2 * i + 1, 1, i + 1, True)
                step(2 * i + 2, 0, i + 2, True)
            return pairs

        @block.gpsimd
        def _(pool):
            o = Order(pool, s_p)
            g = nc.gpsimd
            g.memset(head_rows[:, :], 0.0)
            g.memset(mask_rows[:, :], -NEG)
            g.memset(run[:, :, :], 0.0)
            g.memset(acc[:, :, :, :], 0.0)
            g.memset(oh[:, :, :, :], 1.0)
            o.link(g.memset(node_of[:, :], 1.0))
            o.link(g.affine_select(out=head_rows[:, :], in_=head_rows[:, :], compare_op=ALU.not_equal, fill=1.0, base=0,
                                   pattern=[[0, G], [1, HEADS]], channel_multiplier=-1))
            o.link(g.affine_select(out=mask_rows[:, :], in_=mask_rows[:, :], compare_op=ALU.is_ge, fill=0.0, base=0,
                                   pattern=[[1, NH]], channel_multiplier=-HEADS))
            o.link(g.affine_select(out=mask_rows[:, :], in_=mask_rows[:, :], compare_op=ALU.is_ge, fill=0.0, base=HEADS - 1,
                                   pattern=[[-1, NH]], channel_multiplier=HEADS))
            o.link(g.affine_select(out=mask_rows[:, :], in_=mask_rows[:, :], compare_op=ALU.is_gt, fill=NEG, base=G,
                                   pattern=[[0, NH]], channel_multiplier=-1))
            o.link(g.affine_select(out=node_of[:, :], in_=node_of[:, :], compare_op=ALU.is_ge, fill=0.0, base=0,
                                   pattern=[[-HEADS, G]], channel_multiplier=1))
            o.link(g.affine_select(out=node_of[:, :], in_=node_of[:, :], compare_op=ALU.is_ge, fill=0.0, base=HEADS - 1,
                                   pattern=[[HEADS, G]], channel_multiplier=-1))

            def gather(u, k, n, lag):
                if lag:
                    wait_alone(pool, c, s_msg, u - 1)
                g.tensor_copy(idx[:, k, :], c["e_idx"][:, bass.ds(u * Q, Q)]).then_inc(s_ix, 1)
                wait_alone(pool, c, s_ix, u + 1)
                for q in range(Q):
                    pool.indirect_dma_start(xj[:, k, q, :], None, d["h_r"], bass.IndirectOffsetOnAxis(ap=idx[:, k, q:q + 1], axis=0)
                                            ).then_inc(s_g[k], 16)
            steps(pool, gather)

        @block.sync
        def _(sp):
            sp.dma_start(att_b[:, :], att.rearrange("o h f -> o (h f)").to_broadcast([128, D])).then_inc(s_at, 16)

            def move(u, k, n, lag):
                g = sp.value_load(c["group_i"][0:1, bass.ds(u, 1)], min_val=0, max_val=NG - 1)
                if lag:
                    wait_alone(sp, c, s_z, u - 1)
                sp.dma_start(hl[:, k, :], d["h_l"][bass.ds(g * G, G), :]).then_inc(s_hl[k], 16)
                if lag:
                    gv = sp.value_load(c["group_i"][0:1, bass.ds(u - 1, 1)], min_val=0, max_val=NG - 1)
                    wait_alone(sp, c, s_O, u)
                    wait_alone(sp, c, s_st[k], (n - 1) * 16)
                    sp.dma_start(d["gat"][bass.ds(gv * G, G), :], out[:, 1 - k, :]).then_inc(s_st[1 - k], 16)
            pairs = steps(sp, move)
            for k in range(2):
                wait_alone(sp, c, s_st[k], pairs * 16)

        @block.tensor
        def _(pe):
            pe.wait_ge(s_c, 1)

            def step(u, k, n, lag):
                j = 1 - k
                pe.wait_ge(s_oh, u + 1)
                if lag:
                    pe.wait_ge(s_oht, u)
                for q in range(Q):
                    m = nc.tensor.transpose(p_t[0:G + 1, q * 128:(q + 1) * 128], oh[:, k, q, :], c["ident"][:, :])
                m.then_inc(s_T, 1)
                if lag:
                    pe.wait_ge(s_mh, u)
                    nc.tensor.matmul(p_n[0:G, 0:HEADS], node_of[:, :], mxh[:, :], start=True, stop=True).then_inc(s_N, 1)
                pe.wait_ge(s_oht, u + 1)
                pe.wait_ge(s_hl[k], n * 16)
                if lag:
                    pe.wait_ge(s_zr, u - 1)
                for q in range(Q):
                    m = nc.tensor.matmul(p_z[:, k, q * D:(q + 1) * D], oht[0:G, k, q * 128:(q + 1) * 128], hl[:, k, :], start=True, stop=True)
                m.then_inc(s_z, 1)
                if lag:
                    pe.wait_ge(s_mN, u)
                    for q in range(Q):
                        m = nc.tensor.matmul(p_g[:, q * HEADS:(q + 1) * HEADS], oht[0:G, j, q * 128:(q + 1) * 128], mn[:, j, :],
                                             start=True, stop=True)
                    m.then_inc(s_G, 1)
                    pe.wait_ge(s_msg, u)
                    pe.wait_ge(s_acc, u - 1)
                    for q in range(Q):
                        m = nc.tensor.matmul(p_a[0:G, 0:HEADS * HW], oh[:, j, q, 0:G], msg[:, j, q, :, :].rearrange("p h f -> p (h f)"),
                                             start=q == 0, stop=q == Q - 1)
                    m.then_inc(s_A, 1)
                pe.wait_ge(s_ev, u + 1)
                for q in range(Q):
                    m = nc.tensor.transpose(p_e[0:HEADS, q * 128:(q + 1) * 128], sc[:, k, q * HEADS:(q + 1) * HEADS], c["ident"][:, :])
                m.then_inc(s_E, 1)
                pe.wait_ge(s_eT, u + 1)
                nc.tensor.matmul(p_m[0:NH, :], head_rows[:, :], sct[:, :], start=True, stop=False)
                nc.tensor.matmul(p_m[0:NH, :], mask_rows[:, :], oht[:, k, :], start=False, stop=True).then_inc(s_M, 1)
            steps(pe, step)

        @block.scalar
        def _(act):
            def step(u, k, n, lag):
                j = 1 - k
                wait_alone(act, c, s_T, u + 1)
                nc.scalar.copy(oht[:, k, :], p_t[0:G + 1, :]).then_inc(s_oht, 1)
                if lag:
                    wait_alone(act, c, s_d, u)
                    nc.scalar.activation(msg[:, j, :, :, HF:HW], df[:, j, :].rearrange("p (q h o) -> p q h o", q=Q, o=1), ACT.Exp).then_inc(s_w, 1)
                wait_alone(act, c, s_E, u + 1)
                nc.scalar.copy(sct[:, :], p_e[0:HEADS, :]).then_inc(s_eT, 1)
                if lag:
                    wait_alone(act, c, s_ab, u)
                    nc.scalar.activation(ab[:, :, :], dab[:, :, :], ACT.Exp).then_inc(s_ex, 1)
            steps(act, step)

        @block.vector
        def _(dve):
            vec = nc.vector
            dve.wait_ge(s_at, 16)
            dve.wait_ge(s_p, 7)
            vec.tensor_reduce(head_of[:, :], c["ident"][0:NH, 0:NH].rearrange("p (n h) -> p h n", h=HEADS), AX.X, ALU.add).then_inc(s_c, 1)
            vec.tensor_scalar(gone[:, :], c["goes_on"][:, :], -NEG, NEG, ALU.mult, ALU.add).then_inc(s_c, 1)
            dve.wait_ge(s_c, 2)
            PER, FIRST = 7, 2
            o = Order(dve, s_v)

            def wait_out(u, j, n):
                if j == 0:
                    dve.wait_ge(s_st[0], (n - 1) * 16)
                else:
                    dve.wait_ge(s_st[1], (n - 2) * 16)

            def step(u, k, n, lag):
                j = 1 - k
                v = u - 1
                o.base, o.n = (0, 0) if not lag else (FIRST + v * PER, 0)
                if lag:
                    dve.wait_ge(s_A, v)
                vec.tensor_tensor(oh[:, k, :, 0:G], c["ramp"][:, 0:G].unsqueeze(1).to_broadcast([128, Q, G]),
                                  c["e_dst"][:, bass.ds(u * Q, Q)].unsqueeze(2).to_broadcast([128, Q, G]), ALU.is_equal).then_inc(s_oh, 1)
                if lag:
                    dve.wait_ge(s_M, u)
                    vec.tensor_reduce(mx[:, :], p_m[0:NH, :], AX.X, ALU.max).then_inc(s_mu, 1)
                    dve.wait_ge(s_mu, u)
                    vec.tensor_scalar(mxh[:, :], head_of[:, :], mx[:, 0:1], None, ALU.mult).then_inc(s_mh, 1)
                dve.wait_ge(s_z, u + 1)
                dve.wait_ge(s_g[k], n * 16 * Q)
                vec.tensor_tensor(z[:, :, :], p_z[:, k, :].rearrange("p (q f) -> p q f", q=Q), xj[:, k, :, :], ALU.add).then_inc(s_zr, 1)
                if lag:
                    dve.wait_ge(s_N, u)
                    vec.tensor_copy(mn[:, j, :], p_n[0:G, 0:HEADS]).then_inc(s_mN, 1)
                dve.wait_ge(s_zr, u + 1)
                o.link(vec.scalar_tensor_tensor(zl[:, :, :], z[:, :, :], SLOPE, z[:, :, :], ALU.mult, ALU.max))
                if lag:
                    dve.wait_ge(s_G, u)
                    o.link(vec.tensor_tensor(df[:, j, :], sc[:, j, :], p_g[:, 0:Q * HEADS], ALU.subtract))
                    vec.tensor_scalar(df[:, j, :], df[:, j, :], 0.0, None, ALU.min).then_inc(s_d, 1)
                o.link(vec.tensor_tensor(zl[:, :, :], zl[:, :, :], att_b[:, :].unsqueeze(1).to_broadcast([128, Q, D]), ALU.mult))
                if lag:
                    dve.wait_ge(s_w, u)
                    vec.tensor_tensor(msg[:, j, :, :, 0:HF], xj[:, j, :, :].rearrange("p q (h f) -> p q h f", h=HEADS),
                                      msg[:, j, :, :, HF:HW].to_broadcast([128, Q, HEADS, HF]), ALU.mult).then_inc(s_msg, 1)
                vec.tensor_reduce(sc[:, k, :], zl[:, :, :].rearrange("p q (h f) -> p (q h) f", h=HEADS), AX.X, ALU.add).then_inc(s_ev, 1)
                if lag:
                    begins = gone[0:G, bass.ds(v, 1)]
                    dve.wait_ge(s_mN, u)
                    o.link(vec.scalar_tensor_tensor(run[:, j, :], run[:, k, :], begins, mn[:, j, :], ALU.add, ALU.max))
                    vec.scalar_tensor_tensor(dab[:, 0, :], run[:, k, :], begins, run[:, j, :], ALU.add, ALU.subtract)
                    vec.tensor_tensor(dab[:, 1, :], mn[:, j, :], run[:, j, :], ALU.subtract).then_inc(s_ab, 1)
                    dve.wait_ge(s_ex, u)
                    dve.wait_ge(s_A, u)
                    vec.tensor_tensor(t1[:, :, :], acc[:, k, :, :], ab[:, 0, :].unsqueeze(2).to_broadcast([G, HEADS, HW]), ALU.mult)
                    o.link(vec.tensor_tensor(t2[:, :, :], p_a[0:G, 0:HEADS * HW].rearrange("n (h f) -> n h f", h=HEADS),
                                             ab[:, 1, :].unsqueeze(2).to_broadcast([G, HEADS, HW]), ALU.mult))
                    vec.tensor_tensor(acc[:, j, :, :], t1[:, :, :], t2[:, :, :], ALU.add).then_inc(s_acc, 1)
                    dve.wait_ge(s_acc, u)
                    o.link(vec.tensor_scalar(den[:, :], acc[:, j, :, HF:HW].rearrange("n h o -> n (h o)"), 1e-16, None, ALU.max))
                    o.link(vec.reciprocal(den[:, :], den[:, :]))
                    wait_out(u, j, n)
                    vec.tensor_tensor(out[:, j, :].rearrange("n (h f) -> n h f", h=HEADS), acc[:, j, :, 0:HF],
                                      den[:, :].unsqueeze(2).to_broadcast([G, HEADS, HF]), ALU.mult).then_inc(s_O, 1)

            steps(dve, step)


def gated_conv(nc, c, d, ea, w_f, w_s):
    from contextlib import ExitStack
    with ExitStack() as ctx:
        sb, pb = scope(nc, ctx)
        W = 2 * D
        we = sb("edge_weights", [128, W])
        idx = sb("gate_gather_rows", [128, 2, Q], I32)
        xj = sb("gate_source_rows_sb", [128, 2, Q, W])
        hl = sb("gate_group_rows", [G, 2, W])
        e_n = sb("edge_features", [128, 2, Q, D])
        e_t = sb("edge_features_t", [128, 2, Q * 128])
        oh = sb("gate_node_onehot", [128, 2, Q, G])
        oht = sb("gate_node_onehot_t", [G, 2, Q * 128])
        z = sb("gate_core", [128, 2, Q, W])
        lg = sb("gate_core_log", [128, 2, Q, W])
        gt = sb("gate", [128, Q, D])
        msg = sb("gate_messages", [128, 2, Q, D])
        cur = sb("gate_group_sum", [128, 2, G])
        p_o = pb("gate_onehot_t_psum", [128, 512])
        p_e = pb("edge_t_psum", [128, 512])
        p_z = pb("gate_core_psum", [128, 2, 2, 512])
        p_a = pb("gate_sum_psum", [128, 512])
        names = ("weights_loaded", "weights_negated", "pool_step", "index_copied", "vec_step", "act_step", "onehot", "onehot_t", "onehot_t_copied",
                 "edge_t", "edge_t_copied", "core_sum", "core_sum_read", "log", "softplus", "gate", "messages", "block_sum", "group_sum")
        (s_w, s_wn, s_p, s_ix, s_v, s_a, s_oh, s_T, s_oht, s_eT, s_et, s_z, s_zr, s_ln, s_sp, s_gt, s_msg, s_A, s_O) = (
            c["sems"].take("gate_" + n) for n in names)
        s_g = [c["sems"].take(f"gate_sources_gathered_{k}") for k in range(2)]
        s_hl = [c["sems"].take(f"gate_group_rows_loaded_{k}") for k in range(2)]
        s_e = [c["sems"].take(f"gate_edges_loaded_{k}") for k in range(2)]
        s_st = [c["sems"].take(f"gate_group_sum_stored_{k}") for k in range(2)]
        block = ctx.enter_context(nc.Block())

        def steps(eng, step):
            pairs = eng.value_load(c["pairs_i"][0:1, 0:1], min_val=1, max_val=UM // 2)
            step(0, 0, 1, False)
            with eng.Fori(0, pairs) as i:
                step(2 * i + 1, 1, i + 1, True)
                step(2 * i + 2, 0, i + 2, True)
            return pairs

        @block.gpsimd
        def _(pool):
            def gather(u, k, n, lag):
                if lag:
                    wait_alone(pool, c, s_zr, u - 1)
                nc.gpsimd.tensor_copy(idx[:, k, :], c["e_idx"][:, bass.ds(u * Q, Q)]).then_inc(s_ix, 1)
                wait_alone(pool, c, s_ix, u + 1)
                for q in range(Q):
                    pool.indirect_dma_start(xj[:, k, q, :], None, d["p_src"], bass.IndirectOffsetOnAxis(ap=idx[:, k, q:q + 1], axis=0)
                                            ).then_inc(s_g[k], 16)
            steps(pool, gather)

        @block.sync
        def _(sp):
            sp.dma_start(we[:, 0:D], w_f[2 * D:3 * D, :]).then_inc(s_w, 16)
            sp.dma_start(we[:, D:W], w_s[2 * D:3 * D, :]).then_inc(s_w, 16)

            def move(u, k, n, lag):
                e0 = sp.value_load(c["first_i"][0:1, bass.ds(u, 1)], min_val=0, max_val=E)
                g = sp.value_load(c["group_i"][0:1, bass.ds(u, 1)], min_val=0, max_val=NG - 1)
                if lag:
                    wait_alone(sp, c, s_eT, u - 1)
                sp.dma_start(e_n[:, k, :, :], ea[bass.ds(e0, EB), :].rearrange("(p q) f -> p q f", q=Q)).then_inc(s_e[k], 16)
                if lag:
                    wait_alone(sp, c, s_z, u - 1)
                sp.dma_start(hl[:, k, :], d["p_dst"][bass.ds(g * G, G), :]).then_inc(s_hl[k], 16)
                if lag:
                    gv = sp.value_load(c["group_i"][0:1, bass.ds(u - 1, 1)], min_val=0, max_val=NG - 1)
                    wait_alone(sp, c, s_O, u)
                    wait_alone(sp, c, s_st[k], (n - 1) * 16)
                    sp.dma_start(d["agg_t"][:, bass.ds(gv * G, G)], cur[:, 1 - k, :]).then_inc(s_st[1 - k], 16)
            pairs = steps(sp, move)
            for k in range(2):
                wait_alone(sp, c, s_st[k], pairs * 16)

        @block.tensor
        def _(pe):
            pe.wait_ge(s_wn, 1)

            def step(u, k, n, lag):
                j = 1 - k
                pe.wait_ge(s_e[k], n * 16)
                if lag:
                    pe.wait_ge(s_et, u)
                for q in range(Q):
                    m = nc.tensor.transpose(p_e[:, q * 128:(q + 1) * 128], e_n[:, k, q, :], c["ident"][:, :])
                m.then_inc(s_eT, 1)
                pe.wait_ge(s_oh, u + 1)
                if lag:
                    pe.wait_ge(s_oht, u)
                for q in range(Q):
                    m = nc.tensor.transpose(p_o[0:G, q * 128:(q + 1) * 128], oh[:, k, q, :], c["ident"][:, :])
                m.then_inc(s_T, 1)
                pe.wait_ge(s_et, u + 1)
                pe.wait_ge(s_oht, u + 1)
                pe.wait_ge(s_hl[k], n * 16)
                if lag:
                    pe.wait_ge(s_zr, u - 1)
                for q in range(Q):
                    o = p_z[:, k, q // 2, (q % 2) * W:(q % 2 + 1) * W]
                    nc.tensor.matmul(o, e_t[:, k, q * 128:(q + 1) * 128], we[:, :], start=True, stop=False)
                    m = nc.tensor.matmul(o, oht[:, k, q * 128:(q + 1) * 128], hl[:, k, :], start=False, stop=True)
                m.then_inc(s_z, 1)
                if lag:
                    pe.wait_ge(s_msg, u)
                    pe.wait_ge(s_O, u - 1)
                    for q in range(Q):
                        m = nc.tensor.matmul(p_a[:, 0:G], msg[:, j, q, :], oh[:, j, q, :], start=q == 0, stop=q == Q - 1)
                    m.then_inc(s_A, 1)
            steps(pe, step)

        @block.scalar
        def _(act):
            o = Order(act, s_a)

            def step(u, k, n, lag):
                j = 1 - k
                o.base, o.n = 2 * u, 0
                wait_alone(act, c, s_eT, u + 1)
                nc.scalar.copy(e_t[:, k, :], p_e[:, :]).then_inc(s_et, 1)
                if lag:
                    wait_alone(act, c, s_sp, u)
                    nc.scalar.activation(gt[:, :, :], z[:, j, :, 0:D], ACT.Exp, scale=-1.0).then_inc(s_gt, 1)
                wait_alone(act, c, s_zr, u + 1)
                o.link(nc.scalar.activation(lg[:, k, :, :], z[:, k, :, :], ACT.Abs))
                o.link(nc.scalar.activation(lg[:, k, :, :], lg[:, k, :, :], ACT.Exp, scale=-1.0))
                nc.scalar.activation(lg[:, k, :, :], lg[:, k, :, :], ACT.Ln, bias=1.0).then_inc(s_ln, 1)
            steps(act, step)

        @block.vector
        def _(dve):
            vec = nc.vector
            dve.wait_ge(s_w, 32)
            vec.memset(cur[:, :, :], 0.0)
            vec.tensor_scalar(we[:, 0:D], we[:, 0:D], -1.0, None, ALU.mult).then_inc(s_wn, 1)
            dve.wait_ge(s_wn, 1)

            def step(u, k, n, lag):
                j = 1 - k
                v = u - 1
                if lag:
                    dve.wait_ge(s_A, v)
                vec.tensor_tensor(oh[:, k, :, :], c["ramp"][:, 0:G].unsqueeze(1).to_broadcast([128, Q, G]),
                                  c["e_dst"][:, bass.ds(u * Q, Q)].unsqueeze(2).to_broadcast([128, Q, G]), ALU.is_equal).then_inc(s_oh, 1)
                if lag:
                    dve.wait_ge(s_ln, u)
                    vec.scalar_tensor_tensor(z[:, j, :, :], z[:, j, :, :], 0.0, lg[:, j, :, :], ALU.max, ALU.add).then_inc(s_sp, 1)
                dve.wait_ge(s_T, u + 1)
                vec.tensor_copy(oht[:, k, :], p_o[0:G, :]).then_inc(s_oht, 1)
                if lag:
                    dve.wait_ge(s_gt, u)
                    vec.tensor_tensor(msg[:, j, :, :], gt[:, :, :], z[:, j, :, D:W], ALU.mult).then_inc(s_msg, 1)
                dve.wait_ge(s_z, u + 1)
                dve.wait_ge(s_g[k], n * 16 * Q)
                vec.tensor_tensor(z[:, k, :, :], p_z[:, k, :, :].rearrange("p a (b f) -> p (a b) f", b=2), xj[:, k, :, :], ALU.add).then_inc(s_zr, 1)
                if lag:
                    dve.wait_ge(s_A, u)
                    if j == 0:
                        dve.wait_ge(s_st[0], (n - 1) * 16)
                    else:
                        dve.wait_ge(s_st[1], (n - 2) * 16)
                    vec.scalar_tensor_tensor(cur[:, j, :], cur[:, k, :], c["goes_on"][:, bass.ds(v, 1)], p_a[:, 0:G],
                                             ALU.mult, ALU.add).then_inc(s_O, 1)
                    dve.wait_ge(s_O, u)
            steps(dve, step)


def load_rows(nc, c, tag, dst, src):
    s = c["sems"].take(tag + "_loaded")
    with nc.Block() as block:
        @block.sync
        def _(sp):
            sp.dma_start(dst, src).then_inc(s, 16)
            sp.wait_ge(s, 16)


def residual_branch(nc, c, w_res, b_res, g_res, beta_res, out):
    from contextlib import ExitStack
    with ExitStack() as ctx:
        sb, pb = scope(nc, ctx)
        w = sb("res_w", [128, D])
        vecs = sb("res_vectors", [128, 3])
        y = sb("res_rows", [128, N])
        sq = sb("res_squares", [128, 2, BLK * G])
        eps = sb("res_eps", [128, 1])
        yp = pb("res_psum", [128, 2, 512])
        mp = pb("res_moments", [128, 2, 2, 512])
        s_ld, s_y, s_b, s_mn, s_ct, s_sq, s_vr, s_dv, s_v, s_nm, s_e, s_o = (c["sems"].take("res_" + n) for n in (
            "loaded", "multiplied", "biased", "mean_ready", "centred", "squares_ready", "variance_ready", "deviation_ready",
            "vec_step", "normed", "eps_ready", "out"))
        block = ctx.enter_context(nc.Block())

        @block.sync
        def _(sp):
            sp.dma_start(w[:, :], w_res).then_inc(s_ld, 16)
            with nc.allow_non_contiguous_dma(reason="one value to a partition"):
                for r, row in enumerate((b_res, g_res, beta_res)):
                    sp.dma_start(vecs[:, r:r + 1], row.unsqueeze(1)).then_inc(s_ld, 16)

        @block.tensor
        def _(pe):
            pe.wait_ge(s_ld, 64)
            for b, (c0, n) in enumerate(COLS):
                if b >= 2:
                    pe.wait_ge(s_b, b - 1)
                nc.tensor.matmul(yp[:, b % 2, 0:n], w[:, :], c["x_t"][:, c0:c0 + n], start=True, stop=True).then_inc(s_y, 1)
            for b, (c0, n) in enumerate(COLS):
                pe.wait_ge(s_b, b + 1)
                if b >= 2:
                    pe.wait_ge(s_ct, b - 1)
                nc.tensor.matmul(mp[:, 0, b % 2, 0:n], c["mean_w"][:, :], y[:, c0:c0 + n], start=True, stop=True).then_inc(s_mn, 1)
                pe.wait_ge(s_sq, b + 1)
                if b >= 2:
                    pe.wait_ge(s_dv, b - 1)
                nc.tensor.matmul(mp[:, 1, b % 2, 0:n], c["mean_w"][:, :], sq[:, b % 2, 0:n], start=True, stop=True).then_inc(s_vr, 1)

        @block.scalar
        def _(act):
            act.wait_ge(s_ld, 64)
            act.wait_ge(s_e, 1)
            for b, (c0, n) in enumerate(COLS):
                act.wait_ge(s_y, b + 1)
                nc.scalar.activation(y[:, c0:c0 + n], yp[:, b % 2, 0:n], ACT.Identity, bias=vecs[:, 0:1]).then_inc(s_b, 1)
            for b, (c0, n) in enumerate(COLS):
                act.wait_ge(s_ct, b + 1)
                if b >= 2:
                    act.wait_ge(s_nm, b - 1)
                nc.scalar.activation(sq[:, b % 2, 0:n], y[:, c0:c0 + n], ACT.Square).then_inc(s_sq, 1)
                act.wait_ge(s_vr, b + 1)
                nc.scalar.activation(sq[:, b % 2, 0:n], mp[:, 1, b % 2, 0:n], ACT.Sqrt, bias=eps[:, 0:1]).then_inc(s_dv, 1)
            for b, (c0, n) in enumerate(COLS):
                act.wait_ge(s_nm, b + 1)
                nc.scalar.activation(out[:, c0:c0 + n], y[:, c0:c0 + n], ACT.Gelu, bias=vecs[:, 2:3], scale=vecs[:, 1:2]).then_inc(s_o, 1)

        @block.vector
        def _(dve):
            o = Order(dve, s_v)
            nc.vector.memset(eps[:, :], EPS).then_inc(s_e, 1)
            for b, (c0, n) in enumerate(COLS):
                cols = slice(c0, c0 + n)
                dve.wait_ge(s_mn, b + 1)
                nc.vector.tensor_tensor(y[:, cols], y[:, cols], mp[:, 0, b % 2, 0:n], ALU.subtract).then_inc(s_ct, 1)
                dve.wait_ge(s_dv, b + 1)
                o.link(nc.vector.reciprocal(sq[:, b % 2, 0:n], sq[:, b % 2, 0:n]))
                nc.vector.tensor_tensor(y[:, cols], y[:, cols], sq[:, b % 2, 0:n], ALU.mult).then_inc(s_nm, 1)


def store_nodes(nc, c, out):
    from contextlib import ExitStack
    with ExitStack() as ctx:
        sb, pb = scope(nc, ctx)
        on = sb("out_nodes", [T, NS, D])
        pt = pb("out_psum", [T, 2, 4, D])
        s_t, s_c, s_st = (c["sems"].take("out_" + n) for n in ("tiles_transposed", "tiles_copied", "stored"))
        block = ctx.enter_context(nc.Block())

        @block.tensor
        def _(pe):
            for s in range(NS):
                if s % 4 == 0 and s >= 8:
                    pe.wait_ge(s_c, s // 4 - 1)
                t = nc.tensor.transpose(pt[:, s // 4 % 2, s % 4, :], c["x_t"][:, s * T:(s + 1) * T], c["ident"][:, :])
                if s % 4 == 3 or s == NS - 1:
                    t.then_inc(s_t, 1)

        @block.vector
        def _(dve):
            for q in range(-(-NS // 4)):
                n = min(4, NS - 4 * q)
                dve.wait_ge(s_t, q + 1)
                nc.vector.tensor_copy(on[:, 4 * q:4 * q + n, :], pt[:, q % 2, 0:n, :]).then_inc(s_c, 1)

        @block.sync
        def _(sp):
            sp.wait_ge(s_c, -(-NS // 4))
            sp.dma_start(out.rearrange("(s r) f -> r s f", r=T), on[:, :, :]).then_inc(s_st, 16)
            sp.wait_ge(s_st, 16)


def graph_network(nc, a, out):
    c = shared_tensors(nc)
    c["sems"].begin(c)
    d = dram_scratch(nc)
    constants(nc, c)
    prepare(nc, c, d, a["src"], a["dst"], a["edge_weight"])
    build_adjacency(nc, c, d)
    degrees(nc, c, d)
    c["sems"].end()
    load_transposed(nc, c, "x", a["x"], c["x_t"])

    gcn_layers(nc, c, d, "gcn", [a[f"L0_gnn_W{i}"] for i in (1, 2, 3)], [a[f"L0_gnn_b{i}"] for i in (1, 2, 3)], None)
    add_and_norm(nc, c, "norm0", [c["x_t"], c["h_t"]])
    c["sems"].end()

    node_tables(nc, c, "gat_tables", [([(a["L1_gnn_weight_l"], (0, D), False)], [], d["h_l"]),
                                      ([(a["L1_gnn_weight_r"], (0, D), False)], [], d["h_r"])])
    attention(nc, c, d, a["L1_gnn_att"])
    load_transposed(nc, c, "gat", d["gat"], c["h_t"], a["L1_gnn_bias"])
    add_and_norm(nc, c, "norm1", [c["x_t"], c["h_t"]])
    c["sems"].end()

    wf, ws = a["L2_gnn_W_f"], a["L2_gnn_W_s"]
    node_tables(nc, c, "gate_tables", [([(wf[0:D, :], (0, D), True), (ws[0:D, :], (D, 2 * D), False)],
                                        [(a["L2_gnn_b_f"], (0, D), True), (a["L2_gnn_b_s"], (D, 2 * D), False)], d["p_dst"]),
                                       ([(wf[D:2 * D, :], (0, D), True), (ws[D:2 * D, :], (D, 2 * D), False)], [], d["p_src"])])
    gated_conv(nc, c, d, a["edge_attr_128"], wf, ws)
    load_rows(nc, c, "gate_sum", c["h_t"][:, :], d["agg_t"])
    add_and_norm(nc, c, "norm2", [c["x_t"], c["x_t"], c["h_t"]])
    c["sems"].end()

    L = a["L3_gnn_conv_W"].shape[0]
    rows = {n: [a["L3_gnn_" + n][l] for l in range(L)] for n in ("conv_W", "conv_b", "ln_g", "ln_b")}
    gcn_layers(nc, c, d, "deep", rows["conv_W"], rows["conv_b"], (rows["ln_g"], rows["ln_b"]))
    with nc.sbuf_tensor("identity_branch", [128, N], F32) as branch:
        residual_branch(nc, c, a["L3_gnn_res_W"], a["L3_gnn_res_b"], a["L3_gnn_res_g"], a["L3_gnn_res_beta"], branch)
        add_and_norm(nc, c, "norm3", [c["x_t"], c["h_t"], branch])
    store_nodes(nc, c, out)


_INS = ['x', 'src', 'dst', 'edge_attr_128', 'edge_weight', 'L0_gnn_W1', 'L0_gnn_b1', 'L0_gnn_W2', 'L0_gnn_b2', 'L0_gnn_W3', 'L0_gnn_b3',
        'L1_gnn_weight_l', 'L1_gnn_weight_r', 'L1_gnn_att', 'L1_gnn_bias', 'L2_gnn_W_f', 'L2_gnn_b_f', 'L2_gnn_W_s', 'L2_gnn_b_s',
        'L3_gnn_conv_W', 'L3_gnn_conv_b', 'L3_gnn_ln_g', 'L3_gnn_ln_b', 'L3_gnn_res_W', 'L3_gnn_res_b', 'L3_gnn_res_g', 'L3_gnn_res_beta']


def kernel(**inputs):
    import numpy as _np
    import concourse.bacc as _bacc
    from concourse import mybir as _mybir
    from concourse.bass_utils import run_bass_kernel_spmd as _run

    nc = _bacc.Bacc("TRN2", target_bir_lowering=False, num_devices=1)
    arrays, args = {}, {}
    for name in _INS:
        a = _np.ascontiguousarray(inputs[name])
        if name == 'edge_attr_128':
            rows = _np.zeros((E + EB, D), a.dtype)
            rows[:E] = a
            a = rows
        arrays[f"in_{name}_dram"] = a
        args[name] = nc.dram_tensor(f"in_{name}_dram", a.shape, _mybir.dt.from_np(a.dtype), kind="ExternalInput").ap()
    out = nc.dram_tensor("out_dram", (N, D), F32, kind="ExternalOutput").ap()
    graph_network(nc, args, out)
    r = _run(nc, [arrays], core_ids=[0])
    return r.results[0]["out_dram"]
```

```python
import numpy as np
import concourse.bass as bass
from concourse import mybir

F32 = mybir.dt.float32
I32 = mybir.dt.int32
BF16 = mybir.dt.bfloat16
ALU = mybir.AluOpType
ACT = mybir.ActivationFunctionType
AX = mybir.AxisListType

N = 3125
E = 50000
D = 128
T = 125
NS = N // T
G = 25
NG = N // G
Q = 4
EB = 128 * Q
UM = -(-E // EB) + NG
UM += -UM % 4
PARTS = 3
UT = UM + 8
ER = T
EC = E // ER
BIG = 1.0e6


def wait_alone(eng, c, sem, value):
    eng.wait_ge(sem, value)
    eng.sem_inc(c["ticks"], 1)


class Order:

    def __init__(self, eng, sem):
        self.eng, self.sem, self.n, self.base = eng, sem, 0, 0

    def link(self, ins):
        ins.then_inc(self.sem, 1)
        self.n += 1
        self.eng.wait_ge(self.sem, self.base + self.n)


class Semaphores:

    def __init__(self, nc):
        self.nc, self.taken, self.c, self.stages = nc, [], {}, 0

    def take(self, name):
        self.taken.append(self.nc.alloc_semaphore(name))
        return self.taken[-1]

    def begin(self, c):
        self.c = c
        self.stages += 1
        c["ticks"] = self.take(f"ticks_{self.stages}")

    def end(self):
        self.nc.clear_and_free_semaphores(self.taken)
        self.nc.all_engine_barrier()
        self.taken = []
        self.begin(self.c)


def dram_scratch(nc):
    return {
        "edges": nc.dram_tensor("edge_list", [E + EB, 4], I32).ap(),
        "adj": nc.dram_tensor("adjacency", [NG, 128, NS * G], F32).ap(),
        "dinv": nc.dram_tensor("dinv_row", [N], F32).ap(),
        "h_l": nc.dram_tensor("gat_target_rows", [PARTS, N, D], BF16).ap(),
        "h_r": nc.dram_tensor("gat_source_rows", [N, D], F32).ap(),
        "p_dst": nc.dram_tensor("gate_target_rows", [PARTS, N, 2 * D], BF16).ap(),
        "p_src": nc.dram_tensor("gate_source_rows", [N, 2 * D], F32).ap(),
    }


def constants(nc, c):
    s_c = c["sems"].take("constants_step")
    with nc.Block() as block:
        @block.gpsimd
        def _(pool):
            o = Order(pool, s_c)
            nc.gpsimd.iota(c["ramp_i"][:, :], [[1, 640]], base=0, channel_multiplier=0)
            nc.gpsimd.iota(c["lane_i"][:, :], [[0, 1]], base=0, channel_multiplier=1)
            nc.gpsimd.memset(c["ones"][:, :], 1.0)
            nc.gpsimd.memset(c["ident"][:, :], 0.0)
            o.link(nc.gpsimd.memset(c["mean_w"][:, :], 1.0 / D))
            o.link(nc.gpsimd.tensor_copy(c["ramp"][:, :], c["ramp_i"][:, :]))
            o.link(nc.gpsimd.tensor_copy(c["lane"][:, :], c["lane_i"][:, :]))
            o.link(nc.gpsimd.affine_select(out=c["ident"][:, :], in_=c["ident"][:, :], compare_op=ALU.not_equal,
                                           fill=1.0, base=0, pattern=[[-1, 128]], channel_multiplier=1))


def prepare(nc, c, d, x_src, x_dst, x_w):
    s_ld = c["sems"].take("edge_inputs_loaded")
    s_st = c["sems"].take("edge_list_stored")
    s_v = c["sems"].take("prepare_vector_step")
    s_p = c["sems"].take("prepare_pool_step")
    s_il = c["sems"].take("edge_list_interleaved")
    s_row = c["sems"].take("search_rows_gathered")
    s_ask = c["sems"].take("search_rows_known")
    s_in = c["sems"].take("prepare_matmul_operand")
    s_mm = c["sems"].take("prepare_matmul_done")
    s_tab = c["sems"].take("block_tables_ready")
    s_blk = [c["sems"].take(f"edge_blocks_loaded_{k}") for k in range(2)]

    def sb(name, shape, dt=F32):
        return ctx.enter_context(nc.sbuf_tensor(name, shape, dt))

    from contextlib import ExitStack
    with ExitStack() as ctx:
        ei = sb("edge_in", [ER, 3, EC], I32)
        el = sb("edge_rows", [ER, EC, 4], I32)
        pad = sb("edge_pad", [128, Q, 4], I32)
        thr = sb("group_threshold", [128, NG + 1])
        first = sb("row_first", [ER, 1])
        below = sb("rows_below", [ER, NG + 1])
        rowf = sb("search_row_f", [NG + 1, 1])
        rowi = sb("search_row_i", [NG + 1, 1], I32)
        found = sb("search_rows", [NG + 1, EC], I32)
        foundf = sb("search_rows_f", [NG + 1, EC])
        thrp = sb("own_threshold", [NG + 1, 1])
        cnt = sb("below_in_row", [NG + 1, 1])
        start = sb("group_start", [NG + 1, 1])
        up = sb("next_minus_own", [NG + 1, NG])
        down = sb("own_minus_previous", [NG, NG])
        before = sb("earlier_groups", [NG, NG])
        ramp512 = sb("block_sizes", [NG, UM])
        size = sb("group_size", [NG, 1])
        nblk = sb("group_blocks", [NG, 1])
        hits = sb("threshold_hits", [128, EC])
        base = sb("group_first_block", [NG, 1])
        v = sb("block_edge_offset", [NG, 1])
        dv = sb("block_edge_step", [NG, 1])
        begun = sb("group_begun", [NG, UT])
        begun_v = sb("group_begun_edges", [NG, UT])
        gof = sb("block_group", [128, UT])
        e0f = sb("block_first_edge_f", [128, UT])
        e0r = sb("block_ramp_edges", [128, UT])
        e0i = c["first_i"]
        prs = sb("pairs_f", [1, 2])
        ps = ctx.enter_context(nc.psum_tensor("prep_psum", [128, 2, 512], F32))
        meta = sb("edge_blocks", [128, UT * Q, 4], I32)
        tmp = sb("edge_tmp", [128, UT * Q])
        tmpi = sb("edge_tmp_i", [128, UT * Q], I32)
        sq = sb("edge_src_tile", [128, UT * Q])

        block = ctx.enter_context(nc.Block())

        def load_blocks(eng, k):
            eng.wait_ge(s_tab, 1)
            eng.wait_ge(s_st, 32)
            pairs = eng.value_load(c["pairs_i"][0:1, 0:1], min_val=1, max_val=UM // 2)
            with eng.Fori(0, pairs) as i:
                e0 = eng.value_load(e0i[0:1, bass.ds(2 * i + k, 1)], min_val=0, max_val=E)
                eng.dma_start(meta[:, bass.ds((2 * i + k) * Q, Q), :],
                              d["edges"][bass.ds(e0, EB), :].rearrange("(p q) w -> p q w", q=Q)).then_inc(s_blk[k], 16)
            wait_alone(eng, c, s_blk[k], pairs * 16)

        @block.sync
        def _(sp):
            sp.dma_start(ei[:, 0, :], x_src.rearrange("(p c) -> p c", p=ER)).then_inc(s_ld, 16)
            sp.dma_start(ei[:, 1, :], x_dst.rearrange("(p c) -> p c", p=ER)).then_inc(s_ld, 16)
            sp.dma_start(ei[:, 2, :], x_w.bitcast(I32).rearrange("(p c) -> p c", p=ER)).then_inc(s_ld, 16)
            sp.wait_ge(s_il, 1)
            sp.dma_start(d["edges"][0:E, :].rearrange("(p c) w -> p (c w)", p=ER), el[:, :, :].rearrange("p c w -> p (c w)")).then_inc(s_st, 16)
            sp.dma_start(d["edges"][E:E + EB, :].rearrange("(p c) w -> p (c w)", p=128), pad[:, :, :].rearrange("p c w -> p (c w)")).then_inc(s_st, 16)
            load_blocks(sp, 0)

        @block.scalar
        def _(act):
            load_blocks(act, 1)

        @block.gpsimd
        def _(pool):
            o = Order(pool, s_p)
            nc.gpsimd.memset(meta[:, :, :], 0)
            nc.gpsimd.memset(up[:, :], 0.0)
            nc.gpsimd.memset(down[:, :], 0.0)
            nc.gpsimd.memset(before[:, :], 1.0)
            nc.gpsimd.memset(pad[:, :, :], 0)
            nc.gpsimd.iota(tmpi[:, 0:NG + 1], [[G, NG + 1]], base=0, channel_multiplier=0)
            nc.gpsimd.iota(tmpi[0:NG, 256:256 + UM], [[EB, UM]], base=EB, channel_multiplier=0)
            o.link(nc.gpsimd.iota(tmpi[:, 512:512 + UT], [[EB, UT]], base=0, channel_multiplier=0))
            nc.gpsimd.tensor_copy(thr[:, :], tmpi[:, 0:NG + 1])
            nc.gpsimd.tensor_copy(ramp512[:, :], tmpi[0:NG, 256:256 + UM])
            nc.gpsimd.tensor_copy(e0r[:, :], tmpi[:, 512:512 + UT])
            nc.gpsimd.memset(pad[:, :, 1:2], N + G)
            o.link(nc.gpsimd.tensor_scalar(thrp[:, :], c["lane"][0:NG + 1, :], float(G), 0.0, ALU.mult, ALU.add))
            o.link(nc.gpsimd.affine_select(out=up[:, :], in_=up[:, :], compare_op=ALU.not_equal, fill=1.0,
                                           base=-1, pattern=[[-1, NG]], channel_multiplier=1))
            o.link(nc.gpsimd.affine_select(out=up[:, :], in_=up[:, :], compare_op=ALU.not_equal, fill=-1.0,
                                           base=0, pattern=[[-1, NG]], channel_multiplier=1))
            o.link(nc.gpsimd.affine_select(out=down[:, :], in_=down[:, :], compare_op=ALU.not_equal, fill=1.0,
                                           base=0, pattern=[[-1, NG]], channel_multiplier=1))
            o.link(nc.gpsimd.affine_select(out=down[:, :], in_=down[:, :], compare_op=ALU.not_equal, fill=-1.0,
                                           base=1, pattern=[[-1, NG]], channel_multiplier=1))
            o.link(nc.gpsimd.affine_select(out=before[:, :], in_=before[:, :], compare_op=ALU.is_gt, fill=0.0,
                                           base=0, pattern=[[1, NG]], channel_multiplier=-1))
            pool.wait_ge(s_ask, 1)
            pool.indirect_dma_start(found[:, :], None, x_dst.rearrange("(p c) -> p c", p=ER),
                                    bass.IndirectOffsetOnAxis(ap=rowi[:, 0:1], axis=0)).then_inc(s_row, 16)
            pool.wait_ge(s_row, 16)

        @block.tensor
        def _(pe):
            steps = [(ps[0:NG + 1, 0, 0:1], below[:, :], c["ones"][0:ER, 0:1]),
                     (ps[0:NG, 1, 0:1], up[:, :], start[:, :]),
                     (ps[0:NG, 0, 0:1], before[:, :], nblk[:, :]),
                     (ps[0:1, 1, 0:1], nblk[:, :], c["ones"][0:NG, 0:1]),
                     (ps[0:NG, 0, 0:1], down[:, :], v[:, :]),
                     (ps[:, 1, 0:UT], c["ones"][0:NG, :], begun[:, :]),
                     (ps[:, 0, 0:UT], c["ones"][0:NG, :], begun_v[:, :])]
            pe.wait_ge(s_p, 7)
            for n, (out, lhs, rhs) in enumerate(steps):
                pe.wait_ge(s_in, n + 1)
                nc.tensor.matmul(out, lhs, rhs, start=True, stop=True).then_inc(s_mm, 1)

        @block.vector
        def _(dve):
            o = Order(dve, s_v)
            vec = nc.vector
            dve.wait_ge(s_ld, 48)
            dve.wait_ge(s_p, 2)
            for w in range(3):
                vec.tensor_copy(el[:, :, w], ei[:, w, :])
            vec.memset(el[:, :, 3:4], 0).then_inc(s_il, 1)
            vec.memset(hits[:, :], 0.0)
            o.link(vec.tensor_copy(first[:, :], ei[:, 1, 0:1]))
            vec.tensor_scalar(below[:, :], thr[0:ER, :], first[:, 0:1], None, ALU.is_gt).then_inc(s_in, 1)
            dve.wait_ge(s_mm, 1)
            o.link(vec.tensor_scalar(rowf[:, :], ps[0:NG + 1, 0, 0:1], -1.0, 0.0, ALU.add, ALU.max))
            vec.tensor_copy(rowi[:, :], rowf[:, :]).then_inc(s_ask, 1)
            dve.wait_ge(s_row, 16)
            o.link(vec.tensor_copy(foundf[:, :], found[:, :]))
            o.link(vec.tensor_scalar(hits[0:NG + 1, :], foundf[:, :], thrp[:, 0:1], 0.0, ALU.is_lt, ALU.add, accum_out=cnt[:, :]))
            vec.scalar_tensor_tensor(start[:, :], rowf[:, :], float(EC), cnt[:, :], ALU.mult, ALU.add).then_inc(s_in, 1)
            dve.wait_ge(s_mm, 2)
            o.link(vec.tensor_copy(size[:, :], ps[0:NG, 1, 0:1]))
            o.link(vec.tensor_scalar(hits[0:NG, 0:UM], ramp512[:, :], size[:, 0:1], 1.0, ALU.is_lt, ALU.add, accum_out=nblk[:, :]))
            vec.tensor_copy(size[:, :], nblk[:, :]).then_inc(s_in, 1)
            dve.wait_ge(s_mm, 3)
            vec.tensor_copy(base[:, :], ps[0:NG, 0, 0:1]).then_inc(s_in, 1)
            dve.wait_ge(s_in, 4)
            dve.wait_ge(s_mm, 4)
            o.link(vec.tensor_scalar(prs[:, 0:1], ps[0:1, 1, 0:1], 0.5, None, ALU.mult))
            o.link(vec.tensor_scalar(hits[0:1, 0:UM], c["ramp"][0:1, 0:UM], prs[:, 0:1], 0.0, ALU.is_lt, ALU.add, accum_out=prs[:, 1:2]))
            o.link(vec.tensor_copy(c["pairs_i"][:, :], prs[:, 1:2]))
            o.link(vec.tensor_scalar(prs[:, 0:1], ps[0:1, 1, 0:1], 0.25, -0.5, ALU.mult, ALU.add))
            o.link(vec.tensor_scalar(hits[0:1, 0:UM], c["ramp"][0:1, 0:UM], prs[:, 0:1], 0.0, ALU.is_lt, ALU.add, accum_out=prs[:, 1:2]))
            o.link(vec.tensor_copy(c["quads_i"][:, :], prs[:, 1:2]))
            vec.scalar_tensor_tensor(v[:, :], base[:, :], -float(EB), start[0:NG, :], ALU.mult, ALU.add).then_inc(s_in, 1)
            dve.wait_ge(s_mm, 5)
            o.link(vec.tensor_copy(dv[:, :], ps[0:NG, 0, 0:1]))
            vec.tensor_scalar(begun[:, :], c["ramp"][0:NG, 0:UT], base[:, 0:1], None, ALU.is_ge).then_inc(s_in, 1)
            dve.wait_ge(s_in, 6)
            vec.tensor_scalar(begun_v[:, :], begun[:, :], dv[:, 0:1], None, ALU.mult).then_inc(s_in, 1)
            dve.wait_ge(s_mm, 6)
            o.link(vec.tensor_scalar(gof[:, :], ps[:, 1, 0:UT], -1.0, None, ALU.add))
            dve.wait_ge(s_mm, 7)
            o.link(vec.tensor_tensor(e0f[:, :], ps[:, 0, 0:UT], e0r[:, :], ALU.add))
            o.link(vec.tensor_scalar(e0f[:, :], e0f[:, :], float(E), None, ALU.min))
            o.link(vec.tensor_copy(c["group_i"][:, :], gof[0:1, :]))
            vec.tensor_copy(e0i[:, :], e0f[0:1, :]).then_inc(s_tab, 1)
            vec.memset(c["goes_on"][:, 0:1], 0.0)
            o.link(vec.tensor_tensor(c["goes_on"][:, 1:UT], gof[:, 1:UT], gof[:, 0:UT - 1], ALU.is_equal))
            o.link(vec.tensor_scalar(gof[:, :], gof[:, :], float(G), None, ALU.mult))
            o.link(vec.scalar_tensor_tensor(c["self_at"][:, :], c["goes_on"][:, :], -BIG, gof[:, :], ALU.mult, ALU.add))
            np_ = dve.value_load(c["pairs_i"][0:1, 0:1], min_val=1, max_val=UM // 2)
            for k in range(2):
                dve.wait_ge(s_blk[k], np_ * 16)
            vec.tensor_copy(c["e_idx"][:, :], meta[:, :, 0])
            vec.tensor_copy(c["e_w"][:, :].bitcast(I32), meta[:, :, 2])
            vec.tensor_copy(tmp[:, :], meta[:, :, 0])
            o.link(vec.tensor_copy(c["e_dst"][:, :], meta[:, :, 1]))
            o.link(vec.tensor_scalar(sq[:, :], tmp[:, :], 1.0 / T, None, ALU.mult))
            o.link(vec.tensor_copy(tmpi[:, :], sq[:, :]))
            o.link(vec.tensor_copy(sq[:, :], tmpi[:, :]))
            r = c["e_row"]
            o.link(vec.scalar_tensor_tensor(r[:, :], sq[:, :], -float(T), tmp[:, :], ALU.mult, ALU.add))
            o.link(vec.tensor_scalar(tmp[:, :], r[:, :], 0.0, None, ALU.is_lt))
            o.link(vec.tensor_tensor(sq[:, :], sq[:, :], tmp[:, :], ALU.subtract))
            o.link(vec.scalar_tensor_tensor(r[:, :], tmp[:, :], float(T), r[:, :], ALU.mult, ALU.add))
            o.link(vec.tensor_scalar(tmp[:, :], r[:, :], float(T), None, ALU.is_ge))
            o.link(vec.tensor_tensor(sq[:, :], sq[:, :], tmp[:, :], ALU.add))
            o.link(vec.scalar_tensor_tensor(r[:, :], tmp[:, :], -float(T), r[:, :], ALU.mult, ALU.add))
            dl = c["e_dst"]
            o.link(vec.tensor_tensor(dl[:, :].rearrange("p (u q) -> p u q", q=Q), dl[:, :].rearrange("p (u q) -> p u q", q=Q),
                                     gof[:, :].unsqueeze(2).to_broadcast([128, UT, Q]), ALU.subtract))
            o.link(vec.tensor_scalar(tmp[:, :], dl[:, :], 0.0, None, ALU.is_ge))
            o.link(vec.scalar_tensor_tensor(tmp[:, :], dl[:, :], float(G), tmp[:, :], ALU.is_lt, ALU.mult))
            qq = c["e_cell"]
            o.link(vec.scalar_tensor_tensor(qq[:, :], sq[:, :], float(G), dl[:, :], ALU.mult, ALU.add))
            o.link(vec.scalar_tensor_tensor(qq[:, :], qq[:, :], 1.0, tmp[:, :], ALU.add, ALU.mult))
            o.link(vec.tensor_scalar(qq[:, :], qq[:, :], -1.0, None, ALU.add))


def build_adjacency(nc, c, d):
    from contextlib import ExitStack
    with ExitStack() as ctx:
        def sb(name, shape, dt=F32):
            return ctx.enter_context(nc.sbuf_tensor(name, shape, dt))
        H1 = 13 * G
        H2 = NS * G - H1
        ohr = sb("source_onehot", [128, 2, Q, 128])
        cell = sb("weighted_cell", [128, 2, Q, NS * G])
        selfd = sb("self_loop_distance", [128, NS * G])
        selfi = sb("self_loop_distance_i", [128, NS * G], I32)
        part = sb("adjacency_part", [128, 2, NS * G])
        cur = sb("adjacency_tile", [128, 2, NS * G])
        acc = [ctx.enter_context(nc.psum_tensor(f"adjacency_sum_{k}", [128, 2, 512], F32)) for k in range(2)]
        s_p = c["sems"].take("build_pool_step")
        s_oh = [c["sems"].take(f"onehots_ready_{k}") for k in range(2)]
        s_mm = [c["sems"].take(f"adjacency_summed_{k}") for k in range(2)]
        s_pf = [c["sems"].take(f"adjacency_sum_read_{k}") for k in range(2)]
        s_cur = [c["sems"].take(f"adjacency_tile_ready_{k}") for k in range(2)]
        s_st = [c["sems"].take(f"adjacency_tile_stored_{k}") for k in range(2)]
        block = ctx.enter_context(nc.Block())

        def pair_count(eng):
            return eng.value_load(c["pairs_i"][0:1, 0:1], min_val=1, max_val=UM // 2)

        @block.gpsimd
        def _(pool):
            o = Order(pool, s_p)
            nc.gpsimd.iota(selfi[:, :], [[T, NS], [-1, G]], base=0, channel_multiplier=1)
            nc.gpsimd.memset(ohr[:, :, :, :], 0.0)
            nc.gpsimd.memset(cur[:, :, :], 0.0)
            o.link(nc.gpsimd.memset(part[:, :, :], 0.0))
            nc.gpsimd.memset(ohr[:, :, :, T:T + 1], 1.0)
            o.link(nc.gpsimd.tensor_copy(selfd[:, :], selfi[:, :]))
            o.link(nc.gpsimd.affine_select(out=selfd[:, :], in_=selfd[:, :], compare_op=ALU.is_gt, fill=-3 * BIG,
                                           base=T, pattern=[[0, NS * G]], channel_multiplier=-1))

        @block.vector
        def _(dve):
            vec = nc.vector

            def onehots(u, k):
                for q in range(Q):
                    col = bass.ds(u * Q + q, 1)
                    vec.tensor_scalar(ohr[:, k, q, 0:T], c["ramp"][:, 0:T], c["e_row"][:, col], None, ALU.is_equal)
                    last = vec.tensor_scalar(cell[:, k, q, :], c["ramp"][:, 0:NS * G], c["e_cell"][:, col],
                                             c["e_w"][:, col], ALU.is_equal, ALU.mult)
                last.then_inc(s_oh[k], 1)

            def finish(i, u, k):
                dve.wait_ge(s_mm[k], i + 1)
                vec.scalar_tensor_tensor(part[:, k, 0:H1], selfd[:, 0:H1], c["self_at"][:, bass.ds(u, 1)],
                                         acc[k][:, 0, 0:H1], ALU.is_equal, ALU.add)
                vec.scalar_tensor_tensor(part[:, k, H1:], selfd[:, H1:], c["self_at"][:, bass.ds(u, 1)],
                                         acc[k][:, 1, 0:H2], ALU.is_equal, ALU.add).then_inc(s_pf[k], 1)
                dve.wait_ge(s_pf[k], i + 1)
                dve.wait_ge(s_st[k], i * 16)
                dve.wait_ge(s_cur[1 - k], i + k)
                vec.scalar_tensor_tensor(cur[:, k, :], cur[:, 1 - k, :], c["goes_on"][:, bass.ds(u, 1)],
                                         part[:, k, :], ALU.mult, ALU.add).then_inc(s_cur[k], 1)

            dve.wait_ge(s_p, 3)
            pairs = pair_count(dve)
            onehots(0, 0)
            with dve.Fori(0, pairs) as i:
                dve.wait_ge(s_mm[1], i)
                onehots(2 * i + 1, 1)
                finish(i, 2 * i, 0)
                onehots(2 * i + 2, 0)
                finish(i, 2 * i + 1, 1)

        @block.tensor
        def _(pe):
            pe.wait_ge(s_p, 3)
            pairs = pair_count(pe)
            with pe.Fori(0, pairs) as i:
                for k in range(2):
                    pe.wait_ge(s_oh[k], i + 1)
                    pe.wait_ge(s_pf[k], i)
                    for q in range(Q):
                        nc.tensor.matmul(acc[k][:, 0, 0:H1], ohr[:, k, q, :], cell[:, k, q, 0:H1], start=q == 0, stop=q == Q - 1)
                        last = nc.tensor.matmul(acc[k][:, 1, 0:H2], ohr[:, k, q, :], cell[:, k, q, H1:], start=q == 0, stop=q == Q - 1)
                    last.then_inc(s_mm[k], 1)

        @block.sync
        def _(sp):
            pairs = pair_count(sp)
            with sp.Fori(0, pairs) as i:
                for k in range(2):
                    g = sp.value_load(c["group_i"][0:1, bass.ds(2 * i + k, 1)], min_val=0, max_val=NG - 1)
                    wait_alone(sp, c, s_cur[k], i + 1)
                    wait_alone(sp, c, s_st[1 - k], (i + k) * 16)
                    sp.dma_start(d["adj"][bass.ds(g, 1), :, :].rearrange("o p c -> (o p) c"), cur[:, k, :]).then_inc(s_st[k], 16)
            for k in range(2):
                wait_alone(sp, c, s_st[k], pairs * 16)


def degrees(nc, c, d):
    from contextlib import ExitStack
    with ExitStack() as ctx:
        def sb(name, shape, dt=F32):
            return ctx.enter_context(nc.sbuf_tensor(name, shape, dt))
        sums = sb("degree_parts", [NG, NS * G])
        deg = sb("degree", [NG, G])
        safe = sb("degree_guarded", [NG, G])
        y = sb("inverse_root", [NG, G])
        z = sb("inverse_root_step", [NG, G])
        s_ld = c["sems"].take("degree_parts_loaded")
        s_v = c["sems"].take("degree_vector_step")
        s_a = c["sems"].take("degree_root_ready")
        s_o = c["sems"].take("dinv_ready")
        s_st = c["sems"].take("dinv_stored")
        s_bk = c["sems"].take("dinv_loaded")
        s_in = c["sems"].take("degree_guarded_ready")
        block = ctx.enter_context(nc.Block())

        @block.sync
        def _(sp):
            sp.dma_start(sums[:, :], d["adj"][:, T, :]).then_inc(s_ld, 16)
            sp.wait_ge(s_o, 1)
            sp.dma_start(d["dinv"].rearrange("(g j) -> g j", j=G), y[:, :]).then_inc(s_st, 16)
            sp.wait_ge(s_st, 16)
            with nc.allow_non_contiguous_dma(reason="3125 values, once"):
                sp.dma_start(c["dinv_n"][:, :], d["dinv"].rearrange("(s r) -> r s", r=T)).then_inc(s_bk, 16)
            sp.dma_start(c["dinv_b"][:, :], d["dinv"].unsqueeze(0).to_broadcast([128, N])).then_inc(s_bk, 16)
            sp.wait_ge(s_bk, 32)

        @block.scalar
        def _(act):
            act.wait_ge(s_in, 1)
            nc.scalar.activation(y[:, :], safe[:, :], ACT.Sqrt).then_inc(s_a, 1)

        @block.vector
        def _(dve):
            o = Order(dve, s_v)
            vec = nc.vector
            dve.wait_ge(s_ld, 16)
            o.link(vec.tensor_reduce(deg[:, :], sums[:, :].rearrange("g (s j) -> g j s", j=G), AX.X, ALU.add))
            o.link(vec.tensor_scalar(deg[:, :], deg[:, :], 1.0, None, ALU.add))
            vec.tensor_scalar(safe[:, :], deg[:, :], 1e-30, None, ALU.max).then_inc(s_in, 1)
            dve.wait_ge(s_a, 1)
            o.link(vec.reciprocal(y[:, :], y[:, :]))
            o.link(vec.tensor_tensor(z[:, :], y[:, :], y[:, :], ALU.mult))
            o.link(vec.tensor_tensor(z[:, :], z[:, :], safe[:, :], ALU.mult))
            o.link(vec.tensor_scalar(z[:, :], z[:, :], -0.5, 1.5, ALU.mult, ALU.add))
            o.link(vec.tensor_tensor(y[:, :], y[:, :], z[:, :], ALU.mult))
            vec.scalar_tensor_tensor(y[:, :], deg[:, :], 0.0, y[:, :], ALU.is_gt, ALU.mult).then_inc(s_o, 1)


def shared_tensors(nc):
    def sb(name, shape, dt=F32):
        return nc.alloc_sbuf_tensor(name, shape, dt)
    return {
        "sems": Semaphores(nc), 
        "ramp_i": sb("ramp_i", [128, 640], I32), "ramp": sb("ramp", [128, 640]),
        "lane_i": sb("lane_i", [128, 1], I32), "lane": sb("lane", [128, 1]),
        "ones": sb("ones", [128, 128]), "ident": sb("ident", [128, 128]), "mean_w": sb("mean_w", [128, 128]),
        "pairs_i": sb("block_pairs", [1, 1], I32), "quads_i": sb("block_quads", [1, 1], I32), "group_i": sb("block_group_i", [1, UT], I32),
        "goes_on": sb("block_goes_on", [128, UT]), "self_at": sb("block_self_at", [128, UT]),
        "first_i": sb("block_first_edge", [1, UT], I32),
        "e_idx": sb("edge_src", [128, UT * Q], I32), "e_w": sb("edge_w", [128, UT * Q]),
        "e_row": sb("edge_src_row", [128, UT * Q]), "e_dst": sb("edge_dst_local", [128, UT * Q]),
        "e_cell": sb("edge_cell", [128, UT * Q]),
        "dinv_n": sb("dinv_nodes", [T, NS]), "dinv_b": sb("dinv_all", [128, N]),
        "x_t": sb("x_t", [128, N]), "h_t": sb("h_t", [128, N]),
    }


BLK = 20
NB = NG // BLK
TAIL = NG - NB * BLK
COLS = [(b * BLK * G, BLK * G) for b in range(NB)] + [(NB * BLK * G, TAIL * G)]
EPS = 1e-5
NEG = -float(2 ** 100)
HEADS, HF = 4, 32
SLOPE = 0.2


def scope(nc, stack):
    def sb(name, shape, dt=F32):
        return stack.enter_context(nc.sbuf_tensor(name, shape, dt))

    def pb(name, shape, dt=F32):
        return stack.enter_context(nc.psum_tensor(name, shape, dt))
    return sb, pb


def load_transposed(nc, c, tag, x, out, bias=None):
    from contextlib import ExitStack
    with ExitStack() as ctx:
        sb, pb = scope(nc, ctx)
        xn = sb(tag + "_nodes", [T, NS, D])
        bt = sb(tag + "_bias", [128, 1])
        pt = pb(tag + "_transposed", [128, 2, 4, 128])
        s_ld, s_t, s_c = (c["sems"].take(f"{tag}_{n}") for n in ("loaded", "tiles_transposed", "tiles_copied"))
        block = ctx.enter_context(nc.Block())

        @block.sync
        def _(sp):
            sp.dma_start(xn[:, :, :], x.rearrange("(s r) f -> r s f", r=T)).then_inc(s_ld, 16)
            if bias is not None:
                with nc.allow_non_contiguous_dma(reason="one value to a partition"):
                    sp.dma_start(bt[:, :], bias.unsqueeze(1)).then_inc(s_ld, 16)

        @block.tensor
        def _(pe):
            pe.wait_ge(s_ld, 16 if bias is None else 32)
            for s in range(NS):
                if s % 4 == 0 and s >= 8:
                    pe.wait_ge(s_c, s // 4 - 1)
                t = nc.tensor.transpose(pt[:, s // 4 % 2, s % 4, 0:T], xn[:, s, :], c["ident"][0:T, 0:T])
                if s % 4 == 3 or s == NS - 1:
                    t.then_inc(s_t, 1)

        @block.vector
        def _(dve):
            for q in range(-(-NS // 4)):
                n = min(4, NS - 4 * q)
                dve.wait_ge(s_t, q + 1)
                o, i = out[:, 4 * q * T:(4 * q + n) * T].rearrange("f (s r) -> f s r", r=T), pt[:, q % 2, 0:n, 0:T]
                if bias is None:
                    nc.vector.tensor_copy(o, i).then_inc(s_c, 1)
                else:
                    nc.vector.tensor_scalar(o, i, bt[:, 0:1], None, ALU.add).then_inc(s_c, 1)


def gcn_layers(nc, c, d, tag, weights, bias, norm):
    from contextlib import ExitStack
    L = len(bias)
    with ExitStack() as ctx:
        sb, pb = scope(nc, ctx)
        w = sb(tag + "_weights", [128, L, D])
        vecs = sb(tag + "_vectors", [128, 3, L])
        h = sb(tag + "_scaled_nodes", [T, NS, D])
        ring = sb(tag + "_adjacency", [128, 2, BLK, NS * G])
        tail = sb(tag + "_adjacency_tail", [128, TAIL, NS * G])
        y = sb(tag + "_aggregate", [128, 2, BLK * G])
        eps = sb(tag + "_eps", [128, 1])
        hp = pb(tag + "_node_psum", [128, 2, 4, D])
        op = pb(tag + "_out_psum", [128, 2, 512])
        if norm:
            yb = sb(tag + "_centred", [128, BLK * G])
            sq = sb(tag + "_squares", [128, BLK * G])
            mp = pb(tag + "_moments", [128, 2, 512])
        names = ("weights_loaded", "tail_loaded", "nodes_multiplied", "nodes_scaled", "block_summed",
                 "block_read", "block_biased", "mean_ready", "block_centred", "squares_ready", "variance_ready",
                 "deviation_ready", "block_normed", "vec_step", "block_out", "start_copied")
        (s_w, s_tl, s_hm, s_hs, s_bs, s_br, s_bb, s_mn, s_ct, s_sq, s_vr, s_dv, s_nm, s_v, s_out, s_x0) = (
            c["sems"].take(f"{tag}_{n}") for n in names)
        s_a = [c["sems"].take(f"{tag}_adjacency_loaded_{k}") for k in range(2)]
        NBL = NB + 1
        NHG = -(-NS // 4)
        block = ctx.enter_context(nc.Block())
        HALF = NB // 2
        vec_rows = [bias] + (list(norm) if norm else [])

        @block.sync
        def _(sp):
            for l in range(L):
                sp.dma_start(w[:, l, :], weights[l]).then_inc(s_w, 16)
            with nc.allow_non_contiguous_dma(reason="one value to a partition"):
                for r, rows in enumerate(vec_rows):
                    for l in range(L):
                        sp.dma_start(vecs[:, r, l:l + 1], rows[l].unsqueeze(1)).then_inc(s_w, 16)
            sp.dma_start(tail[:, :, :], d["adj"][NB * BLK:, :, :].rearrange("g p c -> p g c")).then_inc(s_tl, 16)

            def load(b):
                sp.dma_start(ring[:, b % 2, :, :], d["adj"][b * BLK:(b + 1) * BLK, :, :].rearrange("g p c -> p g c")
                             ).then_inc(s_a[b % 2], 16)

            load(0)
            load(1)
            with sp.Fori(0, L - 1) as l:
                for b in range(2, NB + 2):
                    wait_alone(sp, c, s_bs, l * NBL + b - 1)
                    load(b % NB)
            for b in range(2, NB):
                sp.wait_ge(s_bs, (L - 1) * NBL + b - 1)
                load(b)

        LOADS = 16 * L * (1 + len(vec_rows))

        @block.tensor
        def _(pe):
            pe.wait_ge(s_w, LOADS)
            pe.wait_ge(s_tl, 16)

            def moments(l, b, which):
                n = COLS[b][1]
                done = l * NBL + b + 1
                pe.wait_ge(s_bb if which == 0 else s_sq, done)
                src = y[:, b % 2, 0:n] if which == 0 else sq[:, 0:n]
                nc.tensor.matmul(mp[:, which, 0:n], c["mean_w"][:, :], src, start=True, stop=True
                                 ).then_inc(s_mn if which == 0 else s_vr, 1)

            with pe.Fori(0, L) as l:
                pe.wait_ge(s_x0, 1)
                pe.wait_ge(s_out, l * NBL)
                for s in range(NS):
                    q = s // 4
                    if s % 4 == 0:
                        pe.wait_ge(s_hs, l * NHG + q - 1) if q >= 2 else pe.wait_ge(s_hs, l * NHG)
                    m = nc.tensor.matmul(hp[0:T, q % 2, s % 4, :], c["h_t"][:, s * T:(s + 1) * T], w[:, bass.ds(l, 1), :].rearrange("p o f -> p (o f)"),
                                         start=True, stop=True)
                    if s % 4 == 3 or s == NS - 1:
                        m.then_inc(s_hm, 1)
                pe.wait_ge(s_hs, (l + 1) * NHG)
                for b, (_, n) in enumerate(COLS):
                    if b < NB:
                        pe.wait_ge(s_a[b % 2], (l * HALF + b // 2 + 1) * 16)
                    pe.wait_ge(s_br, l * NBL + b - 1) if b >= 1 else pe.wait_ge(s_br, l * NBL)
                    a = ring[:, b % 2, :, :] if b < NB else tail[:, :, :]
                    for s in range(NS):
                        m = nc.tensor.matmul(op[:, b % 2, 0:n], h[:, s, :], a[0:T, :, s * G:(s + 1) * G],
                                             start=s == 0, stop=s == NS - 1)
                        if norm and b >= 1 and s in (8, 17):
                            moments(l, b - 1, 0 if s == 8 else 1)
                    m.then_inc(s_bs, 1)
                if norm:
                    moments(l, NB, 0)
                    moments(l, NB, 1)

        @block.scalar
        def _(act):
            act.wait_ge(s_w, LOADS)
            act.wait_ge(s_x0, 2)
            with act.Fori(0, L) as l:
                for b, (c0, n) in enumerate(COLS):
                    done = l * NBL + b + 1
                    wait_alone(act, c, s_br, done)
                    row = [vecs[:, r, bass.ds(l, 1)] for r in range(3)]
                    yk = y[:, b % 2, 0:n]
                    if not norm:
                        nc.scalar.activation(c["h_t"][:, c0:c0 + n], yk, ACT.Relu, bias=row[0]).then_inc(s_out, 1)
                        continue
                    nc.scalar.activation(yk, yk, ACT.Identity, bias=row[0]).then_inc(s_bb, 1)
                    wait_alone(act, c, s_ct, done)
                    nc.scalar.activation(sq[:, 0:n], yb[:, 0:n], ACT.Square).then_inc(s_sq, 1)
                    wait_alone(act, c, s_vr, done)
                    nc.scalar.activation(sq[:, 0:n], mp[:, 1, 0:n], ACT.Sqrt, bias=eps[:, 0:1]).then_inc(s_dv, 1)
                    wait_alone(act, c, s_nm, done)
                    nc.scalar.activation(c["h_t"][:, c0:c0 + n], yb[:, 0:n], ACT.Gelu, bias=row[2], scale=row[1]
                                         ).then_inc(s_out, 1)

        @block.vector
        def _(dve):
            o = Order(dve, s_v)
            vec = nc.vector
            vec.tensor_copy(c["h_t"][:, :], c["x_t"][:, :]).then_inc(s_x0, 1)
            vec.memset(eps[:, :], EPS).then_inc(s_x0, 1)
            with dve.Fori(0, L) as l:
                for q in range(NHG):
                    n = min(4, NS - 4 * q)
                    dve.wait_ge(s_hm, l * NHG + q + 1)
                    vec.tensor_tensor(h[:, 4 * q:4 * q + n, :], hp[0:T, q % 2, 0:n, :],
                                      c["dinv_n"][:, 4 * q:4 * q + n].unsqueeze(2).to_broadcast([T, n, D]), ALU.mult).then_inc(s_hs, 1)
                for b, (c0, n) in enumerate(COLS):
                    done = l * NBL + b + 1
                    dve.wait_ge(s_bs, done)
                    if b >= 2:
                        dve.wait_ge(s_out, done - 2)
                    yk = y[:, b % 2, 0:n]
                    vec.tensor_tensor(yk, op[:, b % 2, 0:n], c["dinv_b"][:, c0:c0 + n], ALU.mult).then_inc(s_br, 1)
                    if norm:
                        dve.wait_ge(s_mn, done)
                        dve.wait_ge(s_out, done - 1)
                        vec.tensor_tensor(yb[:, 0:n], yk, mp[:, 0, 0:n], ALU.subtract).then_inc(s_ct, 1)
                        dve.wait_ge(s_dv, done)
                        vec.reciprocal(sq[:, 0:n], sq[:, 0:n]).then_inc(s_v, 1)
                        dve.wait_ge(s_v, done)
                        vec.tensor_tensor(yb[:, 0:n], yb[:, 0:n], sq[:, 0:n], ALU.mult).then_inc(s_nm, 1)


def add_and_norm(nc, c, tag, parts):
    from contextlib import ExitStack
    with ExitStack() as ctx:
        sb, pb = scope(nc, ctx)
        t = sb(tag + "_sum", [128, N])
        sq = sb(tag + "_squares", [128, 2, BLK * G])
        eps = sb(tag + "_eps", [128, 1])
        mp = pb(tag + "_moments", [128, 2, 2, 512])
        s_v, s_sum, s_mn, s_ct, s_sq, s_vr, s_dv, s_out, s_e = (c["sems"].take(f"{tag}_{n}") for n in (
            "vec_step", "sum_ready", "mean_ready", "centred", "squares_ready", "variance_ready", "deviation_ready", "out", "eps_ready"))
        block = ctx.enter_context(nc.Block())

        def variance(pe, b):
            n = COLS[b][1]
            pe.wait_ge(s_sq, b + 1)
            if b >= 2:
                pe.wait_ge(s_dv, b - 1)
            nc.tensor.matmul(mp[:, 1, b % 2, 0:n], c["mean_w"][:, :], sq[:, b % 2, 0:n], start=True, stop=True).then_inc(s_vr, 1)

        def deviation(act, b):
            n = COLS[b][1]
            act.wait_ge(s_vr, b + 1)
            nc.scalar.activation(sq[:, b % 2, 0:n], mp[:, 1, b % 2, 0:n], ACT.Sqrt, bias=eps[:, 0:1]).then_inc(s_dv, 1)

        def scale(dve, o, b):
            c0, n = COLS[b]
            dve.wait_ge(s_dv, b + 1)
            o.link(nc.vector.reciprocal(sq[:, b % 2, 0:n], sq[:, b % 2, 0:n]))
            nc.vector.tensor_tensor(c["x_t"][:, c0:c0 + n], t[:, c0:c0 + n], sq[:, b % 2, 0:n], ALU.mult).then_inc(s_out, 1)


        @block.tensor
        def _(pe):
            for b, (c0, n) in enumerate(COLS):
                pe.wait_ge(s_sum, b + 1)
                if b >= 2:
                    pe.wait_ge(s_ct, b - 1)
                nc.tensor.matmul(mp[:, 0, b % 2, 0:n], c["mean_w"][:, :], t[:, c0:c0 + n], start=True, stop=True).then_inc(s_mn, 1)
                if b >= 1:
                    variance(pe, b - 1)
            variance(pe, NB)

        @block.scalar
        def _(act):
            act.wait_ge(s_e, 1)
            for b, (c0, n) in enumerate(COLS):
                act.wait_ge(s_ct, b + 1)
                if b >= 2:
                    act.wait_ge(s_out, b - 1)
                nc.scalar.activation(sq[:, b % 2, 0:n], t[:, c0:c0 + n], ACT.Square).then_inc(s_sq, 1)
                if b >= 1:
                    deviation(act, b - 1)
            deviation(act, NB)

        @block.vector
        def _(dve):
            vec = nc.vector
            o = Order(dve, s_v)
            vec.memset(eps[:, :], EPS).then_inc(s_e, 1)
            for b, (c0, n) in enumerate(COLS):
                cols = slice(c0, c0 + n)
                if len(parts) == 3:
                    o.link(vec.tensor_tensor(t[:, cols], parts[0][:, cols], parts[1][:, cols], ALU.add))
                    vec.tensor_tensor(t[:, cols], t[:, cols], parts[2][:, cols], ALU.add).then_inc(s_sum, 1)
                else:
                    vec.tensor_tensor(t[:, cols], parts[0][:, cols], parts[1][:, cols], ALU.add).then_inc(s_sum, 1)
            for b, (c0, n) in enumerate(COLS):
                cols = slice(c0, c0 + n)
                dve.wait_ge(s_mn, b + 1)
                vec.tensor_tensor(t[:, cols], t[:, cols], mp[:, 0, b % 2, 0:n], ALU.subtract).then_inc(s_ct, 1)
                if b >= 1:
                    scale(dve, o, b - 1)
            scale(dve, o, NB)



def node_tables(nc, c, tag, tables):
    from contextlib import ExitStack
    with ExitStack() as ctx:
        sb, pb = scope(nc, ctx)
        width = sum(b - a for _, (a, b), _ in tables[0][0])
        nt = len(tables)
        w = sb(tag + "_w", [128, nt, width])
        bias = sb(tag + "_bias", [T, nt, width])
        out = sb(tag + "_rows", [T, nt, NS, width])
        split = sb(tag + "_parts", [T, PARTS, NS, width], BF16)
        ready = sb(tag + "_ready", [1, 1])
        CH = 5
        chunks = [slice(t, t + CH) for t in range(0, NS, CH)]
        per = 512 // width
        runs = [(t, s, min(per, NS - s)) for t in range(nt) for s in range(0, NS, per)]
        ps = pb(tag + "_psum", [T, 2, per, width])
        s_w, s_v, s_n, s_b, s_mm, s_o, s_st, s_pt, s_rest = (c["sems"].take(f"{tag}_{n}") for n in (
            "loaded", "vec_step", "weights_ready", "bias_cleared", "tile_multiplied", "rows_ready", "rows_stored", "part_ready", "rest_ready"))
        NRUN = -(-NS // per)
        loads = sum(len(ws) + len(bs) for ws, bs, _ in tables)
        block = ctx.enter_context(nc.Block())

        @block.sync
        def _(sp):
            sp.wait_ge(s_b, 1)
            for t, (ws, bs, _) in enumerate(tables):
                for ap, (a, b), _ in ws:
                    sp.dma_start(w[:, t, a:b], ap).then_inc(s_w, 16)
                for ap, (a, b), _ in bs:
                    sp.dma_start(bias[:, t, a:b], ap.unsqueeze(0).to_broadcast([T, b - a])).then_inc(s_w, 16)
            for p in range(PARTS):
                sp.wait_ge(s_pt, len(chunks) * (p + 1))
                sp.dma_start(tables[0][2][p].rearrange("(s r) f -> r s f", r=T), split[:, p, :, :]).then_inc(s_st, 16)
            for t in range(1, nt):
                sp.wait_ge(s_o, NRUN * (t + 1))
                sp.dma_start(tables[t][2].rearrange("(s r) f -> r s f", r=T), out[:, t, :, :]).then_inc(s_st, 16)
            sp.wait_ge(s_st, 16 * (PARTS + nt - 1))

        @block.scalar
        def _(act):
            for p in range(PARTS):
                for k, ch in enumerate(chunks):
                    if p == 0:
                        act.wait_ge(s_o, min(NRUN, -(-ch.stop // per)))
                    else:
                        act.wait_ge(s_rest, (p - 1) * len(chunks) + k + 1)
                    nc.scalar.copy(split[:, p, ch, :], out[:, 0, ch, :]).then_inc(s_pt, 1)

        @block.vector
        def _(dve):
            o = Order(dve, s_v)
            nc.vector.memset(bias[:, :, :], 0.0).then_inc(s_b, 1)
            dve.wait_ge(s_w, 16 * loads)
            for t, (ws, bs, _) in enumerate(tables):
                for _, (a, b), negate in ws:
                    if negate:
                        o.link(nc.vector.tensor_scalar(w[:, t, a:b], w[:, t, a:b], -1.0, None, ALU.mult))
                for _, (a, b), negate in bs:
                    if negate:
                        o.link(nc.vector.tensor_scalar(bias[:, t, a:b], bias[:, t, a:b], -1.0, None, ALU.mult))
            nc.vector.memset(ready[:, :], 0.0).then_inc(s_n, 1)
            for m, (t, s, n) in enumerate(runs):
                dve.wait_ge(s_mm, m + 1)
                nc.vector.tensor_tensor(out[:, t, s:s + n, :], ps[:, m % 2, 0:n, :],
                                        bias[:, t, :].unsqueeze(1).to_broadcast([T, n, width]), ALU.add).then_inc(s_o, 1)
                if m == NRUN - 1:
                    for p in range(PARTS - 1):
                        for k, ch in enumerate(chunks):
                            dve.wait_ge(s_pt, p * len(chunks) + k + 1)
                            nc.vector.tensor_tensor(out[:, 0, ch, :], out[:, 0, ch, :], split[:, p, ch, :], ALU.subtract).then_inc(s_rest, 1)

        @block.tensor
        def _(pe):
            pe.wait_ge(s_n, 1)
            for m, (t, s0, n) in enumerate(runs):
                if m >= 2:
                    pe.wait_ge(s_o, m - 1)
                for s in range(n):
                    i = nc.tensor.matmul(ps[:, m % 2, s, :], c["x_t"][:, (s0 + s) * T:(s0 + s + 1) * T], w[:, t, :], start=True, stop=True)
                i.then_inc(s_mm, 1)


LAG = 4


def done(i, b):
    return i * 4 + b + 1


def turns(i, b):
    return i + b // 4 + 1


def run_steps(eng, c, step):
    quads = eng.value_load(c["quads_i"][0:1, 0:1], min_val=1, max_val=UM // 4)
    for b in range(-1, LAG):
        step(0, b)
    with eng.Fori(0, quads) as i:
        for b in range(LAG, LAG + 4):
            step(i, b)
    return quads


def gather_blocks(pool, nc, c, table, idx, rows, s_idx, s_got, s_used):
    def gather(i, b):
        k = (b + 1) % 4
        if b + 1 >= 4:
            wait_alone(pool, c, s_used, done(i, b + 1 - 4))
        nc.gpsimd.tensor_copy(idx[:, k, :], c["e_idx"][:, bass.ds((i * 4 + b + 1) * Q, Q)]).then_inc(s_idx, 1)
        wait_alone(pool, c, s_idx, done(i, b + 1))
        for q in range(Q):
            pool.indirect_dma_start(rows[:, k, q, :], None, table, bass.IndirectOffsetOnAxis(ap=idx[:, k, q:q + 1], axis=0)
                                    ).then_inc(s_got[k], 16)
    quads = run_steps(pool, c, gather)
    wait_alone(pool, c, s_got[0], (quads + 2) * 16 * Q)


def attention(nc, c, d, att, bias):
    from contextlib import ExitStack
    with ExitStack() as ctx:
        sb, pb = scope(nc, ctx)
        NH = HEADS * G
        QH = Q * HEADS
        att_b = sb("att_row", [128, D])
        bias_t = sb("att_bias", [128, 1])
        neg = sb("att_mask_value", [128, 1])
        head_of = sb("head_of", [NH, HEADS])
        feature_of = sb("feature_of", [NH, D])
        node_of = sb("node_of", [NH, G])
        ident_b = sb("ident_bf16", [128, 128], BF16)
        begins = sb("block_begins", [128, UT])
        idx = sb("gather_rows", [128, 4, Q], I32)
        xj = sb("source_rows", [128, 4, Q, D])
        hl = sb("group_rows", [PARTS * G, 4, D], BF16)
        oh = sb("node_onehot", [128, 4, Q, G])
        pen = sb("pair_mask", [128, 4, Q, NH], BF16)
        oht = sb("node_onehot_t", [NH, 4, Q * 128])
        ohtb = sb("node_onehot_t_bf16", [PARTS * G, 2, Q * 128], BF16)
        rl = sb("score_terms_positive", [128, 2, Q * D])
        zl = sb("score_terms", [128, Q, D])
        za = sb("weighted_terms", [128, Q, D])
        sc = sb("scores", [128, 4, QH])
        scx = sb("scores_by_pair", [128, Q, NH])
        mx = sb("block_max", [NH, 1])
        mxh = sb("block_max_by_head", [NH, HEADS])
        mxn = sb("block_max_by_node", [NH, G])
        dg = sb("score_less_max", [128, QH])
        df = sb("score_less_max_guarded", [128, 2, QH])
        wt = sb("weights", [128, 2, Q, D])
        msg = sb("messages", [128, 2, Q, D])
        run = sb("running_max", [128, 2, G])
        part = sb("running_sums", [128, 2, 2, G])
        dab = sb("max_changes", [128, 2, 2, G])
        ab = sb("rescale", [128, 2, 2, G])
        t1 = sb("rescaled_run", [128, 2, G])
        t2 = sb("rescaled_block", [128, 2, G])
        den = sb("weight_sum", [128, G])
        inv = sb("weight_sum_inverse", [128, G])
        o_u = sb("group_out_unbiased", [128, G])
        out = sb("group_out", [128, 2, G])
        p_t = pb("onehot_t_psum", [128, 2, 512])
        p_z = pb("score_psum", [128, 2, 512])
        p_m = pb("masked_scores", [128, 2, 512])
        p_g = pb("max_psum", [128, 512])
        p_a = pb("block_sum_psum", [128, 512])
        names = ("inputs_loaded", "pool_step", "begins_ready", "index_copied", "onehot", "pair_mask", "onehot_t", "onehot_t_copied", "terms_sum", "terms_positive",
                 "terms", "weighted_terms", "scores", "scores_by_pair", "masked", "max", "max_split", "max_spread", "less_max_raw", "less_max", "weights",
                 "messages", "block_sum", "run_max", "changes", "rescale", "block_rescaled", "run_updated", "sum_guarded",
                 "sum_inverse", "unbiased", "group_out")
        (s_in, s_p, s_bg, s_ix, s_oh, s_pn, s_T, s_oht, s_z, s_rl, s_zl, s_za, s_sc, s_sx, s_M, s_mx, s_ms, s_G, s_dr, s_d, s_w,
         s_msg, s_A, s_rm, s_ch, s_ex, s_t2, s_run, s_sg, s_si, s_ou, s_O) = (c["sems"].take("att_" + n) for n in names)
        s_g = [c["sems"].take(f"att_sources_gathered_{k}") for k in range(4)]
        s_hl = [c["sems"].take(f"att_group_rows_loaded_{k}") for k in range(4)]
        s_st = [c["sems"].take(f"att_group_out_stored_{k}") for k in range(2)]
        block = ctx.enter_context(nc.Block())

        @block.gpsimd
        def _(pool):
            o = Order(pool, s_p)
            g = nc.gpsimd
            for t in (run, part, dab, head_of, feature_of):
                g.memset(t[tuple(slice(None) for _ in t.shape)], 0.0)
            g.memset(neg[:, :], NEG)
            o.link(g.memset(node_of[:, :], 0.0))
            o.link(g.affine_select(out=head_of[:, :], in_=head_of[:, :], compare_op=ALU.is_gt, fill=1.0, base=0,
                                   pattern=[[G, HEADS]], channel_multiplier=-1))
            o.link(g.affine_select(out=head_of[:, :], in_=head_of[:, :], compare_op=ALU.is_gt, fill=0.0, base=G,
                                   pattern=[[G, HEADS]], channel_multiplier=-1))
            for h in range(HEADS):
                o.link(g.affine_select(out=node_of[:, :], in_=node_of[:, :], compare_op=ALU.not_equal, fill=1.0, base=-h * G,
                                       pattern=[[-1, G]], channel_multiplier=1))
            g.tensor_copy(feature_of[:, :].rearrange("p (h f) -> p h f", h=HEADS), head_of[:, :].unsqueeze(2).to_broadcast([NH, HEADS, HF]))
            o.link(g.tensor_copy(ident_b[:, :], c["ident"][:, :]))
            gather_blocks(pool, nc, c, d["h_r"], idx, xj, s_ix, s_g, s_msg)

        @block.sync
        def _(sp):
            sp.dma_start(att_b[:, :], att.rearrange("o h f -> o (h f)").to_broadcast([128, D])).then_inc(s_in, 16)
            with nc.allow_non_contiguous_dma(reason="one value to a partition"):
                sp.dma_start(bias_t[:, :], bias.unsqueeze(1)).then_inc(s_in, 16)

            def load(i, b):
                g = sp.value_load(c["group_i"][0:1, bass.ds(i * 4 + b, 1)], min_val=0, max_val=NG - 1)
                if b >= 4:
                    wait_alone(sp, c, s_z, done(i, b - 4))
                for p in range(PARTS):
                    sp.dma_start(hl[p * G:(p + 1) * G, b % 4, :], d["h_l"][p, bass.ds(g * G, G), :]).then_inc(s_hl[b % 4], 16)

            load(0, 0)

            def move(i, b):
                load(i, b + 2)
                if b >= 2:
                    g = sp.value_load(c["group_i"][0:1, bass.ds(i * 4 + b - 2, 1)], min_val=0, max_val=NG - 1)
                    wait_alone(sp, c, s_O, done(i, b - 2))
                    if b >= 3:
                        wait_alone(sp, c, s_st[(b - 3) % 2], (i * 2 + (b - 3) // 2 + 1) * 16)
                    sp.dma_start(c["h_t"][:, bass.ds(g * G, G)], out[:, b % 2, :]).then_inc(s_st[b % 2], 16)
            quads = run_steps(sp, c, move)
            wait_alone(sp, c, s_hl[1], (quads + 2) * 16 * PARTS)
            for k in range(2):
                wait_alone(sp, c, s_st[k], (quads * 2 + 1) * 16)

        @block.tensor
        def _(pe):
            pe.wait_ge(s_p, 8)

            def step(i, b):
                n, k, j = (b + 1) % 4, b % 4, (b - 1) % 4
                pe.wait_ge(s_pn, done(i, b + 1))
                if b >= 1:
                    pe.wait_ge(s_oht, done(i, b - 1))
                for q in range(Q):
                    m = nc.tensor.matmul(p_t[0:NH, n % 2, q * 128:(q + 1) * 128], pen[:, n, q, :],
                                         ident_b[:, :], start=True, stop=True)
                m.then_inc(s_T, 1)
                if b >= 1:
                    pe.wait_ge(s_ms, done(i, b - 1))
                    for q in range(Q):
                        nc.tensor.matmul(p_g[:, q * HEADS:(q + 1) * HEADS], oht[:, j, q * 128:(q + 1) * 128], mxh[:, :], start=True, stop=True)
                    nc.tensor.matmul(p_g[:, QH:QH + G], feature_of[:, :], mxn[:, :], start=True, stop=True).then_inc(s_G, 1)
                pe.wait_ge(s_oht, done(i, b + 1))
                pe.wait_ge(s_hl[n], turns(i, b + 1) * 16 * PARTS)
                pe.wait_ge(s_g[n], turns(i, b + 1) * 16 * Q)
                if b >= 1:
                    pe.wait_ge(s_zl, done(i, b - 1))
                nc.tensor.matmul(p_z[:, n % 2, :], c["ident"][:, :], xj[:, n, :, :].rearrange("p q f -> p (q f)"), start=True, stop=False)
                for q in range(Q):
                    m = nc.tensor.matmul(p_z[:, n % 2, q * D:(q + 1) * D], ohtb[0:PARTS * G, n % 2, q * 128:(q + 1) * 128], hl[:, n, :],
                                         start=False, stop=q == Q - 1)
                m.then_inc(s_z, 1)
                if b >= 0:
                    pe.wait_ge(s_sx, done(i, b))
                    if b >= 2:
                        pe.wait_ge(s_mx, done(i, b - 2))
                    for q in range(Q):
                        o = p_m[0:NH, k % 2, q * 128:(q + 1) * 128]
                        nc.tensor.matmul(o, pen[:, k, q, :], ident_b[:, :], start=True, stop=False)
                        m = nc.tensor.matmul(o, scx[:, q, :], c["ident"][:, :], start=False, stop=True)
                    m.then_inc(s_M, 1)
                if b >= 1:
                    pe.wait_ge(s_msg, done(i, b - 1))
                    if b >= 2:
                        pe.wait_ge(s_t2, done(i, b - 2))
                    for q in range(Q):
                        nc.tensor.matmul(p_a[:, 0:G], msg[:, j % 2, q, :], oh[:, j, q, :], start=q == 0, stop=q == Q - 1)
                    for q in range(Q):
                        m = nc.tensor.matmul(p_a[:, G:2 * G], wt[:, j % 2, q, :], oh[:, j, q, :], start=q == 0, stop=q == Q - 1)
                    m.then_inc(s_A, 1)
            run_steps(pe, c, step)

        @block.scalar
        def _(act):
            def mask(i, b):
                wait_alone(act, c, s_oh, done(i, b))
                nc.scalar.activation(pen[:, b % 4, :, :].rearrange("p q (h n) -> p q h n", h=HEADS), oh[:, b % 4, :, :].unsqueeze(2).to_broadcast([128, Q, HEADS, G]),
                                     ACT.Identity, bias=neg[:, 0:1], scale=-NEG).then_inc(s_pn, 1)
            act.wait_ge(s_p, 8)
            mask(0, 0)

            def step(i, b):
                n, j = (b + 1) % 4, (b - 1) % 4
                wait_alone(act, c, s_T, done(i, b + 1))
                nc.scalar.activation(ohtb[:, n % 2, :], p_t[0:PARTS * G, n % 2, :], ACT.Identity, bias=1.0, scale=-1.0 / NEG)
                nc.scalar.activation(oht[:, n, :], p_t[0:NH, n % 2, :], ACT.Identity, bias=1.0, scale=-1.0 / NEG).then_inc(s_oht, 1)
                if b >= 0:
                    wait_alone(act, c, s_sc, done(i, b))
                    if b >= 1:
                        wait_alone(act, c, s_M, done(i, b - 1))
                    nc.scalar.activation(scx[:, :, :].rearrange("p q (h n) -> p (q h) n", h=HEADS), sc[:, b % 4, :].unsqueeze(2).to_broadcast([128, QH, G]),
                                         ACT.Copy).then_inc(s_sx, 1)
                if b >= 1:
                    wait_alone(act, c, s_d, done(i, b - 1))
                    nc.scalar.activation(wt[:, j % 2, :, :].rearrange("p q (h f) -> p (q h) f", h=HEADS), df[:, j % 2, :].unsqueeze(2).to_broadcast([128, QH, HF]),
                                         ACT.Exp).then_inc(s_w, 1)
                    wait_alone(act, c, s_ch, done(i, b - 1))
                    nc.scalar.activation(ab[:, j % 2, :, :], dab[:, j % 2, :, :], ACT.Exp).then_inc(s_ex, 1)
                wait_alone(act, c, s_z, done(i, b + 1))
                nc.scalar.activation(rl[:, n % 2, :], p_z[:, n % 2, :], ACT.Relu, scale=1.0 - SLOPE).then_inc(s_rl, 1)
                mask(i, b + 2)
            run_steps(act, c, step)

        @block.vector
        def _(dve):
            vec = nc.vector
            dve.wait_ge(s_in, 32)
            dve.wait_ge(s_p, 8)
            vec.tensor_scalar(begins[:, :], c["goes_on"][:, :], -NEG, NEG, ALU.mult, ALU.add).then_inc(s_bg, 1)
            dve.wait_ge(s_bg, 1)

            def onehots(i, b):
                vec.tensor_tensor(oh[:, b % 4, :, :], c["ramp"][:, 0:G].unsqueeze(1).to_broadcast([128, Q, G]),
                                  c["e_dst"][:, bass.ds((i * 4 + b) * Q, Q)].unsqueeze(2).to_broadcast([128, Q, G]), ALU.is_equal).then_inc(s_oh, 1)
            onehots(0, 0)

            def step(i, b):
                k, j, e = b % 4, (b - 1) % 4, (b - 2) % 4
                if b >= 1:
                    dve.wait_ge(s_M, done(i, b - 1))
                    vec.tensor_reduce(mx[:, :], p_m[0:NH, j % 2, :], AX.X, ALU.max).then_inc(s_mx, 1)
                    dve.wait_ge(s_mx, done(i, b - 1))
                    vec.tensor_scalar(mxh[:, :], head_of[:, :], mx[:, 0:1], None, ALU.mult)
                    vec.tensor_scalar(mxn[:, :], node_of[:, :], mx[:, 0:1], None, ALU.mult).then_inc(s_ms, 1)
                if b >= 0:
                    dve.wait_ge(s_rl, done(i, b))
                    vec.scalar_tensor_tensor(zl[:, :, :].rearrange("p q f -> p (q f)"), p_z[:, k % 2, :], SLOPE, rl[:, k % 2, :], ALU.mult, ALU.add).then_inc(s_zl, 1)
                    dve.wait_ge(s_zl, done(i, b))
                    vec.tensor_tensor(za[:, :, :], zl[:, :, :], att_b[:, :].unsqueeze(1).to_broadcast([128, Q, D]), ALU.mult).then_inc(s_za, 1)
                    dve.wait_ge(s_za, done(i, b))
                    vec.tensor_reduce(sc[:, k, :], za[:, :, :].rearrange("p q (h f) -> p (q h) f", h=HEADS), AX.X, ALU.add).then_inc(s_sc, 1)
                if b >= 1:
                    dve.wait_ge(s_G, done(i, b - 1))
                    vec.tensor_tensor(dg[:, :], sc[:, j, :], p_g[:, 0:QH], ALU.subtract).then_inc(s_dr, 1)
                    vec.scalar_tensor_tensor(run[:, j % 2, :], run[:, 1 - j % 2, :], begins[:, bass.ds(i * 4 + b - 1, 1)], p_g[:, QH:QH + G], ALU.add, ALU.max
                                             ).then_inc(s_rm, 1)
                    dve.wait_ge(s_dr, done(i, b - 1))
                    vec.tensor_scalar(df[:, j % 2, :], dg[:, :], 0.0, None, ALU.min).then_inc(s_d, 1)
                    dve.wait_ge(s_rm, done(i, b - 1))
                    vec.scalar_tensor_tensor(dab[:, j % 2, 0, :], run[:, 1 - j % 2, :], begins[:, bass.ds(i * 4 + b - 1, 1)], run[:, j % 2, :], ALU.add, ALU.subtract)
                    vec.tensor_tensor(dab[:, j % 2, 1, :], p_g[:, QH:QH + G], run[:, j % 2, :], ALU.subtract).then_inc(s_ch, 1)
                if b >= 2:
                    p = e % 2
                    dve.wait_ge(s_ex, done(i, b - 2))
                    dve.wait_ge(s_A, done(i, b - 2))
                    vec.tensor_tensor(t1[:, :, :], part[:, 1 - p, :, :], ab[:, p, 0, :].unsqueeze(1).to_broadcast([128, 2, G]), ALU.mult)
                    vec.tensor_tensor(t2[:, :, :], p_a[:, 0:2 * G].rearrange("p (a n) -> p a n", a=2),
                                      ab[:, p, 1, :].unsqueeze(1).to_broadcast([128, 2, G]), ALU.mult).then_inc(s_t2, 1)
                    dve.wait_ge(s_t2, done(i, b - 2))
                    vec.tensor_tensor(part[:, p, :, :], t1[:, :, :], t2[:, :, :], ALU.add).then_inc(s_run, 1)
                onehots(i, b + 2)
                if b >= 1:
                    dve.wait_ge(s_w, done(i, b - 1))
                    vec.tensor_tensor(msg[:, j % 2, :, :], xj[:, j, :, :], wt[:, j % 2, :, :], ALU.mult).then_inc(s_msg, 1)
                if b >= 2:
                    p = e % 2
                    dve.wait_ge(s_run, done(i, b - 2))
                    vec.tensor_scalar(den[:, :], part[:, p, 1, :], 1e-16, None, ALU.max).then_inc(s_sg, 1)
                    dve.wait_ge(s_sg, done(i, b - 2))
                    vec.reciprocal(inv[:, :], den[:, :]).then_inc(s_si, 1)
                    dve.wait_ge(s_si, done(i, b - 2))
                    vec.tensor_tensor(o_u[:, :], part[:, p, 0, :], inv[:, :], ALU.mult).then_inc(s_ou, 1)
                    dve.wait_ge(s_ou, done(i, b - 2))
                    if b >= 4:
                        dve.wait_ge(s_st[p], (i * 2 + (b - 4) // 2 + 1) * 16)
                    vec.tensor_scalar(out[:, p, :], o_u[:, :], bias_t[:, 0:1], None, ALU.add).then_inc(s_O, 1)
            run_steps(dve, c, step)


def gated_conv(nc, c, d, ea, w_f, w_s):
    from contextlib import ExitStack
    with ExitStack() as ctx:
        sb, pb = scope(nc, ctx)
        W = 2 * D
        we = sb("edge_weights", [128, W])
        ident_b = sb("gate_ident_bf16", [128, 128], BF16)
        idx = sb("gate_gather_rows", [128, 4, Q], I32)
        xj = sb("gate_source_rows_sb", [128, 4, Q, W])
        hl = sb("gate_group_rows", [PARTS * G, 4, W], BF16)
        e_n = sb("edge_features", [128, 4, Q, D])
        e_t = sb("edge_features_t", [128, 2, Q * 128])
        oh = sb("gate_node_onehot", [128, 4, Q, G])
        ohb = sb("gate_node_onehot_bf16", [128, 4, Q, PARTS * G], BF16)
        oht = sb("gate_node_onehot_t", [PARTS * G, 2, Q * 128], BF16)
        z = sb("gate_core", [128, 2, Q, W])
        lg = sb("gate_core_log", [128, 2, Q, W])
        sp_ = sb("gate_core_softplus", [128, Q, W])
        gt = sb("gate", [128, Q, D])
        msg = sb("gate_messages", [128, 2, Q, D])
        cur = sb("gate_group_sum", [128, 2, G])
        p_o = pb("gate_onehot_t_psum", [128, 512])
        p_e = pb("edge_t_psum", [128, 512])
        p_z = pb("gate_core_psum", [128, 2, 2, 512])
        p_a = pb("gate_sum_psum", [128, 512])
        names = ("weights_loaded", "weights_negated", "pool_step", "index_copied", "onehot_raw", "onehot", "onehot_t", "onehot_t_copied",
                 "edge_t", "edge_t_copied", "core_sum", "core_sum_read", "core_abs", "core_exp", "log", "softplus", "gate", "messages", "block_sum", "group_sum")
        (s_w, s_wn, s_p, s_ix, s_or, s_oh, s_T, s_oht, s_eT, s_et, s_z, s_zr, s_ab, s_ex, s_ln, s_sp, s_gt, s_msg, s_A, s_O) = (
            c["sems"].take("gate_" + n) for n in names)
        s_g = [c["sems"].take(f"gate_sources_gathered_{k}") for k in range(4)]
        s_hl = [c["sems"].take(f"gate_group_rows_loaded_{k}") for k in range(4)]
        s_e = [c["sems"].take(f"gate_edges_loaded_{k}") for k in range(4)]
        s_st = [c["sems"].take(f"gate_group_sum_stored_{k}") for k in range(2)]
        block = ctx.enter_context(nc.Block())

        @block.gpsimd
        def _(pool):
            nc.gpsimd.tensor_copy(ident_b[:, :], c["ident"][:, :]).then_inc(s_p, 1)
            gather_blocks(pool, nc, c, d["p_src"], idx, xj, s_ix, s_g, s_zr)

        @block.sync
        def _(sp):
            sp.dma_start(we[:, 0:D], w_f[2 * D:3 * D, :]).then_inc(s_w, 16)
            sp.dma_start(we[:, D:W], w_s[2 * D:3 * D, :]).then_inc(s_w, 16)

            def load(i, b):
                k = b % 4
                e0 = sp.value_load(c["first_i"][0:1, bass.ds(i * 4 + b, 1)], min_val=0, max_val=E)
                g = sp.value_load(c["group_i"][0:1, bass.ds(i * 4 + b, 1)], min_val=0, max_val=NG - 1)
                if b >= 4:
                    wait_alone(sp, c, s_z, done(i, b - 4))
                sp.dma_start(e_n[:, k, :, :], ea[bass.ds(e0, EB), :].rearrange("(p q) f -> p q f", q=Q)).then_inc(s_e[k], 16)
                for p in range(PARTS):
                    sp.dma_start(hl[p * G:(p + 1) * G, k, :], d["p_dst"][p, bass.ds(g * G, G), :]).then_inc(s_hl[k], 16)

            load(0, 0)

            def move(i, b):
                load(i, b + 2)
                if b >= 1:
                    g = sp.value_load(c["group_i"][0:1, bass.ds(i * 4 + b - 1, 1)], min_val=0, max_val=NG - 1)
                    wait_alone(sp, c, s_O, done(i, b - 1))
                    if b >= 2:
                        wait_alone(sp, c, s_st[b % 2], (i * 2 + (b - 2) // 2 + 1) * 16)
                    sp.dma_start(c["h_t"][:, bass.ds(g * G, G)], cur[:, (b - 1) % 2, :]).then_inc(s_st[(b - 1) % 2], 16)
            quads = run_steps(sp, c, move)
            wait_alone(sp, c, s_hl[1], (quads + 2) * 16 * PARTS)
            wait_alone(sp, c, s_e[1], (quads + 2) * 16)
            wait_alone(sp, c, s_st[0], (quads * 2 + 2) * 16)
            wait_alone(sp, c, s_st[1], (quads * 2 + 1) * 16)

        @block.tensor
        def _(pe):
            pe.wait_ge(s_wn, 1)
            pe.wait_ge(s_p, 1)

            def step(i, b):
                n, k, j = (b + 1) % 4, b % 4, (b - 1) % 4
                pe.wait_ge(s_oh, done(i, b + 1))
                if b >= 0:
                    pe.wait_ge(s_oht, done(i, b))
                for q in range(Q):
                    m = nc.tensor.matmul(p_o[0:PARTS * G, q * 128:(q + 1) * 128], ohb[:, n, q, :], ident_b[:, :], start=True, stop=True)
                m.then_inc(s_T, 1)
                pe.wait_ge(s_e[n], turns(i, b + 1) * 16)
                if b >= 0:
                    pe.wait_ge(s_et, done(i, b))
                for q in range(Q):
                    m = nc.tensor.transpose(p_e[:, q * 128:(q + 1) * 128], e_n[:, n, q, :], c["ident"][:, :])
                m.then_inc(s_eT, 1)
                pe.wait_ge(s_et, done(i, b + 1))
                pe.wait_ge(s_oht, done(i, b + 1))
                pe.wait_ge(s_hl[n], turns(i, b + 1) * 16 * PARTS)
                if b >= 1:
                    pe.wait_ge(s_zr, done(i, b - 1))
                for q in range(Q):
                    o = p_z[:, n % 2, q // 2, (q % 2) * W:(q % 2 + 1) * W]
                    nc.tensor.matmul(o, e_t[:, n % 2, q * 128:(q + 1) * 128], we[:, :], start=True, stop=False)
                    m = nc.tensor.matmul(o, oht[:, n % 2, q * 128:(q + 1) * 128], hl[:, n, :], start=False, stop=True)
                m.then_inc(s_z, 1)
                if b >= 1:
                    pe.wait_ge(s_msg, done(i, b - 1))
                    if b >= 2:
                        pe.wait_ge(s_O, done(i, b - 2))
                    for q in range(Q):
                        m = nc.tensor.matmul(p_a[:, 0:G], msg[:, j % 2, q, :], oh[:, j, q, :], start=q == 0, stop=q == Q - 1)
                    m.then_inc(s_A, 1)
            run_steps(pe, c, step)

        @block.scalar
        def _(act):
            nc.scalar.preload_act_table_set("natural_log_exp_and_others")

            def step(i, b):
                n, k, j = (b + 1) % 4, b % 4, (b - 1) % 4
                wait_alone(act, c, s_eT, done(i, b + 1))
                nc.scalar.copy(e_t[:, n % 2, :], p_e[:, :]).then_inc(s_et, 1)
                if b >= 0:
                    wait_alone(act, c, s_zr, done(i, b))
                    nc.scalar.activation(lg[:, k % 2, :, :], z[:, k % 2, :, :], ACT.Abs).then_inc(s_ab, 1)
                if b >= 1:
                    wait_alone(act, c, s_sp, done(i, b - 1))
                    nc.scalar.activation(gt[:, :, :], sp_[:, :, 0:D], ACT.Exp, scale=-1.0).then_inc(s_gt, 1)
                if b >= 0:
                    wait_alone(act, c, s_ab, done(i, b))
                    nc.scalar.activation(lg[:, k % 2, :, :], lg[:, k % 2, :, :], ACT.Exp, scale=-1.0).then_inc(s_ex, 1)
                    wait_alone(act, c, s_ex, done(i, b))
                    nc.scalar.activation(lg[:, k % 2, :, :], lg[:, k % 2, :, :], ACT.Ln, bias=1.0).then_inc(s_ln, 1)
            run_steps(act, c, step)

        @block.vector
        def _(dve):
            vec = nc.vector
            dve.wait_ge(s_w, 32)
            vec.memset(cur[:, :, :], 0.0)
            vec.tensor_scalar(we[:, 0:D], we[:, 0:D], -1.0, None, ALU.mult).then_inc(s_wn, 1)
            dve.wait_ge(s_wn, 1)

            def onehots(i, b):
                vec.tensor_tensor(oh[:, b % 4, :, :], c["ramp"][:, 0:G].unsqueeze(1).to_broadcast([128, Q, G]),
                                  c["e_dst"][:, bass.ds((i * 4 + b) * Q, Q)].unsqueeze(2).to_broadcast([128, Q, G]), ALU.is_equal).then_inc(s_or, 1)
                dve.wait_ge(s_or, done(i, b))
                vec.tensor_copy(ohb[:, b % 4, :, :].rearrange("p q (a n) -> p q a n", a=PARTS),
                                oh[:, b % 4, :, :].unsqueeze(2).to_broadcast([128, Q, PARTS, G])).then_inc(s_oh, 1)
            onehots(0, 0)

            def step(i, b):
                n, k, j = (b + 1) % 4, b % 4, (b - 1) % 4
                dve.wait_ge(s_T, done(i, b + 1))
                vec.tensor_copy(oht[:, n % 2, :], p_o[0:PARTS * G, :]).then_inc(s_oht, 1)
                if b >= 0:
                    dve.wait_ge(s_z, done(i, b))
                    dve.wait_ge(s_g[k], turns(i, b) * 16 * Q)
                    vec.tensor_tensor(z[:, k % 2, :, :], p_z[:, k % 2, :, :].rearrange("p a (b f) -> p (a b) f", b=2), xj[:, k, :, :], ALU.add).then_inc(s_zr, 1)
                if b >= 1:
                    dve.wait_ge(s_ln, done(i, b - 1))
                    vec.scalar_tensor_tensor(sp_[:, :, :], z[:, j % 2, :, :], 0.0, lg[:, j % 2, :, :], ALU.max, ALU.add).then_inc(s_sp, 1)
                onehots(i, b + 2)
                if b >= 1:
                    dve.wait_ge(s_gt, done(i, b - 1))
                    vec.tensor_tensor(msg[:, j % 2, :, :], gt[:, :, :], sp_[:, :, D:W], ALU.mult).then_inc(s_msg, 1)
                    dve.wait_ge(s_A, done(i, b - 1))
                    if b >= 3:
                        dve.wait_ge(s_st[j % 2], (i * 2 + (b - 3) // 2 + 1) * 16)
                    if b >= 2:
                        dve.wait_ge(s_O, done(i, b - 2))
                    vec.scalar_tensor_tensor(cur[:, j % 2, :], cur[:, 1 - j % 2, :], c["goes_on"][:, bass.ds(i * 4 + b - 1, 1)], p_a[:, 0:G],
                                             ALU.mult, ALU.add).then_inc(s_O, 1)
            run_steps(dve, c, step)


def residual_branch(nc, c, w_res, b_res, g_res, beta_res, out):
    from contextlib import ExitStack
    with ExitStack() as ctx:
        sb, pb = scope(nc, ctx)
        w = sb("res_w", [128, D])
        vecs = sb("res_vectors", [128, 3])
        y = sb("res_rows", [128, N])
        sq = sb("res_squares", [128, 2, BLK * G])
        eps = sb("res_eps", [128, 1])
        yp = pb("res_psum", [128, 2, 512])
        mp = pb("res_moments", [128, 2, 2, 512])
        s_ld, s_y, s_b, s_mn, s_ct, s_sq, s_vr, s_dv, s_v, s_nm, s_e, s_o = (c["sems"].take("res_" + n) for n in (
            "loaded", "multiplied", "biased", "mean_ready", "centred", "squares_ready", "variance_ready", "deviation_ready",
            "vec_step", "normed", "eps_ready", "out"))
        block = ctx.enter_context(nc.Block())

        @block.sync
        def _(sp):
            sp.dma_start(w[:, :], w_res).then_inc(s_ld, 16)
            with nc.allow_non_contiguous_dma(reason="one value to a partition"):
                for r, row in enumerate((b_res, g_res, beta_res)):
                    sp.dma_start(vecs[:, r:r + 1], row.unsqueeze(1)).then_inc(s_ld, 16)

        @block.tensor
        def _(pe):
            pe.wait_ge(s_ld, 64)
            for b, (c0, n) in enumerate(COLS):
                if b >= 2:
                    pe.wait_ge(s_b, b - 1)
                nc.tensor.matmul(yp[:, b % 2, 0:n], w[:, :], c["x_t"][:, c0:c0 + n], start=True, stop=True).then_inc(s_y, 1)
            for b, (c0, n) in enumerate(COLS):
                pe.wait_ge(s_b, b + 1)
                if b >= 2:
                    pe.wait_ge(s_ct, b - 1)
                nc.tensor.matmul(mp[:, 0, b % 2, 0:n], c["mean_w"][:, :], y[:, c0:c0 + n], start=True, stop=True).then_inc(s_mn, 1)
                pe.wait_ge(s_sq, b + 1)
                if b >= 2:
                    pe.wait_ge(s_dv, b - 1)
                nc.tensor.matmul(mp[:, 1, b % 2, 0:n], c["mean_w"][:, :], sq[:, b % 2, 0:n], start=True, stop=True).then_inc(s_vr, 1)

        @block.scalar
        def _(act):
            act.wait_ge(s_ld, 64)
            act.wait_ge(s_e, 1)
            for b, (c0, n) in enumerate(COLS):
                act.wait_ge(s_y, b + 1)
                nc.scalar.activation(y[:, c0:c0 + n], yp[:, b % 2, 0:n], ACT.Identity, bias=vecs[:, 0:1]).then_inc(s_b, 1)
            for b, (c0, n) in enumerate(COLS):
                act.wait_ge(s_ct, b + 1)
                if b >= 2:
                    act.wait_ge(s_nm, b - 1)
                nc.scalar.activation(sq[:, b % 2, 0:n], y[:, c0:c0 + n], ACT.Square).then_inc(s_sq, 1)
                act.wait_ge(s_vr, b + 1)
                nc.scalar.activation(sq[:, b % 2, 0:n], mp[:, 1, b % 2, 0:n], ACT.Sqrt, bias=eps[:, 0:1]).then_inc(s_dv, 1)
            for b, (c0, n) in enumerate(COLS):
                act.wait_ge(s_nm, b + 1)
                nc.scalar.activation(out[:, c0:c0 + n], y[:, c0:c0 + n], ACT.Gelu, bias=vecs[:, 2:3], scale=vecs[:, 1:2]).then_inc(s_o, 1)

        @block.vector
        def _(dve):
            o = Order(dve, s_v)
            nc.vector.memset(eps[:, :], EPS).then_inc(s_e, 1)
            for b, (c0, n) in enumerate(COLS):
                cols = slice(c0, c0 + n)
                dve.wait_ge(s_mn, b + 1)
                nc.vector.tensor_tensor(y[:, cols], y[:, cols], mp[:, 0, b % 2, 0:n], ALU.subtract).then_inc(s_ct, 1)
                dve.wait_ge(s_dv, b + 1)
                o.link(nc.vector.reciprocal(sq[:, b % 2, 0:n], sq[:, b % 2, 0:n]))
                nc.vector.tensor_tensor(y[:, cols], y[:, cols], sq[:, b % 2, 0:n], ALU.mult).then_inc(s_nm, 1)


def store_nodes(nc, c, out):
    from contextlib import ExitStack
    with ExitStack() as ctx:
        sb, pb = scope(nc, ctx)
        on = sb("out_nodes", [T, NS, D])
        pt = pb("out_psum", [T, 2, 4, D])
        s_t, s_c, s_st = (c["sems"].take("out_" + n) for n in ("tiles_transposed", "tiles_copied", "stored"))
        block = ctx.enter_context(nc.Block())

        @block.tensor
        def _(pe):
            for s in range(NS):
                if s % 4 == 0 and s >= 8:
                    pe.wait_ge(s_c, s // 4 - 1)
                t = nc.tensor.transpose(pt[:, s // 4 % 2, s % 4, :], c["x_t"][:, s * T:(s + 1) * T], c["ident"][:, :])
                if s % 4 == 3 or s == NS - 1:
                    t.then_inc(s_t, 1)

        @block.vector
        def _(dve):
            for q in range(-(-NS // 4)):
                n = min(4, NS - 4 * q)
                dve.wait_ge(s_t, q + 1)
                nc.vector.tensor_copy(on[:, 4 * q:4 * q + n, :], pt[:, q % 2, 0:n, :]).then_inc(s_c, 1)

        @block.sync
        def _(sp):
            sp.wait_ge(s_c, -(-NS // 4))
            sp.dma_start(out.rearrange("(s r) f -> r s f", r=T), on[:, :, :]).then_inc(s_st, 16)
            sp.wait_ge(s_st, 16)


def graph_network(nc, a, out):
    c = shared_tensors(nc)
    c["sems"].begin(c)
    d = dram_scratch(nc)
    constants(nc, c)
    prepare(nc, c, d, a["src"], a["dst"], a["edge_weight"])
    build_adjacency(nc, c, d)
    degrees(nc, c, d)
    c["sems"].end()
    load_transposed(nc, c, "x", a["x"], c["x_t"])

    gcn_layers(nc, c, d, "gcn", [a[f"L0_gnn_W{i}"] for i in (1, 2, 3)], [a[f"L0_gnn_b{i}"] for i in (1, 2, 3)], None)
    add_and_norm(nc, c, "norm0", [c["x_t"], c["h_t"]])
    c["sems"].end()

    node_tables(nc, c, "gat_tables", [([(a["L1_gnn_weight_l"], (0, D), False)], [], d["h_l"]),
                                      ([(a["L1_gnn_weight_r"], (0, D), False)], [], d["h_r"])])
    attention(nc, c, d, a["L1_gnn_att"], a["L1_gnn_bias"])
    add_and_norm(nc, c, "norm1", [c["x_t"], c["h_t"]])
    c["sems"].end()

    wf, ws = a["L2_gnn_W_f"], a["L2_gnn_W_s"]
    node_tables(nc, c, "gate_tables", [([(wf[0:D, :], (0, D), True), (ws[0:D, :], (D, 2 * D), False)],
                                        [(a["L2_gnn_b_f"], (0, D), True), (a["L2_gnn_b_s"], (D, 2 * D), False)], d["p_dst"]),
                                       ([(wf[D:2 * D, :], (0, D), True), (ws[D:2 * D, :], (D, 2 * D), False)], [], d["p_src"])])
    gated_conv(nc, c, d, a["edge_attr_128"], wf, ws)
    add_and_norm(nc, c, "norm2", [c["x_t"], c["x_t"], c["h_t"]])
    c["sems"].end()

    L = a["L3_gnn_conv_W"].shape[0]
    rows = {n: [a["L3_gnn_" + n][l] for l in range(L)] for n in ("conv_W", "conv_b", "ln_g", "ln_b")}
    gcn_layers(nc, c, d, "deep", rows["conv_W"], rows["conv_b"], (rows["ln_g"], rows["ln_b"]))
    with nc.sbuf_tensor("identity_branch", [128, N], F32) as branch:
        residual_branch(nc, c, a["L3_gnn_res_W"], a["L3_gnn_res_b"], a["L3_gnn_res_g"], a["L3_gnn_res_beta"], branch)
        add_and_norm(nc, c, "norm3", [c["x_t"], c["h_t"], branch])
    store_nodes(nc, c, out)


_INS = ['x', 'src', 'dst', 'edge_attr_128', 'edge_weight', 'L0_gnn_W1', 'L0_gnn_b1', 'L0_gnn_W2', 'L0_gnn_b2', 'L0_gnn_W3', 'L0_gnn_b3',
        'L1_gnn_weight_l', 'L1_gnn_weight_r', 'L1_gnn_att', 'L1_gnn_bias', 'L2_gnn_W_f', 'L2_gnn_b_f', 'L2_gnn_W_s', 'L2_gnn_b_s',
        'L3_gnn_conv_W', 'L3_gnn_conv_b', 'L3_gnn_ln_g', 'L3_gnn_ln_b', 'L3_gnn_res_W', 'L3_gnn_res_b', 'L3_gnn_res_g', 'L3_gnn_res_beta']


def kernel(**inputs):
    import numpy as _np
    import concourse.bacc as _bacc
    from concourse import mybir as _mybir
    from concourse.bass_utils import run_bass_kernel_spmd as _run

    nc = _bacc.Bacc("TRN2", target_bir_lowering=False, num_devices=1)
    arrays, args = {}, {}
    for name in _INS:
        a = _np.ascontiguousarray(inputs[name])
        if name == 'edge_attr_128':
            rows = _np.zeros((E + EB, D), a.dtype)
            rows[:E] = a
            a = rows
        arrays[f"in_{name}_dram"] = a
        args[name] = nc.dram_tensor(f"in_{name}_dram", a.shape, _mybir.dt.from_np(a.dtype), kind="ExternalInput").ap()
    out = nc.dram_tensor("out_dram", (N, D), F32, kind="ExternalOutput").ap()
    graph_network(nc, args, out)
    r = _run(nc, [arrays], core_ids=[0])
    return r.results[0]["out_dram"]
```

```python
import numpy as np
import concourse.bass as bass
from concourse import mybir

F32 = mybir.dt.float32
I32 = mybir.dt.int32
BF16 = mybir.dt.bfloat16
ALU = mybir.AluOpType
ACT = mybir.ActivationFunctionType
AX = mybir.AxisListType

N = 3125
E = 50000
D = 128
T = 125
NS = N // T
G = 25
NG = N // G
Q = 4
EB = 128 * Q
UM = -(-E // EB) + NG
UM += -UM % 4
PARTS = 3
UT = UM + 8
ER = T
EC = E // ER
BIG = 1.0e6


def wait_alone(eng, c, sem, value):
    eng.wait_ge(sem, value)
    eng.sem_inc(c["ticks"], 1)


class Order:

    def __init__(self, eng, sem):
        self.eng, self.sem, self.n, self.base = eng, sem, 0, 0

    def link(self, ins):
        ins.then_inc(self.sem, 1)
        self.n += 1
        self.eng.wait_ge(self.sem, self.base + self.n)


class Semaphores:

    def __init__(self, nc):
        self.nc, self.taken, self.c, self.stages = nc, [], {}, 0

    def take(self, name):
        self.taken.append(self.nc.alloc_semaphore(name))
        return self.taken[-1]

    def begin(self, c):
        self.c = c
        self.stages += 1
        c["ticks"] = self.take(f"ticks_{self.stages}")

    def end(self):
        self.nc.clear_and_free_semaphores(self.taken)
        self.nc.all_engine_barrier()
        self.taken = []
        self.begin(self.c)


def dram_scratch(nc):
    return {
        "edges": nc.dram_tensor("edge_list", [E + EB, 4], I32).ap(),
        "adj": nc.dram_tensor("adjacency", [NG, 128, NS * G], F32).ap(),
        "dinv": nc.dram_tensor("dinv_row", [N], F32).ap(),
        "h_l": nc.dram_tensor("gat_target_rows", [PARTS, N, D], BF16).ap(),
        "h_r": nc.dram_tensor("gat_source_rows", [N, D], F32).ap(),
        "gat": nc.dram_tensor("gat_out", [N, D], F32).ap(),
        "p_dst": nc.dram_tensor("gate_target_rows", [PARTS, N, 2 * D], BF16).ap(),
        "p_src": nc.dram_tensor("gate_source_rows", [N, 2 * D], F32).ap(),
    }


def constants(nc, c):
    s_c = c["sems"].take("constants_step")
    with nc.Block() as block:
        @block.gpsimd
        def _(pool):
            o = Order(pool, s_c)
            nc.gpsimd.iota(c["ramp_i"][:, :], [[1, 640]], base=0, channel_multiplier=0)
            nc.gpsimd.iota(c["lane_i"][:, :], [[0, 1]], base=0, channel_multiplier=1)
            nc.gpsimd.memset(c["ones"][:, :], 1.0)
            nc.gpsimd.memset(c["ident"][:, :], 0.0)
            o.link(nc.gpsimd.memset(c["mean_w"][:, :], 1.0 / D))
            o.link(nc.gpsimd.tensor_copy(c["ramp"][:, :], c["ramp_i"][:, :]))
            o.link(nc.gpsimd.tensor_copy(c["lane"][:, :], c["lane_i"][:, :]))
            o.link(nc.gpsimd.affine_select(out=c["ident"][:, :], in_=c["ident"][:, :], compare_op=ALU.not_equal,
                                           fill=1.0, base=0, pattern=[[-1, 128]], channel_multiplier=1))


def prepare(nc, c, d, x_src, x_dst, x_w):
    s_ld = c["sems"].take("edge_inputs_loaded")
    s_st = c["sems"].take("edge_list_stored")
    s_v = c["sems"].take("prepare_vector_step")
    s_p = c["sems"].take("prepare_pool_step")
    s_il = c["sems"].take("edge_list_interleaved")
    s_row = c["sems"].take("search_rows_gathered")
    s_ask = c["sems"].take("search_rows_known")
    s_in = c["sems"].take("prepare_matmul_operand")
    s_mm = c["sems"].take("prepare_matmul_done")
    s_tab = c["sems"].take("block_tables_ready")
    s_blk = [c["sems"].take(f"edge_blocks_loaded_{k}") for k in range(2)]

    def sb(name, shape, dt=F32):
        return ctx.enter_context(nc.sbuf_tensor(name, shape, dt))

    from contextlib import ExitStack
    with ExitStack() as ctx:
        ei = sb("edge_in", [ER, 3, EC], I32)
        el = sb("edge_rows", [ER, EC, 4], I32)
        pad = sb("edge_pad", [128, Q, 4], I32)
        thr = sb("group_threshold", [128, NG + 1])
        first = sb("row_first", [ER, 1])
        below = sb("rows_below", [ER, NG + 1])
        rowf = sb("search_row_f", [NG + 1, 1])
        rowi = sb("search_row_i", [NG + 1, 1], I32)
        found = sb("search_rows", [NG + 1, EC], I32)
        foundf = sb("search_rows_f", [NG + 1, EC])
        thrp = sb("own_threshold", [NG + 1, 1])
        cnt = sb("below_in_row", [NG + 1, 1])
        start = sb("group_start", [NG + 1, 1])
        up = sb("next_minus_own", [NG + 1, NG])
        down = sb("own_minus_previous", [NG, NG])
        before = sb("earlier_groups", [NG, NG])
        ramp512 = sb("block_sizes", [NG, UM])
        size = sb("group_size", [NG, 1])
        nblk = sb("group_blocks", [NG, 1])
        hits = sb("threshold_hits", [128, EC])
        base = sb("group_first_block", [NG, 1])
        v = sb("block_edge_offset", [NG, 1])
        dv = sb("block_edge_step", [NG, 1])
        begun = sb("group_begun", [NG, UT])
        begun_v = sb("group_begun_edges", [NG, UT])
        gof = sb("block_group", [128, UT])
        e0f = sb("block_first_edge_f", [128, UT])
        e0r = sb("block_ramp_edges", [128, UT])
        e0i = c["first_i"]
        prs = sb("pairs_f", [1, 2])
        ps = ctx.enter_context(nc.psum_tensor("prep_psum", [128, 2, 512], F32))
        meta = sb("edge_blocks", [128, UT * Q, 4], I32)
        tmp = sb("edge_tmp", [128, UT * Q])
        tmpi = sb("edge_tmp_i", [128, UT * Q], I32)
        sq = sb("edge_src_tile", [128, UT * Q])

        block = ctx.enter_context(nc.Block())

        def load_blocks(eng, k):
            eng.wait_ge(s_tab, 1)
            eng.wait_ge(s_st, 32)
            pairs = eng.value_load(c["pairs_i"][0:1, 0:1], min_val=1, max_val=UM // 2)
            with eng.Fori(0, pairs) as i:
                e0 = eng.value_load(e0i[0:1, bass.ds(2 * i + k, 1)], min_val=0, max_val=E)
                eng.dma_start(meta[:, bass.ds((2 * i + k) * Q, Q), :],
                              d["edges"][bass.ds(e0, EB), :].rearrange("(p q) w -> p q w", q=Q)).then_inc(s_blk[k], 16)
            wait_alone(eng, c, s_blk[k], pairs * 16)

        @block.sync
        def _(sp):
            sp.dma_start(ei[:, 0, :], x_src.rearrange("(p c) -> p c", p=ER)).then_inc(s_ld, 16)
            sp.dma_start(ei[:, 1, :], x_dst.rearrange("(p c) -> p c", p=ER)).then_inc(s_ld, 16)
            sp.dma_start(ei[:, 2, :], x_w.bitcast(I32).rearrange("(p c) -> p c", p=ER)).then_inc(s_ld, 16)
            sp.wait_ge(s_il, 1)
            sp.dma_start(d["edges"][0:E, :].rearrange("(p c) w -> p (c w)", p=ER), el[:, :, :].rearrange("p c w -> p (c w)")).then_inc(s_st, 16)
            sp.dma_start(d["edges"][E:E + EB, :].rearrange("(p c) w -> p (c w)", p=128), pad[:, :, :].rearrange("p c w -> p (c w)")).then_inc(s_st, 16)
            load_blocks(sp, 0)

        @block.scalar
        def _(act):
            load_blocks(act, 1)

        @block.gpsimd
        def _(pool):
            o = Order(pool, s_p)
            nc.gpsimd.memset(meta[:, :, :], 0)
            nc.gpsimd.memset(up[:, :], 0.0)
            nc.gpsimd.memset(down[:, :], 0.0)
            nc.gpsimd.memset(before[:, :], 1.0)
            nc.gpsimd.memset(pad[:, :, :], 0)
            nc.gpsimd.iota(tmpi[:, 0:NG + 1], [[G, NG + 1]], base=0, channel_multiplier=0)
            nc.gpsimd.iota(tmpi[0:NG, 256:256 + UM], [[EB, UM]], base=EB, channel_multiplier=0)
            o.link(nc.gpsimd.iota(tmpi[:, 512:512 + UT], [[EB, UT]], base=0, channel_multiplier=0))
            nc.gpsimd.tensor_copy(thr[:, :], tmpi[:, 0:NG + 1])
            nc.gpsimd.tensor_copy(ramp512[:, :], tmpi[0:NG, 256:256 + UM])
            nc.gpsimd.tensor_copy(e0r[:, :], tmpi[:, 512:512 + UT])
            nc.gpsimd.memset(pad[:, :, 1:2], N + G)
            o.link(nc.gpsimd.tensor_scalar(thrp[:, :], c["lane"][0:NG + 1, :], float(G), 0.0, ALU.mult, ALU.add))
            o.link(nc.gpsimd.affine_select(out=up[:, :], in_=up[:, :], compare_op=ALU.not_equal, fill=1.0,
                                           base=-1, pattern=[[-1, NG]], channel_multiplier=1))
            o.link(nc.gpsimd.affine_select(out=up[:, :], in_=up[:, :], compare_op=ALU.not_equal, fill=-1.0,
                                           base=0, pattern=[[-1, NG]], channel_multiplier=1))
            o.link(nc.gpsimd.affine_select(out=down[:, :], in_=down[:, :], compare_op=ALU.not_equal, fill=1.0,
                                           base=0, pattern=[[-1, NG]], channel_multiplier=1))
            o.link(nc.gpsimd.affine_select(out=down[:, :], in_=down[:, :], compare_op=ALU.not_equal, fill=-1.0,
                                           base=1, pattern=[[-1, NG]], channel_multiplier=1))
            o.link(nc.gpsimd.affine_select(out=before[:, :], in_=before[:, :], compare_op=ALU.is_gt, fill=0.0,
                                           base=0, pattern=[[1, NG]], channel_multiplier=-1))
            pool.wait_ge(s_ask, 1)
            pool.indirect_dma_start(found[:, :], None, x_dst.rearrange("(p c) -> p c", p=ER),
                                    bass.IndirectOffsetOnAxis(ap=rowi[:, 0:1], axis=0)).then_inc(s_row, 16)
            pool.wait_ge(s_row, 16)

        @block.tensor
        def _(pe):
            steps = [(ps[0:NG + 1, 0, 0:1], below[:, :], c["ones"][0:ER, 0:1]),
                     (ps[0:NG, 1, 0:1], up[:, :], start[:, :]),
                     (ps[0:NG, 0, 0:1], before[:, :], nblk[:, :]),
                     (ps[0:1, 1, 0:1], nblk[:, :], c["ones"][0:NG, 0:1]),
                     (ps[0:NG, 0, 0:1], down[:, :], v[:, :]),
                     (ps[:, 1, 0:UT], c["ones"][0:NG, :], begun[:, :]),
                     (ps[:, 0, 0:UT], c["ones"][0:NG, :], begun_v[:, :])]
            pe.wait_ge(s_p, 7)
            for n, (out, lhs, rhs) in enumerate(steps):
                pe.wait_ge(s_in, n + 1)
                nc.tensor.matmul(out, lhs, rhs, start=True, stop=True).then_inc(s_mm, 1)

        @block.vector
        def _(dve):
            o = Order(dve, s_v)
            vec = nc.vector
            dve.wait_ge(s_ld, 48)
            dve.wait_ge(s_p, 2)
            for w in range(3):
                vec.tensor_copy(el[:, :, w], ei[:, w, :])
            vec.memset(el[:, :, 3:4], 0).then_inc(s_il, 1)
            vec.memset(hits[:, :], 0.0)
            o.link(vec.tensor_copy(first[:, :], ei[:, 1, 0:1]))
            vec.tensor_scalar(below[:, :], thr[0:ER, :], first[:, 0:1], None, ALU.is_gt).then_inc(s_in, 1)
            dve.wait_ge(s_mm, 1)
            o.link(vec.tensor_scalar(rowf[:, :], ps[0:NG + 1, 0, 0:1], -1.0, 0.0, ALU.add, ALU.max))
            vec.tensor_copy(rowi[:, :], rowf[:, :]).then_inc(s_ask, 1)
            dve.wait_ge(s_row, 16)
            o.link(vec.tensor_copy(foundf[:, :], found[:, :]))
            o.link(vec.tensor_scalar(hits[0:NG + 1, :], foundf[:, :], thrp[:, 0:1], 0.0, ALU.is_lt, ALU.add, accum_out=cnt[:, :]))
            vec.scalar_tensor_tensor(start[:, :], rowf[:, :], float(EC), cnt[:, :], ALU.mult, ALU.add).then_inc(s_in, 1)
            dve.wait_ge(s_mm, 2)
            o.link(vec.tensor_copy(size[:, :], ps[0:NG, 1, 0:1]))
            o.link(vec.tensor_scalar(hits[0:NG, 0:UM], ramp512[:, :], size[:, 0:1], 1.0, ALU.is_lt, ALU.add, accum_out=nblk[:, :]))
            vec.tensor_copy(size[:, :], nblk[:, :]).then_inc(s_in, 1)
            dve.wait_ge(s_mm, 3)
            vec.tensor_copy(base[:, :], ps[0:NG, 0, 0:1]).then_inc(s_in, 1)
            dve.wait_ge(s_in, 4)
            dve.wait_ge(s_mm, 4)
            o.link(vec.tensor_scalar(prs[:, 0:1], ps[0:1, 1, 0:1], 0.5, None, ALU.mult))
            o.link(vec.tensor_scalar(hits[0:1, 0:UM], c["ramp"][0:1, 0:UM], prs[:, 0:1], 0.0, ALU.is_lt, ALU.add, accum_out=prs[:, 1:2]))
            o.link(vec.tensor_copy(c["pairs_i"][:, :], prs[:, 1:2]))
            o.link(vec.tensor_scalar(prs[:, 0:1], ps[0:1, 1, 0:1], 0.25, -0.5, ALU.mult, ALU.add))
            o.link(vec.tensor_scalar(hits[0:1, 0:UM], c["ramp"][0:1, 0:UM], prs[:, 0:1], 0.0, ALU.is_lt, ALU.add, accum_out=prs[:, 1:2]))
            o.link(vec.tensor_copy(c["quads_i"][:, :], prs[:, 1:2]))
            vec.scalar_tensor_tensor(v[:, :], base[:, :], -float(EB), start[0:NG, :], ALU.mult, ALU.add).then_inc(s_in, 1)
            dve.wait_ge(s_mm, 5)
            o.link(vec.tensor_copy(dv[:, :], ps[0:NG, 0, 0:1]))
            vec.tensor_scalar(begun[:, :], c["ramp"][0:NG, 0:UT], base[:, 0:1], None, ALU.is_ge).then_inc(s_in, 1)
            dve.wait_ge(s_in, 6)
            vec.tensor_scalar(begun_v[:, :], begun[:, :], dv[:, 0:1], None, ALU.mult).then_inc(s_in, 1)
            dve.wait_ge(s_mm, 6)
            o.link(vec.tensor_scalar(gof[:, :], ps[:, 1, 0:UT], -1.0, None, ALU.add))
            dve.wait_ge(s_mm, 7)
            o.link(vec.tensor_tensor(e0f[:, :], ps[:, 0, 0:UT], e0r[:, :], ALU.add))
            o.link(vec.tensor_scalar(e0f[:, :], e0f[:, :], float(E), None, ALU.min))
            o.link(vec.tensor_copy(c["group_i"][:, :], gof[0:1, :]))
            vec.tensor_copy(e0i[:, :], e0f[0:1, :]).then_inc(s_tab, 1)
            vec.memset(c["goes_on"][:, 0:1], 0.0)
            o.link(vec.tensor_tensor(c["goes_on"][:, 1:UT], gof[:, 1:UT], gof[:, 0:UT - 1], ALU.is_equal))
            o.link(vec.tensor_scalar(gof[:, :], gof[:, :], float(G), None, ALU.mult))
            o.link(vec.scalar_tensor_tensor(c["self_at"][:, :], c["goes_on"][:, :], -BIG, gof[:, :], ALU.mult, ALU.add))
            np_ = dve.value_load(c["pairs_i"][0:1, 0:1], min_val=1, max_val=UM // 2)
            for k in range(2):
                dve.wait_ge(s_blk[k], np_ * 16)
            vec.tensor_copy(c["e_idx"][:, :], meta[:, :, 0])
            vec.tensor_copy(c["e_w"][:, :].bitcast(I32), meta[:, :, 2])
            vec.tensor_copy(tmp[:, :], meta[:, :, 0])
            o.link(vec.tensor_copy(c["e_dst"][:, :], meta[:, :, 1]))
            o.link(vec.tensor_scalar(sq[:, :], tmp[:, :], 1.0 / T, None, ALU.mult))
            o.link(vec.tensor_copy(tmpi[:, :], sq[:, :]))
            o.link(vec.tensor_copy(sq[:, :], tmpi[:, :]))
            r = c["e_row"]
            o.link(vec.scalar_tensor_tensor(r[:, :], sq[:, :], -float(T), tmp[:, :], ALU.mult, ALU.add))
            o.link(vec.tensor_scalar(tmp[:, :], r[:, :], 0.0, None, ALU.is_lt))
            o.link(vec.tensor_tensor(sq[:, :], sq[:, :], tmp[:, :], ALU.subtract))
            o.link(vec.scalar_tensor_tensor(r[:, :], tmp[:, :], float(T), r[:, :], ALU.mult, ALU.add))
            o.link(vec.tensor_scalar(tmp[:, :], r[:, :], float(T), None, ALU.is_ge))
            o.link(vec.tensor_tensor(sq[:, :], sq[:, :], tmp[:, :], ALU.add))
            o.link(vec.scalar_tensor_tensor(r[:, :], tmp[:, :], -float(T), r[:, :], ALU.mult, ALU.add))
            dl = c["e_dst"]
            o.link(vec.tensor_tensor(dl[:, :].rearrange("p (u q) -> p u q", q=Q), dl[:, :].rearrange("p (u q) -> p u q", q=Q),
                                     gof[:, :].unsqueeze(2).to_broadcast([128, UT, Q]), ALU.subtract))
            o.link(vec.tensor_scalar(tmp[:, :], dl[:, :], 0.0, None, ALU.is_ge))
            o.link(vec.scalar_tensor_tensor(tmp[:, :], dl[:, :], float(G), tmp[:, :], ALU.is_lt, ALU.mult))
            qq = c["e_cell"]
            o.link(vec.scalar_tensor_tensor(qq[:, :], sq[:, :], float(G), dl[:, :], ALU.mult, ALU.add))
            o.link(vec.scalar_tensor_tensor(qq[:, :], qq[:, :], 1.0, tmp[:, :], ALU.add, ALU.mult))
            o.link(vec.tensor_scalar(qq[:, :], qq[:, :], -1.0, None, ALU.add))


def build_adjacency(nc, c, d):
    from contextlib import ExitStack
    with ExitStack() as ctx:
        def sb(name, shape, dt=F32):
            return ctx.enter_context(nc.sbuf_tensor(name, shape, dt))
        H1 = 13 * G
        H2 = NS * G - H1
        ohr = sb("source_onehot", [128, 2, Q, 128])
        cell = sb("weighted_cell", [128, 2, Q, NS * G])
        selfd = sb("self_loop_distance", [128, NS * G])
        selfi = sb("self_loop_distance_i", [128, NS * G], I32)
        part = sb("adjacency_part", [128, 2, NS * G])
        cur = sb("adjacency_tile", [128, 2, NS * G])
        acc = [ctx.enter_context(nc.psum_tensor(f"adjacency_sum_{k}", [128, 2, 512], F32)) for k in range(2)]
        s_p = c["sems"].take("build_pool_step")
        s_oh = [c["sems"].take(f"onehots_ready_{k}") for k in range(2)]
        s_mm = [c["sems"].take(f"adjacency_summed_{k}") for k in range(2)]
        s_pf = [c["sems"].take(f"adjacency_sum_read_{k}") for k in range(2)]
        s_cur = [c["sems"].take(f"adjacency_tile_ready_{k}") for k in range(2)]
        s_st = [c["sems"].take(f"adjacency_tile_stored_{k}") for k in range(2)]
        block = ctx.enter_context(nc.Block())

        def pair_count(eng):
            return eng.value_load(c["pairs_i"][0:1, 0:1], min_val=1, max_val=UM // 2)

        @block.gpsimd
        def _(pool):
            o = Order(pool, s_p)
            nc.gpsimd.iota(selfi[:, :], [[T, NS], [-1, G]], base=0, channel_multiplier=1)
            nc.gpsimd.memset(ohr[:, :, :, :], 0.0)
            nc.gpsimd.memset(cur[:, :, :], 0.0)
            o.link(nc.gpsimd.memset(part[:, :, :], 0.0))
            nc.gpsimd.memset(ohr[:, :, :, T:T + 1], 1.0)
            o.link(nc.gpsimd.tensor_copy(selfd[:, :], selfi[:, :]))
            o.link(nc.gpsimd.affine_select(out=selfd[:, :], in_=selfd[:, :], compare_op=ALU.is_gt, fill=-3 * BIG,
                                           base=T, pattern=[[0, NS * G]], channel_multiplier=-1))

        @block.vector
        def _(dve):
            vec = nc.vector

            def onehots(u, k):
                for q in range(Q):
                    col = bass.ds(u * Q + q, 1)
                    vec.tensor_scalar(ohr[:, k, q, 0:T], c["ramp"][:, 0:T], c["e_row"][:, col], None, ALU.is_equal)
                    last = vec.tensor_scalar(cell[:, k, q, :], c["ramp"][:, 0:NS * G], c["e_cell"][:, col],
                                             c["e_w"][:, col], ALU.is_equal, ALU.mult)
                last.then_inc(s_oh[k], 1)

            def finish(i, u, k):
                dve.wait_ge(s_mm[k], i + 1)
                vec.scalar_tensor_tensor(part[:, k, 0:H1], selfd[:, 0:H1], c["self_at"][:, bass.ds(u, 1)],
                                         acc[k][:, 0, 0:H1], ALU.is_equal, ALU.add)
                vec.scalar_tensor_tensor(part[:, k, H1:], selfd[:, H1:], c["self_at"][:, bass.ds(u, 1)],
                                         acc[k][:, 1, 0:H2], ALU.is_equal, ALU.add).then_inc(s_pf[k], 1)
                dve.wait_ge(s_pf[k], i + 2)
                dve.wait_ge(s_st[k], (i + 1) * 16)
                dve.wait_ge(s_cur[1 - k], i + 1 + k)
                vec.scalar_tensor_tensor(cur[:, k, :], cur[:, 1 - k, :], c["goes_on"][:, bass.ds(u, 1)],
                                         part[:, k, :], ALU.mult, ALU.add).then_inc(s_cur[k], 1)

            dve.wait_ge(s_p, 3)
            for k in range(2):
                dve.sem_inc(s_pf[k], 1)
                dve.sem_inc(s_cur[k], 1)
            pairs = pair_count(dve)
            onehots(0, 0)
            with dve.Fori(0, pairs) as i:
                onehots(2 * i + 1, 1)
                finish(i, 2 * i, 0)
                onehots(2 * i + 2, 0)
                finish(i, 2 * i + 1, 1)

        @block.tensor
        def _(pe):
            pe.wait_ge(s_p, 3)
            pairs = pair_count(pe)
            with pe.Fori(0, pairs) as i:
                for k in range(2):
                    pe.wait_ge(s_oh[k], i + 1)
                    pe.wait_ge(s_pf[k], i + 1)
                    for q in range(Q):
                        nc.tensor.matmul(acc[k][:, 0, 0:H1], ohr[:, k, q, :], cell[:, k, q, 0:H1], start=q == 0, stop=q == Q - 1)
                        last = nc.tensor.matmul(acc[k][:, 1, 0:H2], ohr[:, k, q, :], cell[:, k, q, H1:], start=q == 0, stop=q == Q - 1)
                    last.then_inc(s_mm[k], 1)

        @block.sync
        def _(sp):
            pairs = pair_count(sp)
            for k in range(2):
                sp.sem_inc(s_st[k], 16)
            with sp.Fori(0, pairs) as i:
                for k in range(2):
                    g = sp.value_load(c["group_i"][0:1, bass.ds(2 * i + k, 1)], min_val=0, max_val=NG - 1)
                    wait_alone(sp, c, s_cur[k], i + 2)
                    wait_alone(sp, c, s_st[1 - k], (i + 1 + k) * 16)
                    sp.dma_start(d["adj"][bass.ds(g, 1), :, :].rearrange("o p c -> (o p) c"), cur[:, k, :]).then_inc(s_st[k], 16)
            for k in range(2):
                wait_alone(sp, c, s_st[k], (pairs + 1) * 16)


def degrees(nc, c, d):
    from contextlib import ExitStack
    with ExitStack() as ctx:
        def sb(name, shape, dt=F32):
            return ctx.enter_context(nc.sbuf_tensor(name, shape, dt))
        sums = sb("degree_parts", [NG, NS * G])
        deg = sb("degree", [NG, G])
        safe = sb("degree_guarded", [NG, G])
        y = sb("inverse_root", [NG, G])
        z = sb("inverse_root_step", [NG, G])
        s_ld = c["sems"].take("degree_parts_loaded")
        s_v = c["sems"].take("degree_vector_step")
        s_a = c["sems"].take("degree_root_ready")
        s_o = c["sems"].take("dinv_ready")
        s_st = c["sems"].take("dinv_stored")
        s_bk = c["sems"].take("dinv_loaded")
        s_in = c["sems"].take("degree_guarded_ready")
        block = ctx.enter_context(nc.Block())

        @block.sync
        def _(sp):
            sp.dma_start(sums[:, :], d["adj"][:, T, :]).then_inc(s_ld, 16)
            sp.wait_ge(s_o, 1)
            sp.dma_start(d["dinv"].rearrange("(g j) -> g j", j=G), y[:, :]).then_inc(s_st, 16)
            sp.wait_ge(s_st, 16)
            with nc.allow_non_contiguous_dma(reason="3125 values, once"):
                sp.dma_start(c["dinv_n"][:, :], d["dinv"].rearrange("(s r) -> r s", r=T)).then_inc(s_bk, 16)
            sp.dma_start(c["dinv_b"][:, :], d["dinv"].unsqueeze(0).to_broadcast([128, N])).then_inc(s_bk, 16)
            sp.wait_ge(s_bk, 32)

        @block.scalar
        def _(act):
            act.wait_ge(s_in, 1)
            nc.scalar.activation(y[:, :], safe[:, :], ACT.Sqrt).then_inc(s_a, 1)

        @block.vector
        def _(dve):
            o = Order(dve, s_v)
            vec = nc.vector
            dve.wait_ge(s_ld, 16)
            o.link(vec.tensor_reduce(deg[:, :], sums[:, :].rearrange("g (s j) -> g j s", j=G), AX.X, ALU.add))
            o.link(vec.tensor_scalar(deg[:, :], deg[:, :], 1.0, None, ALU.add))
            vec.tensor_scalar(safe[:, :], deg[:, :], 1e-30, None, ALU.max).then_inc(s_in, 1)
            dve.wait_ge(s_a, 1)
            o.link(vec.reciprocal(y[:, :], y[:, :]))
            o.link(vec.tensor_tensor(z[:, :], y[:, :], y[:, :], ALU.mult))
            o.link(vec.tensor_tensor(z[:, :], z[:, :], safe[:, :], ALU.mult))
            o.link(vec.tensor_scalar(z[:, :], z[:, :], -0.5, 1.5, ALU.mult, ALU.add))
            o.link(vec.tensor_tensor(y[:, :], y[:, :], z[:, :], ALU.mult))
            vec.scalar_tensor_tensor(y[:, :], deg[:, :], 0.0, y[:, :], ALU.is_gt, ALU.mult).then_inc(s_o, 1)


def shared_tensors(nc):
    def sb(name, shape, dt=F32):
        return nc.alloc_sbuf_tensor(name, shape, dt)
    return {
        "sems": Semaphores(nc),
        "ramp_i": sb("ramp_i", [128, 640], I32), "ramp": sb("ramp", [128, 640]),
        "lane_i": sb("lane_i", [128, 1], I32), "lane": sb("lane", [128, 1]),
        "ones": sb("ones", [128, 128]), "ident": sb("ident", [128, 128]), "mean_w": sb("mean_w", [128, 128]),
        "pairs_i": sb("block_pairs", [1, 1], I32), "quads_i": sb("block_quads", [1, 1], I32), "group_i": sb("block_group_i", [1, UT], I32),
        "goes_on": sb("block_goes_on", [128, UT]), "self_at": sb("block_self_at", [128, UT]),
        "first_i": sb("block_first_edge", [1, UT], I32),
        "e_idx": sb("edge_src", [128, UT * Q], I32), "e_w": sb("edge_w", [128, UT * Q]),
        "e_row": sb("edge_src_row", [128, UT * Q]), "e_dst": sb("edge_dst_local", [128, UT * Q]),
        "e_cell": sb("edge_cell", [128, UT * Q]),
        "dinv_n": sb("dinv_nodes", [T, NS]), "dinv_b": sb("dinv_all", [128, N]),
        "x_t": sb("x_t", [128, N]), "h_t": sb("h_t", [128, N]),
    }


BLK = 20
NB = NG // BLK
TAIL = NG - NB * BLK
COLS = [(b * BLK * G, BLK * G) for b in range(NB)] + [(NB * BLK * G, TAIL * G)]
EPS = 1e-5
NEG = -float(2 ** 100)
HEADS, HF = 4, 32
SLOPE = 0.2
LOG_EXP = "natural_log_exp_and_others"


def scope(nc, stack):
    def sb(name, shape, dt=F32):
        return stack.enter_context(nc.sbuf_tensor(name, shape, dt))

    def pb(name, shape, dt=F32):
        return stack.enter_context(nc.psum_tensor(name, shape, dt))
    return sb, pb


def load_transposed(nc, c, tag, x, out, bias=None):
    from contextlib import ExitStack
    with ExitStack() as ctx:
        sb, pb = scope(nc, ctx)
        xn = sb(tag + "_nodes", [T, NS, D])
        bt = sb(tag + "_bias", [128, 1])
        pt = pb(tag + "_transposed", [128, 2, 4, 128])
        s_ld, s_t, s_c = (c["sems"].take(f"{tag}_{n}") for n in ("loaded", "tiles_transposed", "tiles_copied"))
        block = ctx.enter_context(nc.Block())

        @block.sync
        def _(sp):
            sp.dma_start(xn[:, :, :], x.rearrange("(s r) f -> r s f", r=T)).then_inc(s_ld, 16)
            if bias is not None:
                with nc.allow_non_contiguous_dma(reason="one value to a partition"):
                    sp.dma_start(bt[:, :], bias.unsqueeze(1)).then_inc(s_ld, 16)

        @block.tensor
        def _(pe):
            pe.wait_ge(s_ld, 16 if bias is None else 32)
            for s in range(NS):
                if s % 4 == 0 and s >= 8:
                    pe.wait_ge(s_c, s // 4 - 1)
                t = nc.tensor.transpose(pt[:, s // 4 % 2, s % 4, 0:T], xn[:, s, :], c["ident"][0:T, 0:T])
                if s % 4 == 3 or s == NS - 1:
                    t.then_inc(s_t, 1)

        @block.vector
        def _(dve):
            for q in range(-(-NS // 4)):
                n = min(4, NS - 4 * q)
                dve.wait_ge(s_t, q + 1)
                o, i = out[:, 4 * q * T:(4 * q + n) * T].rearrange("f (s r) -> f s r", r=T), pt[:, q % 2, 0:n, 0:T]
                if bias is None:
                    nc.vector.tensor_copy(o, i).then_inc(s_c, 1)
                else:
                    nc.vector.tensor_scalar(o, i, bt[:, 0:1], None, ALU.add).then_inc(s_c, 1)


def gcn_layers(nc, c, d, tag, weights, bias, norm):
    from contextlib import ExitStack
    L = len(bias)
    with ExitStack() as ctx:
        sb, pb = scope(nc, ctx)
        w = sb(tag + "_weights", [128, L, D])
        vecs = sb(tag + "_vectors", [128, 3, L])
        h = sb(tag + "_scaled_nodes", [T, NS, D])
        ring = sb(tag + "_adjacency", [128, 2, BLK, NS * G])
        tail = sb(tag + "_adjacency_tail", [128, TAIL, NS * G])
        y = sb(tag + "_aggregate", [128, 2, BLK * G])
        eps = sb(tag + "_eps", [128, 1])
        hp = pb(tag + "_node_psum", [128, 2, 4, D])
        op = pb(tag + "_out_psum", [128, 2, 512])
        if norm:
            yb = sb(tag + "_normed", [128, BLK * G])
            wm = sb(tag + "_weight_means", [128, 2, L])
            sq = sb(tag + "_squares", [128, BLK * G])
            mp = pb(tag + "_moments", [128, 2, 512])
        names = ("weights_loaded", "tail_loaded", "nodes_multiplied", "nodes_scaled", "block_summed",
                 "block_read", "centring_step", "bias_mean_ready", "weights_centred", "squares_ready", "variance_ready",
                 "deviation_ready", "block_normed", "vec_step", "block_out", "start_copied")
        (s_w, s_tl, s_hm, s_hs, s_bs, s_br, s_cs, s_bm, s_wc, s_sq, s_vr, s_dv, s_nm, s_v, s_out, s_x0) = (
            c["sems"].take(f"{tag}_{n}") for n in names)
        s_a = [c["sems"].take(f"{tag}_adjacency_loaded_{k}") for k in range(2)]
        NBL = NB + 1
        NHG = -(-NS // 4)
        block = ctx.enter_context(nc.Block())
        HALF = NB // 2
        vec_rows = [bias] + (list(norm) if norm else [])

        @block.sync
        def _(sp):
            for l in range(L):
                sp.dma_start(w[:, l, :], weights[l]).then_inc(s_w, 16)
            with nc.allow_non_contiguous_dma(reason="one value to a partition"):
                for r, rows in enumerate(vec_rows):
                    for l in range(L):
                        sp.dma_start(vecs[:, r, l:l + 1], rows[l].unsqueeze(1)).then_inc(s_w, 16)
            sp.dma_start(tail[:, :, :], d["adj"][NB * BLK:, :, :].rearrange("g p c -> p g c")).then_inc(s_tl, 16)

            def load(b):
                sp.dma_start(ring[:, b % 2, :, :], d["adj"][b * BLK:(b + 1) * BLK, :, :].rearrange("g p c -> p g c")
                             ).then_inc(s_a[b % 2], 16)

            load(0)
            load(1)
            with sp.Fori(0, L - 1) as l:
                for b in range(2, NB + 2):
                    wait_alone(sp, c, s_bs, l * NBL + b - 1)
                    load(b % NB)
            for b in range(2, NB):
                sp.wait_ge(s_bs, (L - 1) * NBL + b - 1)
                load(b)

        LOADS = 16 * L * (1 + len(vec_rows))

        @block.tensor
        def _(pe):
            pe.wait_ge(s_w, LOADS)
            pe.wait_ge(s_tl, 16)

            if norm:
                nc.tensor.matmul(mp[:, 0, 0:L], c["mean_w"][:, :], vecs[:, 0, :], start=True, stop=True).then_inc(s_bm, 1)
                pe.wait_ge(s_wc, 1)

            def variance(l, b):
                n = COLS[b][1]
                pe.wait_ge(s_sq, l * NBL + b + 1)
                nc.tensor.matmul(mp[:, 1, 0:n], c["mean_w"][:, :], sq[:, 0:n], start=True, stop=True).then_inc(s_vr, 1)

            with pe.Fori(0, L) as l:
                pe.wait_ge(s_x0, 1)
                pe.wait_ge(s_out, l * NBL + 1)
                for s in range(NS):
                    q = s // 4
                    if s % 4 == 0:
                        pe.wait_ge(s_hs, l * NHG + max(q, 1))
                    m = nc.tensor.matmul(hp[0:T, q % 2, s % 4, :], c["h_t"][:, s * T:(s + 1) * T], w[:, bass.ds(l, 1), :].rearrange("p o f -> p (o f)"),
                                         start=True, stop=True)
                    if s % 4 == 3 or s == NS - 1:
                        m.then_inc(s_hm, 1)
                pe.wait_ge(s_hs, (l + 1) * NHG + 1)
                for b, (_, n) in enumerate(COLS):
                    if b < NB:
                        pe.wait_ge(s_a[b % 2], (l * HALF + b // 2 + 1) * 16)
                    pe.wait_ge(s_br, l * NBL + max(b, 1))
                    a = ring[:, b % 2, :, :] if b < NB else tail[:, :, :]
                    for s in range(NS):
                        m = nc.tensor.matmul(op[:, b % 2, 0:n], h[:, s, :], a[0:T, :, s * G:(s + 1) * G],
                                             start=s == 0, stop=s == NS - 1)
                        if norm and b >= 1 and s == 4:
                            variance(l, b - 1)
                    m.then_inc(s_bs, 1)
                if norm:
                    variance(l, NB)

        @block.scalar
        def _(act):
            act.wait_ge(s_w, LOADS)
            act.wait_ge(s_x0, 2)
            act.sem_inc(s_out, 1)
            with act.Fori(0, L) as l:
                for b, (c0, n) in enumerate(COLS):
                    done = l * NBL + b + 1
                    wait_alone(act, c, s_br, done + 1)
                    row = [vecs[:, r, bass.ds(l, 1)] for r in range(3)]
                    yk = y[:, b % 2, 0:n]
                    if not norm:
                        nc.scalar.activation(c["h_t"][:, c0:c0 + n], yk, ACT.Relu, bias=row[0]).then_inc(s_out, 1)
                        continue
                    nc.scalar.activation(sq[:, 0:n], yk, ACT.Square, bias=row[0]).then_inc(s_sq, 1)
                    nc.scalar.preload_act_table_set(LOG_EXP)
                    wait_alone(act, c, s_vr, done)
                    nc.scalar.activation(sq[:, 0:n], mp[:, 1, 0:n], ACT.Ln, bias=eps[:, 0:1]).then_inc(s_v, 1)
                    wait_alone(act, c, s_v, done)
                    nc.scalar.activation(sq[:, 0:n], sq[:, 0:n], ACT.Exp, scale=-0.5).then_inc(s_dv, 1)
                    wait_alone(act, c, s_nm, done)
                    nc.scalar.activation(c["h_t"][:, c0:c0 + n], yb[:, 0:n], ACT.Gelu, bias=row[2], scale=row[1]
                                         ).then_inc(s_out, 1)

        @block.vector
        def _(dve):
            o = Order(dve, s_v)
            vec = nc.vector
            vec.tensor_copy(c["h_t"][:, :], c["x_t"][:, :]).then_inc(s_x0, 1)
            vec.memset(eps[:, :], EPS).then_inc(s_x0, 1)
            if norm:
                dve.wait_ge(s_w, LOADS)
                vec.tensor_reduce(wm[:, 0, :], w[:, :, :], AX.X, ALU.add).then_inc(s_cs, 1)
                dve.wait_ge(s_cs, 1)
                vec.tensor_scalar(wm[:, 1, :], wm[:, 0, :], 1.0 / D, None, ALU.mult).then_inc(s_cs, 1)
                dve.wait_ge(s_cs, 2)
                vec.tensor_tensor(w[:, :, :], w[:, :, :], wm[:, 1, :].unsqueeze(2).to_broadcast([128, L, D]), ALU.subtract).then_inc(s_cs, 1)
                dve.wait_ge(s_bm, 1)
                dve.wait_ge(s_cs, 3)
                vec.tensor_tensor(vecs[:, 0, :], vecs[:, 0, :], mp[:, 0, 0:L], ALU.subtract).then_inc(s_wc, 1)
                dve.wait_ge(s_wc, 1)
            dve.sem_inc(s_hs, 1)
            dve.sem_inc(s_br, 1)
            with dve.Fori(0, L) as l:
                for q in range(NHG):
                    n = min(4, NS - 4 * q)
                    dve.wait_ge(s_hm, l * NHG + q + 1)
                    vec.tensor_tensor(h[:, 4 * q:4 * q + n, :], hp[0:T, q % 2, 0:n, :],
                                      c["dinv_n"][:, 4 * q:4 * q + n].unsqueeze(2).to_broadcast([T, n, D]), ALU.mult).then_inc(s_hs, 1)
                for b, (c0, n) in enumerate(COLS):
                    done = l * NBL + b + 1
                    dve.wait_ge(s_bs, done)
                    if b >= 2:
                        dve.wait_ge(s_out, done - 1)
                    yk = y[:, b % 2, 0:n]
                    vec.tensor_tensor(yk, op[:, b % 2, 0:n], c["dinv_b"][:, c0:c0 + n], ALU.mult).then_inc(s_br, 1)
                    if norm:
                        dve.wait_ge(s_out, done)
                        dve.wait_ge(s_dv, done)
                        vec.scalar_tensor_tensor(yb[:, 0:n], yk, vecs[:, 0, bass.ds(l, 1)], sq[:, 0:n], ALU.add, ALU.mult).then_inc(s_nm, 1)


def add_and_norm(nc, c, tag, parts):
    from contextlib import ExitStack
    with ExitStack() as ctx:
        sb, pb = scope(nc, ctx)
        t = sb(tag + "_sum", [128, N])
        sq = sb(tag + "_squares", [128, 2, BLK * G])
        eps = sb(tag + "_eps", [128, 1])
        mp = pb(tag + "_moments", [128, 2, 2, 512])
        s_v, s_v2, s_sum, s_mn, s_ct, s_sq, s_vr, s_dv, s_out, s_e = (c["sems"].take(f"{tag}_{n}") for n in (
            "vec_step", "act_step", "sum_ready", "mean_ready", "centred", "squares_ready", "variance_ready", "deviation_ready", "out", "eps_ready"))
        block = ctx.enter_context(nc.Block())

        def variance(pe, b):
            n = COLS[b][1]
            pe.wait_ge(s_sq, b + 1)
            if b >= 2:
                pe.wait_ge(s_dv, b - 1)
            nc.tensor.matmul(mp[:, 1, b % 2, 0:n], c["mean_w"][:, :], sq[:, b % 2, 0:n], start=True, stop=True).then_inc(s_vr, 1)

        def deviation(act, o, b):
            n = COLS[b][1]
            act.wait_ge(s_vr, b + 1)
            o.link(nc.scalar.activation(sq[:, b % 2, 0:n], mp[:, 1, b % 2, 0:n], ACT.Ln, bias=eps[:, 0:1]))
            nc.scalar.activation(sq[:, b % 2, 0:n], sq[:, b % 2, 0:n], ACT.Exp, scale=-0.5).then_inc(s_dv, 1)

        def scale(dve, o, b):
            c0, n = COLS[b]
            dve.wait_ge(s_dv, b + 1)
            nc.vector.tensor_tensor(c["x_t"][:, c0:c0 + n], t[:, c0:c0 + n], sq[:, b % 2, 0:n], ALU.mult).then_inc(s_out, 1)


        @block.tensor
        def _(pe):
            for b, (c0, n) in enumerate(COLS):
                pe.wait_ge(s_sum, b + 1)
                if b >= 2:
                    pe.wait_ge(s_ct, b - 1)
                nc.tensor.matmul(mp[:, 0, b % 2, 0:n], c["mean_w"][:, :], t[:, c0:c0 + n], start=True, stop=True).then_inc(s_mn, 1)
                if b >= 1:
                    variance(pe, b - 1)
            variance(pe, NB)

        @block.scalar
        def _(act):
            nc.scalar.preload_act_table_set(LOG_EXP)
            o = Order(act, s_v2)
            act.wait_ge(s_e, 1)
            for b, (c0, n) in enumerate(COLS):
                act.wait_ge(s_ct, b + 1)
                if b >= 2:
                    act.wait_ge(s_out, b - 1)
                nc.scalar.activation(sq[:, b % 2, 0:n], t[:, c0:c0 + n], ACT.Square).then_inc(s_sq, 1)
                if b >= 1:
                    deviation(act, o, b - 1)
            deviation(act, o, NB)

        @block.vector
        def _(dve):
            vec = nc.vector
            o = Order(dve, s_v)
            vec.memset(eps[:, :], EPS).then_inc(s_e, 1)
            for b, (c0, n) in enumerate(COLS):
                cols = slice(c0, c0 + n)
                if len(parts) == 3:
                    o.link(vec.tensor_tensor(t[:, cols], parts[0][:, cols], parts[1][:, cols], ALU.add))
                    vec.tensor_tensor(t[:, cols], t[:, cols], parts[2][:, cols], ALU.add).then_inc(s_sum, 1)
                else:
                    vec.tensor_tensor(t[:, cols], parts[0][:, cols], parts[1][:, cols], ALU.add).then_inc(s_sum, 1)
            for b, (c0, n) in enumerate(COLS):
                cols = slice(c0, c0 + n)
                dve.wait_ge(s_mn, b + 1)
                vec.tensor_tensor(t[:, cols], t[:, cols], mp[:, 0, b % 2, 0:n], ALU.subtract).then_inc(s_ct, 1)
                if b >= 1:
                    scale(dve, o, b - 1)
            scale(dve, o, NB)



def node_tables(nc, c, tag, tables):
    from contextlib import ExitStack
    with ExitStack() as ctx:
        sb, pb = scope(nc, ctx)
        width = sum(b - a for _, (a, b), _ in tables[0][0])
        nt = len(tables)
        w = sb(tag + "_w", [128, nt, width])
        bias = sb(tag + "_bias", [T, nt, width])
        out = sb(tag + "_rows", [T, nt, NS, width])
        split = sb(tag + "_parts", [T, PARTS, NS, width], BF16)
        ready = sb(tag + "_ready", [1, 1])
        CH = 5
        chunks = [slice(t, t + CH) for t in range(0, NS, CH)]
        per = 512 // width
        runs = [(t, s, min(per, NS - s)) for t in range(nt) for s in range(0, NS, per)]
        ps = pb(tag + "_psum", [T, 2, per, width])
        s_w, s_v, s_n, s_b, s_mm, s_o, s_st, s_pt, s_rest = (c["sems"].take(f"{tag}_{n}") for n in (
            "loaded", "vec_step", "weights_ready", "bias_cleared", "tile_multiplied", "rows_ready", "rows_stored", "part_ready", "rest_ready"))
        NRUN = -(-NS // per)
        loads = sum(len(ws) + len(bs) for ws, bs, _ in tables)
        block = ctx.enter_context(nc.Block())

        @block.sync
        def _(sp):
            sp.wait_ge(s_b, 1)
            for t, (ws, bs, _) in enumerate(tables):
                for ap, (a, b), _ in ws:
                    sp.dma_start(w[:, t, a:b], ap).then_inc(s_w, 16)
                for ap, (a, b), _ in bs:
                    sp.dma_start(bias[:, t, a:b], ap.unsqueeze(0).to_broadcast([T, b - a])).then_inc(s_w, 16)
            for p in range(PARTS):
                sp.wait_ge(s_pt, len(chunks) * (p + 1))
                sp.dma_start(tables[0][2][p].rearrange("(s r) f -> r s f", r=T), split[:, p, :, :]).then_inc(s_st, 16)
            for t in range(1, nt):
                sp.wait_ge(s_o, NRUN * (t + 1))
                sp.dma_start(tables[t][2].rearrange("(s r) f -> r s f", r=T), out[:, t, :, :]).then_inc(s_st, 16)
            sp.wait_ge(s_st, 16 * (PARTS + nt - 1))

        @block.scalar
        def _(act):
            for p in range(PARTS):
                for k, ch in enumerate(chunks):
                    if p == 0:
                        act.wait_ge(s_o, min(NRUN, -(-ch.stop // per)))
                    else:
                        act.wait_ge(s_rest, (p - 1) * len(chunks) + k + 1)
                    nc.scalar.copy(split[:, p, ch, :], out[:, 0, ch, :]).then_inc(s_pt, 1)

        @block.vector
        def _(dve):
            o = Order(dve, s_v)
            nc.vector.memset(bias[:, :, :], 0.0).then_inc(s_b, 1)
            dve.wait_ge(s_w, 16 * loads)
            for t, (ws, bs, _) in enumerate(tables):
                for _, (a, b), negate in ws:
                    if negate:
                        o.link(nc.vector.tensor_scalar(w[:, t, a:b], w[:, t, a:b], -1.0, None, ALU.mult))
                for _, (a, b), negate in bs:
                    if negate:
                        o.link(nc.vector.tensor_scalar(bias[:, t, a:b], bias[:, t, a:b], -1.0, None, ALU.mult))
            nc.vector.memset(ready[:, :], 0.0).then_inc(s_n, 1)
            for m, (t, s, n) in enumerate(runs):
                dve.wait_ge(s_mm, m + 1)
                nc.vector.tensor_tensor(out[:, t, s:s + n, :], ps[:, m % 2, 0:n, :],
                                        bias[:, t, :].unsqueeze(1).to_broadcast([T, n, width]), ALU.add).then_inc(s_o, 1)
                if m == NRUN - 1:
                    for p in range(PARTS - 1):
                        for k, ch in enumerate(chunks):
                            dve.wait_ge(s_pt, p * len(chunks) + k + 1)
                            nc.vector.tensor_tensor(out[:, 0, ch, :], out[:, 0, ch, :], split[:, p, ch, :], ALU.subtract).then_inc(s_rest, 1)

        @block.tensor
        def _(pe):
            pe.wait_ge(s_n, 1)
            for m, (t, s0, n) in enumerate(runs):
                if m >= 2:
                    pe.wait_ge(s_o, m - 1)
                for s in range(n):
                    i = nc.tensor.matmul(ps[:, m % 2, s, :], c["x_t"][:, (s0 + s) * T:(s0 + s + 1) * T], w[:, t, :], start=True, stop=True)
                i.then_inc(s_mm, 1)


LAG = 4


def done(i, b):
    return i * 4 + b + 1


def turns(i, b):
    return i + b // 4 + 1


def run_steps(eng, c, step):
    quads = eng.value_load(c["quads_i"][0:1, 0:1], min_val=1, max_val=UM // 4)
    for b in range(-1, LAG):
        step(0, b)
    with eng.Fori(0, quads) as i:
        for b in range(LAG, LAG + 4):
            step(i, b)
    return quads


def gather_blocks(pool, nc, c, table, idx, rows, s_idx, s_got, s_used):
    def gather(i, b):
        k = (b + 1) % 4
        if b + 1 >= 4:
            wait_alone(pool, c, s_used, done(i, b + 1 - 4))
        nc.gpsimd.tensor_copy(idx[:, k, :], c["e_idx"][:, bass.ds((i * 4 + b + 1) * Q, Q)]).then_inc(s_idx, 1)
        wait_alone(pool, c, s_idx, done(i, b + 1))
        for q in range(Q):
            pool.indirect_dma_start(rows[:, k, q, :], None, table, bass.IndirectOffsetOnAxis(ap=idx[:, k, q:q + 1], axis=0)
                                    ).then_inc(s_got[k], 16)
    quads = run_steps(pool, c, gather)
    wait_alone(pool, c, s_got[0], (quads + 2) * 16 * Q)


def attention(nc, c, d, att):
    from contextlib import ExitStack
    with ExitStack() as ctx:
        sb, pb = scope(nc, ctx)
        NH = HEADS * G
        QH = Q * HEADS
        HW = HF + 1
        att_b = sb("att_row", [128, D])
        neg = sb("att_mask_value", [128, 1])
        head_of = sb("head_of", [NH, HEADS])
        node_of = sb("node_of", [NH, G])
        ident_b = sb("ident_bf16", [128, 128], BF16)
        begins = sb("block_begins", [128, UT])
        idx = sb("gather_rows", [128, 4, Q], I32)
        xj = sb("source_rows", [128, 4, Q, D])
        hl = sb("group_rows", [PARTS * G, 4, D], BF16)
        oh = sb("node_onehot", [128, 4, Q, G])
        pen = sb("pair_mask", [128, 4, Q, NH], BF16)
        oht = sb("node_onehot_t", [NH, 4, Q * 128])
        ohtb = sb("node_onehot_t_bf16", [PARTS * G, 2, Q * 128], BF16)
        z = sb("score_sums", [128, Q, D])
        zl = sb("score_terms", [128, Q, D])
        za = sb("weighted_terms", [128, Q, D])
        sc = sb("scores", [128, 4, QH])
        scx = sb("scores_by_pair", [128, Q, NH])
        mx = sb("block_max", [NH, 1])
        mxh = sb("block_max_by_head", [NH, HEADS])
        dg = sb("score_less_max", [128, QH])
        df = sb("score_less_max_guarded", [128, 2, QH])
        msg = sb("messages", [128, 2, Q, HEADS, HW])
        run = sb("running_max", [G, 2, HEADS])
        part = sb("running_sums", [G, 2, HEADS, HW])
        dab = sb("max_changes", [G, 2, 2, HEADS])
        ab = sb("rescale", [G, 2, 2, HEADS])
        t1 = sb("rescaled_run", [G, HEADS, HW])
        t2 = sb("rescaled_block", [G, HEADS, HW])
        den = sb("weight_sum", [G, HEADS])
        inv = sb("weight_sum_inverse", [G, HEADS])
        out = sb("group_out", [G, 2, D])
        p_z = pb("score_psum", [128, 2, 512])
        p_t = pb("onehot_t_psum", [128, 2, 512])
        p_m = pb("masked_scores", [128, 2, 512])
        p_g = pb("max_psum", [128, 512])
        p_a = pb("block_sum_psum", [128, 512])
        names = ("inputs_loaded", "pool_step", "begins_ready", "index_copied", "onehot", "pair_mask", "onehot_t", "onehot_t_copied", "terms_sum", "terms_read",
                 "terms", "weighted_terms", "scores", "scores_by_pair", "masked", "max", "max_split", "max_spread", "less_max_raw", "less_max", "weights",
                 "messages", "block_sum", "run_max", "changes", "rescale", "block_rescaled", "run_updated", "sum_guarded",
                 "sum_inverse", "group_out")
        (s_in, s_p, s_bg, s_ix, s_oh, s_pn, s_T, s_oht, s_z, s_zr, s_zl, s_za, s_sc, s_sx, s_M, s_mx, s_ms, s_G, s_dr, s_d, s_w,
         s_msg, s_A, s_rm, s_ch, s_ex, s_t2, s_run, s_sg, s_si, s_O) = (c["sems"].take("att_" + n) for n in names)
        s_g = [c["sems"].take(f"att_sources_gathered_{k}") for k in range(4)]
        s_hl = [c["sems"].take(f"att_group_rows_loaded_{k}") for k in range(4)]
        s_st = [c["sems"].take(f"att_group_out_stored_{k}") for k in range(2)]
        block = ctx.enter_context(nc.Block())

        @block.gpsimd
        def _(pool):
            o = Order(pool, s_p)
            g = nc.gpsimd
            for t in (run, part, head_of):
                g.memset(t[tuple(slice(None) for _ in t.shape)], 0.0)
            g.memset(neg[:, :], NEG)
            o.link(g.memset(node_of[:, :], 0.0))
            o.link(g.affine_select(out=head_of[:, :], in_=head_of[:, :], compare_op=ALU.is_gt, fill=1.0, base=0,
                                   pattern=[[G, HEADS]], channel_multiplier=-1))
            o.link(g.affine_select(out=head_of[:, :], in_=head_of[:, :], compare_op=ALU.is_gt, fill=0.0, base=G,
                                   pattern=[[G, HEADS]], channel_multiplier=-1))
            for h in range(HEADS):
                o.link(g.affine_select(out=node_of[:, :], in_=node_of[:, :], compare_op=ALU.not_equal, fill=1.0, base=-h * G,
                                       pattern=[[-1, G]], channel_multiplier=1))
            o.link(g.tensor_copy(ident_b[:, :], c["ident"][:, :]))
            gather_blocks(pool, nc, c, d["h_r"], idx, xj, s_ix, s_g, s_msg)

        @block.sync
        def _(sp):
            sp.dma_start(att_b[:, :], att.rearrange("o h f -> o (h f)").to_broadcast([128, D])).then_inc(s_in, 16)

            def load(i, b):
                g = sp.value_load(c["group_i"][0:1, bass.ds(i * 4 + b, 1)], min_val=0, max_val=NG - 1)
                if b >= 4:
                    wait_alone(sp, c, s_z, done(i, b - 4))
                for p in range(PARTS):
                    sp.dma_start(hl[p * G:(p + 1) * G, b % 4, :], d["h_l"][p, bass.ds(g * G, G), :]).then_inc(s_hl[b % 4], 16)

            load(0, 0)

            def move(i, b):
                load(i, b + 2)
                if b >= 2:
                    g = sp.value_load(c["group_i"][0:1, bass.ds(i * 4 + b - 2, 1)], min_val=0, max_val=NG - 1)
                    wait_alone(sp, c, s_O, done(i, b - 2))
                    if b >= 3:
                        wait_alone(sp, c, s_st[(b - 3) % 2], (i * 2 + (b - 3) // 2 + 1) * 16)
                    sp.dma_start(d["gat"][bass.ds(g * G, G), :], out[:, b % 2, :]).then_inc(s_st[b % 2], 16)
            quads = run_steps(sp, c, move)
            wait_alone(sp, c, s_hl[1], (quads + 2) * 16 * PARTS)
            for k in range(2):
                wait_alone(sp, c, s_st[k], (quads * 2 + 1) * 16)

        @block.tensor
        def _(pe):
            pe.wait_ge(s_p, 8)

            def masks(i, b):
                pe.wait_ge(s_pn, done(i, b))
                if b >= 2:
                    pe.wait_ge(s_oht, done(i, b - 2))
                for q in range(Q):
                    m = nc.tensor.matmul(p_t[0:NH, b % 2, q * 128:(q + 1) * 128], pen[:, b % 4, q, :],
                                         ident_b[:, :], start=True, stop=True)
                m.then_inc(s_T, 1)
            masks(0, 0)

            def step(i, b):
                n, k, j = (b + 1) % 4, b % 4, (b - 1) % 4
                if b >= 1:
                    pe.wait_ge(s_ms, done(i, b - 1))
                    for q in range(Q):
                        nc.tensor.matmul(p_g[:, q * HEADS:(q + 1) * HEADS], oht[:, j, q * 128:(q + 1) * 128], mxh[:, :], start=True, stop=True)
                    nc.tensor.matmul(p_g[0:G, QH:QH + HEADS], node_of[:, :], mxh[:, :], start=True, stop=True).then_inc(s_G, 1)
                pe.wait_ge(s_oht, done(i, b + 1))
                pe.wait_ge(s_hl[n], turns(i, b + 1) * 16 * PARTS)
                if b >= 1:
                    pe.wait_ge(s_zr, done(i, b - 1))
                for q in range(Q):
                    m = nc.tensor.matmul(p_z[:, n % 2, q * D:(q + 1) * D], ohtb[0:PARTS * G, n % 2, q * 128:(q + 1) * 128], hl[:, n, :],
                                         start=True, stop=True)
                m.then_inc(s_z, 1)
                if b >= 0:
                    pe.wait_ge(s_sx, done(i, b))
                    if b >= 2:
                        pe.wait_ge(s_mx, done(i, b - 2))
                    for q in range(Q):
                        o = p_m[0:NH, k % 2, q * 128:(q + 1) * 128]
                        nc.tensor.matmul(o, pen[:, k, q, :], ident_b[:, :], start=True, stop=False)
                        m = nc.tensor.matmul(o, scx[:, q, :], c["ident"][:, :], start=False, stop=True)
                    m.then_inc(s_M, 1)
                masks(i, b + 2)
                if b >= 1:
                    pe.wait_ge(s_msg, done(i, b - 1))
                    if b >= 2:
                        pe.wait_ge(s_t2, done(i, b - 2))
                    for q in range(Q):
                        m = nc.tensor.matmul(p_a[0:G, 0:HEADS * HW], oh[:, j, q, :], msg[:, j % 2, q, :, :].rearrange("p h f -> p (h f)"),
                                             start=q == 0, stop=q == Q - 1)
                    m.then_inc(s_A, 1)
            run_steps(pe, c, step)

        @block.scalar
        def _(act):
            def mask(i, b):
                wait_alone(act, c, s_oh, done(i, b))
                nc.scalar.activation(pen[:, b % 4, :, :].rearrange("p q (h n) -> p q h n", h=HEADS), oh[:, b % 4, :, :].unsqueeze(2).to_broadcast([128, Q, HEADS, G]),
                                     ACT.Identity, bias=neg[:, 0:1], scale=-NEG).then_inc(s_pn, 1)

            def transposed(i, b):
                wait_alone(act, c, s_T, done(i, b))
                nc.scalar.activation(ohtb[:, b % 2, :], p_t[0:PARTS * G, b % 2, :], ACT.Identity, bias=1.0, scale=-1.0 / NEG)
                nc.scalar.activation(oht[:, b % 4, :], p_t[0:NH, b % 2, :], ACT.Identity, bias=1.0, scale=-1.0 / NEG).then_inc(s_oht, 1)
            act.wait_ge(s_p, 8)
            mask(0, 0)
            transposed(0, 0)

            def step(i, b):
                n, j = (b + 1) % 4, (b - 1) % 4
                if b >= 0:
                    wait_alone(act, c, s_sc, done(i, b))
                    if b >= 1:
                        wait_alone(act, c, s_M, done(i, b - 1))
                    nc.scalar.activation(scx[:, :, :].rearrange("p q (h n) -> p (q h) n", h=HEADS), sc[:, b % 4, :].unsqueeze(2).to_broadcast([128, QH, G]),
                                         ACT.Copy).then_inc(s_sx, 1)
                if b >= 1:
                    wait_alone(act, c, s_d, done(i, b - 1))
                    nc.scalar.activation(msg[:, j % 2, :, :, HF:HW], df[:, j % 2, :].rearrange("p (q h o) -> p q h o", q=Q, o=1), ACT.Exp).then_inc(s_w, 1)
                    wait_alone(act, c, s_ch, done(i, b - 1))
                    nc.scalar.activation(ab[:, j % 2, :, :], dab[:, j % 2, :, :], ACT.Exp).then_inc(s_ex, 1)
                mask(i, b + 2)
                transposed(i, b + 2)
            run_steps(act, c, step)

        @block.vector
        def _(dve):
            vec = nc.vector
            dve.wait_ge(s_in, 16)
            dve.wait_ge(s_p, 8)
            vec.tensor_scalar(begins[:, :], c["goes_on"][:, :], -NEG, NEG, ALU.mult, ALU.add).then_inc(s_bg, 1)
            dve.wait_ge(s_bg, 1)

            def onehots(i, b):
                vec.tensor_tensor(oh[:, b % 4, :, :], c["ramp"][:, 0:G].unsqueeze(1).to_broadcast([128, Q, G]),
                                  c["e_dst"][:, bass.ds((i * 4 + b) * Q, Q)].unsqueeze(2).to_broadcast([128, Q, G]), ALU.is_equal).then_inc(s_oh, 1)
            onehots(0, 0)

            def step(i, b):
                k, j, e = b % 4, (b - 1) % 4, (b - 2) % 4
                if b >= 0:
                    dve.wait_ge(s_z, done(i, b))
                    dve.wait_ge(s_g[k], turns(i, b) * 16 * Q)
                    vec.tensor_tensor(z[:, :, :].rearrange("p q f -> p (q f)"), p_z[:, k % 2, :], xj[:, k, :, :].rearrange("p q f -> p (q f)"), ALU.add).then_inc(s_zr, 1)
                    dve.wait_ge(s_zr, done(i, b))
                    vec.scalar_tensor_tensor(zl[:, :, :], z[:, :, :], SLOPE, z[:, :, :], ALU.mult, ALU.max).then_inc(s_zl, 1)
                if b >= 1:
                    dve.wait_ge(s_M, done(i, b - 1))
                    vec.tensor_reduce(mx[:, :], p_m[0:NH, j % 2, :], AX.X, ALU.max).then_inc(s_mx, 1)
                    dve.wait_ge(s_mx, done(i, b - 1))
                    vec.tensor_scalar(mxh[:, :], head_of[:, :], mx[:, 0:1], None, ALU.mult).then_inc(s_ms, 1)
                if b >= 0:
                    dve.wait_ge(s_zl, done(i, b))
                    vec.tensor_tensor(za[:, :, :], zl[:, :, :], att_b[:, :].unsqueeze(1).to_broadcast([128, Q, D]), ALU.mult).then_inc(s_za, 1)
                    dve.wait_ge(s_za, done(i, b))
                    vec.tensor_reduce(sc[:, k, :], za[:, :, :].rearrange("p q (h f) -> p (q h) f", h=HEADS), AX.X, ALU.add).then_inc(s_sc, 1)
                if b >= 1:
                    dve.wait_ge(s_G, done(i, b - 1))
                    vec.tensor_tensor(dg[:, :], sc[:, j, :], p_g[:, 0:QH], ALU.subtract).then_inc(s_dr, 1)
                    vec.scalar_tensor_tensor(run[:, j % 2, :], run[:, 1 - j % 2, :], begins[0:G, bass.ds(i * 4 + b - 1, 1)], p_g[0:G, QH:QH + HEADS], ALU.add, ALU.max
                                             ).then_inc(s_rm, 1)
                    dve.wait_ge(s_dr, done(i, b - 1))
                    vec.tensor_scalar(df[:, j % 2, :], dg[:, :], 0.0, None, ALU.min).then_inc(s_d, 1)
                    dve.wait_ge(s_rm, done(i, b - 1))
                    vec.scalar_tensor_tensor(dab[:, j % 2, 0, :], run[:, 1 - j % 2, :], begins[0:G, bass.ds(i * 4 + b - 1, 1)], run[:, j % 2, :], ALU.add, ALU.subtract)
                    vec.tensor_tensor(dab[:, j % 2, 1, :], p_g[0:G, QH:QH + HEADS], run[:, j % 2, :], ALU.subtract).then_inc(s_ch, 1)
                if b >= 2:
                    p = e % 2
                    dve.wait_ge(s_ex, done(i, b - 2))
                    dve.wait_ge(s_A, done(i, b - 2))
                    vec.tensor_tensor(t1[:, :, :], part[:, 1 - p, :, :], ab[:, p, 0, :].unsqueeze(2).to_broadcast([G, HEADS, HW]), ALU.mult)
                    vec.tensor_tensor(t2[:, :, :], p_a[0:G, 0:HEADS * HW].rearrange("n (h f) -> n h f", h=HEADS),
                                      ab[:, p, 1, :].unsqueeze(2).to_broadcast([G, HEADS, HW]), ALU.mult).then_inc(s_t2, 1)
                    dve.wait_ge(s_t2, done(i, b - 2))
                    vec.tensor_tensor(part[:, p, :, :], t1[:, :, :], t2[:, :, :], ALU.add).then_inc(s_run, 1)
                onehots(i, b + 2)
                if b >= 2:
                    p = e % 2
                    dve.wait_ge(s_run, done(i, b - 2))
                    vec.tensor_scalar(den[:, :], part[:, p, :, HF:HW].rearrange("n h o -> n (h o)"), 1e-16, None, ALU.max).then_inc(s_sg, 1)
                    dve.wait_ge(s_sg, done(i, b - 2))
                    vec.reciprocal(inv[:, :], den[:, :]).then_inc(s_si, 1)
                    dve.wait_ge(s_si, done(i, b - 2))
                    if b >= 4:
                        dve.wait_ge(s_st[p], (i * 2 + (b - 4) // 2 + 1) * 16)
                    vec.tensor_tensor(out[:, p, :].rearrange("n (h f) -> n h f", h=HEADS), part[:, p, :, 0:HF],
                                      inv[:, :].unsqueeze(2).to_broadcast([G, HEADS, HF]), ALU.mult).then_inc(s_O, 1)
                if b >= 1:
                    dve.wait_ge(s_w, done(i, b - 1))
                    vec.tensor_tensor(msg[:, j % 2, :, :, 0:HF], xj[:, j, :, :].rearrange("p q (h f) -> p q h f", h=HEADS),
                                      msg[:, j % 2, :, :, HF:HW].to_broadcast([128, Q, HEADS, HF]), ALU.mult).then_inc(s_msg, 1)
            run_steps(dve, c, step)


def gated_conv(nc, c, d, ea, w_f, w_s):
    from contextlib import ExitStack
    with ExitStack() as ctx:
        sb, pb = scope(nc, ctx)
        W = 2 * D
        we = sb("edge_weights", [128, W])
        ident_b = sb("gate_ident_bf16", [128, 128], BF16)
        idx = sb("gate_gather_rows", [128, 4, Q], I32)
        xj = sb("gate_source_rows_sb", [128, 4, Q, W])
        hl = sb("gate_group_rows", [PARTS * G, 4, W], BF16)
        e_n = sb("edge_features", [128, 4, Q, D])
        e_t = sb("edge_features_t", [128, 2, Q * 128])
        oh = sb("gate_node_onehot", [128, 4, Q, G])
        ohb = sb("gate_node_onehot_bf16", [128, 4, Q, PARTS * G], BF16)
        oht = sb("gate_node_onehot_t", [PARTS * G, 2, Q * 128], BF16)
        z = sb("gate_core", [128, 2, Q, W])
        lg = sb("gate_core_log", [128, 2, Q, W])
        sp_ = sb("gate_core_softplus", [128, Q, W])
        gt = sb("gate", [128, Q, D])
        msg = sb("gate_messages", [128, 2, Q, D])
        cur = sb("gate_group_sum", [128, 2, G])
        p_o = pb("gate_onehot_t_psum", [128, 512])
        p_e = pb("edge_t_psum", [128, 512])
        p_z = pb("gate_core_psum", [128, 2, 2, 512])
        p_a = pb("gate_sum_psum", [128, 512])
        names = ("weights_loaded", "weights_negated", "pool_step", "index_copied", "onehot_raw", "onehot", "onehot_t", "onehot_t_copied",
                 "edge_t", "edge_t_copied", "core_sum", "core_sum_read", "core_abs", "core_exp", "log", "softplus", "gate", "messages", "block_sum", "group_sum")
        (s_w, s_wn, s_p, s_ix, s_or, s_oh, s_T, s_oht, s_eT, s_et, s_z, s_zr, s_ab, s_ex, s_ln, s_sp, s_gt, s_msg, s_A, s_O) = (
            c["sems"].take("gate_" + n) for n in names)
        s_g = [c["sems"].take(f"gate_sources_gathered_{k}") for k in range(4)]
        s_hl = [c["sems"].take(f"gate_group_rows_loaded_{k}") for k in range(4)]
        s_e = [c["sems"].take(f"gate_edges_loaded_{k}") for k in range(4)]
        s_st = [c["sems"].take(f"gate_group_sum_stored_{k}") for k in range(2)]
        block = ctx.enter_context(nc.Block())

        @block.gpsimd
        def _(pool):
            nc.gpsimd.tensor_copy(ident_b[:, :], c["ident"][:, :]).then_inc(s_p, 1)
            gather_blocks(pool, nc, c, d["p_src"], idx, xj, s_ix, s_g, s_zr)

        @block.sync
        def _(sp):
            sp.dma_start(we[:, 0:D], w_f[2 * D:3 * D, :]).then_inc(s_w, 16)
            sp.dma_start(we[:, D:W], w_s[2 * D:3 * D, :]).then_inc(s_w, 16)

            def load(i, b):
                k = b % 4
                e0 = sp.value_load(c["first_i"][0:1, bass.ds(i * 4 + b, 1)], min_val=0, max_val=E)
                g = sp.value_load(c["group_i"][0:1, bass.ds(i * 4 + b, 1)], min_val=0, max_val=NG - 1)
                if b >= 4:
                    wait_alone(sp, c, s_z, done(i, b - 4))
                sp.dma_start(e_n[:, k, :, :], ea[bass.ds(e0, EB), :].rearrange("(p q) f -> p q f", q=Q)).then_inc(s_e[k], 16)
                for p in range(PARTS):
                    sp.dma_start(hl[p * G:(p + 1) * G, k, :], d["p_dst"][p, bass.ds(g * G, G), :]).then_inc(s_hl[k], 16)

            load(0, 0)
            load(0, 1)

            def move(i, b):
                load(i, b + 3)
                if b >= 1:
                    g = sp.value_load(c["group_i"][0:1, bass.ds(i * 4 + b - 1, 1)], min_val=0, max_val=NG - 1)
                    wait_alone(sp, c, s_O, done(i, b - 1))
                    if b >= 2:
                        wait_alone(sp, c, s_st[b % 2], (i * 2 + (b - 2) // 2 + 1) * 16)
                    sp.dma_start(c["h_t"][:, bass.ds(g * G, G)], cur[:, (b - 1) % 2, :]).then_inc(s_st[(b - 1) % 2], 16)
            quads = run_steps(sp, c, move)
            for k in (1, 2):
                wait_alone(sp, c, s_hl[k], (quads + 2) * 16 * PARTS)
            wait_alone(sp, c, s_e[2], (quads + 2) * 16)
            wait_alone(sp, c, s_st[0], (quads * 2 + 2) * 16)
            wait_alone(sp, c, s_st[1], (quads * 2 + 1) * 16)

        @block.tensor
        def _(pe):
            pe.wait_ge(s_wn, 1)
            pe.wait_ge(s_p, 1)

            def transposes(i, b):
                pe.wait_ge(s_oh, done(i, b))
                if b >= 1:
                    pe.wait_ge(s_oht, done(i, b - 1))
                for q in range(Q):
                    m = nc.tensor.matmul(p_o[0:PARTS * G, q * 128:(q + 1) * 128], ohb[:, b % 4, q, :], ident_b[:, :], start=True, stop=True)
                m.then_inc(s_T, 1)
                pe.wait_ge(s_e[b % 4], turns(i, b) * 16)
                if b >= 1:
                    pe.wait_ge(s_et, done(i, b - 1))
                for q in range(Q):
                    m = nc.tensor.transpose(p_e[:, q * 128:(q + 1) * 128], e_n[:, b % 4, q, :], c["ident"][:, :])
                m.then_inc(s_eT, 1)
            transposes(0, 0)

            def step(i, b):
                n, j = (b + 1) % 4, (b - 1) % 4
                pe.wait_ge(s_et, done(i, b + 1))
                pe.wait_ge(s_oht, done(i, b + 1))
                pe.wait_ge(s_hl[n], turns(i, b + 1) * 16 * PARTS)
                if b >= 1:
                    pe.wait_ge(s_zr, done(i, b - 1))
                for q in range(Q):
                    o = p_z[:, n % 2, q // 2, (q % 2) * W:(q % 2 + 1) * W]
                    nc.tensor.matmul(o, e_t[:, n % 2, q * 128:(q + 1) * 128], we[:, :], start=True, stop=False)
                    m = nc.tensor.matmul(o, oht[:, n % 2, q * 128:(q + 1) * 128], hl[:, n, :], start=False, stop=True)
                m.then_inc(s_z, 1)
                transposes(i, b + 2)
                if b >= 1:
                    pe.wait_ge(s_msg, done(i, b - 1))
                    if b >= 2:
                        pe.wait_ge(s_O, done(i, b - 2))
                    for q in range(Q):
                        m = nc.tensor.matmul(p_a[:, 0:G], msg[:, j % 2, q, :], oh[:, j, q, :], start=q == 0, stop=q == Q - 1)
                    m.then_inc(s_A, 1)
            run_steps(pe, c, step)

        @block.scalar
        def _(act):
            nc.scalar.preload_act_table_set(LOG_EXP)

            def copy_edges(i, b):
                wait_alone(act, c, s_eT, done(i, b))
                nc.scalar.copy(e_t[:, b % 2, :], p_e[:, :]).then_inc(s_et, 1)
            copy_edges(0, 0)

            def step(i, b):
                k, j = b % 4, (b - 1) % 4
                if b >= 0:
                    wait_alone(act, c, s_zr, done(i, b))
                    nc.scalar.activation(lg[:, k % 2, :, :], z[:, k % 2, :, :], ACT.Abs).then_inc(s_ab, 1)
                if b >= 1:
                    wait_alone(act, c, s_sp, done(i, b - 1))
                    nc.scalar.activation(gt[:, :, :], sp_[:, :, 0:D], ACT.Exp, scale=-1.0).then_inc(s_gt, 1)
                if b >= 0:
                    wait_alone(act, c, s_ab, done(i, b))
                    nc.scalar.activation(lg[:, k % 2, :, :], lg[:, k % 2, :, :], ACT.Exp, scale=-1.0).then_inc(s_ex, 1)
                    wait_alone(act, c, s_ex, done(i, b))
                    nc.scalar.activation(lg[:, k % 2, :, :], lg[:, k % 2, :, :], ACT.Ln, bias=1.0).then_inc(s_ln, 1)
                copy_edges(i, b + 2)
            run_steps(act, c, step)

        @block.vector
        def _(dve):
            vec = nc.vector
            dve.wait_ge(s_w, 32)
            vec.memset(cur[:, :, :], 0.0)
            vec.tensor_scalar(we[:, 0:D], we[:, 0:D], -1.0, None, ALU.mult).then_inc(s_wn, 1)
            dve.wait_ge(s_wn, 1)

            def onehots(i, b):
                vec.tensor_tensor(oh[:, b % 4, :, :], c["ramp"][:, 0:G].unsqueeze(1).to_broadcast([128, Q, G]),
                                  c["e_dst"][:, bass.ds((i * 4 + b) * Q, Q)].unsqueeze(2).to_broadcast([128, Q, G]), ALU.is_equal).then_inc(s_or, 1)
                dve.wait_ge(s_or, done(i, b))
                vec.tensor_copy(ohb[:, b % 4, :, :].rearrange("p q (a n) -> p q a n", a=PARTS),
                                oh[:, b % 4, :, :].unsqueeze(2).to_broadcast([128, Q, PARTS, G])).then_inc(s_oh, 1)

            def copy_onehots(i, b):
                dve.wait_ge(s_T, done(i, b))
                vec.tensor_copy(oht[:, b % 2, :], p_o[0:PARTS * G, :]).then_inc(s_oht, 1)
            onehots(0, 0)
            copy_onehots(0, 0)

            def step(i, b):
                n, j = (b + 1) % 4, (b - 1) % 4
                if b >= 1:
                    dve.wait_ge(s_ln, done(i, b - 1))
                    vec.scalar_tensor_tensor(sp_[:, :, :], z[:, j % 2, :, :], 0.0, lg[:, j % 2, :, :], ALU.max, ALU.add).then_inc(s_sp, 1)
                onehots(i, b + 2)
                if b >= 1:
                    dve.wait_ge(s_gt, done(i, b - 1))
                    vec.tensor_tensor(msg[:, j % 2, :, :], gt[:, :, :], sp_[:, :, D:W], ALU.mult).then_inc(s_msg, 1)
                dve.wait_ge(s_z, done(i, b + 1))
                dve.wait_ge(s_g[n], turns(i, b + 1) * 16 * Q)
                vec.tensor_tensor(z[:, n % 2, :, :], p_z[:, n % 2, :, :].rearrange("p a (b f) -> p (a b) f", b=2), xj[:, n, :, :], ALU.add).then_inc(s_zr, 1)
                copy_onehots(i, b + 2)
                if b >= 1:
                    dve.wait_ge(s_A, done(i, b - 1))
                    if b >= 3:
                        dve.wait_ge(s_st[j % 2], (i * 2 + (b - 3) // 2 + 1) * 16)
                    if b >= 2:
                        dve.wait_ge(s_O, done(i, b - 2))
                    vec.scalar_tensor_tensor(cur[:, j % 2, :], cur[:, 1 - j % 2, :], c["goes_on"][:, bass.ds(i * 4 + b - 1, 1)], p_a[:, 0:G],
                                             ALU.mult, ALU.add).then_inc(s_O, 1)
            run_steps(dve, c, step)


def residual_branch(nc, c, w_res, b_res, g_res, beta_res, out):
    from contextlib import ExitStack
    with ExitStack() as ctx:
        sb, pb = scope(nc, ctx)
        w = sb("res_w", [128, D])
        vecs = sb("res_vectors", [128, 3])
        y = sb("res_rows", [128, N])
        sq = sb("res_squares", [128, 2, BLK * G])
        eps = sb("res_eps", [128, 1])
        yp = pb("res_psum", [128, 2, 512])
        mp = pb("res_moments", [128, 2, 2, 512])
        s_ld, s_y, s_b, s_mn, s_ct, s_sq, s_vr, s_dv, s_v, s_nm, s_e, s_o = (c["sems"].take("res_" + n) for n in (
            "loaded", "multiplied", "biased", "mean_ready", "centred", "squares_ready", "variance_ready", "deviation_ready",
            "act_step", "normed", "eps_ready", "out"))
        block = ctx.enter_context(nc.Block())

        @block.sync
        def _(sp):
            sp.dma_start(w[:, :], w_res).then_inc(s_ld, 16)
            with nc.allow_non_contiguous_dma(reason="one value to a partition"):
                for r, row in enumerate((b_res, g_res, beta_res)):
                    sp.dma_start(vecs[:, r:r + 1], row.unsqueeze(1)).then_inc(s_ld, 16)

        @block.tensor
        def _(pe):
            pe.wait_ge(s_ld, 64)
            for b, (c0, n) in enumerate(COLS):
                if b >= 2:
                    pe.wait_ge(s_b, b - 1)
                nc.tensor.matmul(yp[:, b % 2, 0:n], w[:, :], c["x_t"][:, c0:c0 + n], start=True, stop=True).then_inc(s_y, 1)
            for b, (c0, n) in enumerate(COLS):
                pe.wait_ge(s_b, b + 1)
                if b >= 2:
                    pe.wait_ge(s_ct, b - 1)
                nc.tensor.matmul(mp[:, 0, b % 2, 0:n], c["mean_w"][:, :], y[:, c0:c0 + n], start=True, stop=True).then_inc(s_mn, 1)
                pe.wait_ge(s_sq, b + 1)
                if b >= 2:
                    pe.wait_ge(s_dv, b - 1)
                nc.tensor.matmul(mp[:, 1, b % 2, 0:n], c["mean_w"][:, :], sq[:, b % 2, 0:n], start=True, stop=True).then_inc(s_vr, 1)

        @block.scalar
        def _(act):
            nc.scalar.preload_act_table_set(LOG_EXP)
            o = Order(act, s_v)
            act.wait_ge(s_ld, 64)
            act.wait_ge(s_e, 1)
            for b, (c0, n) in enumerate(COLS):
                act.wait_ge(s_y, b + 1)
                nc.scalar.activation(y[:, c0:c0 + n], yp[:, b % 2, 0:n], ACT.Identity, bias=vecs[:, 0:1]).then_inc(s_b, 1)
            for b, (c0, n) in enumerate(COLS):
                act.wait_ge(s_ct, b + 1)
                if b >= 2:
                    act.wait_ge(s_nm, b - 1)
                nc.scalar.activation(sq[:, b % 2, 0:n], y[:, c0:c0 + n], ACT.Square).then_inc(s_sq, 1)
                act.wait_ge(s_vr, b + 1)
                o.link(nc.scalar.activation(sq[:, b % 2, 0:n], mp[:, 1, b % 2, 0:n], ACT.Ln, bias=eps[:, 0:1]))
                nc.scalar.activation(sq[:, b % 2, 0:n], sq[:, b % 2, 0:n], ACT.Exp, scale=-0.5).then_inc(s_dv, 1)
            for b, (c0, n) in enumerate(COLS):
                act.wait_ge(s_nm, b + 1)
                nc.scalar.activation(out[:, c0:c0 + n], y[:, c0:c0 + n], ACT.Gelu, bias=vecs[:, 2:3], scale=vecs[:, 1:2]).then_inc(s_o, 1)

        @block.vector
        def _(dve):
            nc.vector.memset(eps[:, :], EPS).then_inc(s_e, 1)
            for b, (c0, n) in enumerate(COLS):
                cols = slice(c0, c0 + n)
                dve.wait_ge(s_mn, b + 1)
                nc.vector.tensor_tensor(y[:, cols], y[:, cols], mp[:, 0, b % 2, 0:n], ALU.subtract).then_inc(s_ct, 1)
                dve.wait_ge(s_dv, b + 1)
                nc.vector.tensor_tensor(y[:, cols], y[:, cols], sq[:, b % 2, 0:n], ALU.mult).then_inc(s_nm, 1)


def store_nodes(nc, c, out):
    from contextlib import ExitStack
    with ExitStack() as ctx:
        sb, pb = scope(nc, ctx)
        on = sb("out_nodes", [T, NS, D])
        pt = pb("out_psum", [T, 2, 4, D])
        s_t, s_c, s_st = (c["sems"].take("out_" + n) for n in ("tiles_transposed", "tiles_copied", "stored"))
        block = ctx.enter_context(nc.Block())

        @block.tensor
        def _(pe):
            for s in range(NS):
                if s % 4 == 0 and s >= 8:
                    pe.wait_ge(s_c, s // 4 - 1)
                t = nc.tensor.transpose(pt[:, s // 4 % 2, s % 4, :], c["x_t"][:, s * T:(s + 1) * T], c["ident"][:, :])
                if s % 4 == 3 or s == NS - 1:
                    t.then_inc(s_t, 1)

        @block.vector
        def _(dve):
            for q in range(-(-NS // 4)):
                n = min(4, NS - 4 * q)
                dve.wait_ge(s_t, q + 1)
                nc.vector.tensor_copy(on[:, 4 * q:4 * q + n, :], pt[:, q % 2, 0:n, :]).then_inc(s_c, 1)

        @block.sync
        def _(sp):
            sp.wait_ge(s_c, -(-NS // 4))
            sp.dma_start(out.rearrange("(s r) f -> r s f", r=T), on[:, :, :]).then_inc(s_st, 16)
            sp.wait_ge(s_st, 16)


def graph_network(nc, a, out):
    c = shared_tensors(nc)
    c["sems"].begin(c)
    d = dram_scratch(nc)
    constants(nc, c)
    prepare(nc, c, d, a["src"], a["dst"], a["edge_weight"])
    build_adjacency(nc, c, d)
    degrees(nc, c, d)
    c["sems"].end()
    load_transposed(nc, c, "x", a["x"], c["x_t"])

    gcn_layers(nc, c, d, "gcn", [a[f"L0_gnn_W{i}"] for i in (1, 2, 3)], [a[f"L0_gnn_b{i}"] for i in (1, 2, 3)], None)
    add_and_norm(nc, c, "norm0", [c["x_t"], c["h_t"]])
    c["sems"].end()

    node_tables(nc, c, "gat_tables", [([(a["L1_gnn_weight_l"], (0, D), False)], [], d["h_l"]),
                                      ([(a["L1_gnn_weight_r"], (0, D), False)], [], d["h_r"])])
    attention(nc, c, d, a["L1_gnn_att"])
    load_transposed(nc, c, "gat", d["gat"], c["h_t"], a["L1_gnn_bias"])
    add_and_norm(nc, c, "norm1", [c["x_t"], c["h_t"]])
    c["sems"].end()

    wf, ws = a["L2_gnn_W_f"], a["L2_gnn_W_s"]
    node_tables(nc, c, "gate_tables", [([(wf[0:D, :], (0, D), True), (ws[0:D, :], (D, 2 * D), False)],
                                        [(a["L2_gnn_b_f"], (0, D), True), (a["L2_gnn_b_s"], (D, 2 * D), False)], d["p_dst"]),
                                       ([(wf[D:2 * D, :], (0, D), True), (ws[D:2 * D, :], (D, 2 * D), False)], [], d["p_src"])])
    gated_conv(nc, c, d, a["edge_attr_128"], wf, ws)
    add_and_norm(nc, c, "norm2", [c["x_t"], c["x_t"], c["h_t"]])
    c["sems"].end()

    L = a["L3_gnn_conv_W"].shape[0]
    rows = {n: [a["L3_gnn_" + n][l] for l in range(L)] for n in ("conv_W", "conv_b", "ln_g", "ln_b")}
    gcn_layers(nc, c, d, "deep", rows["conv_W"], rows["conv_b"], (rows["ln_g"], rows["ln_b"]))
    with nc.sbuf_tensor("identity_branch", [128, N], F32) as branch:
        residual_branch(nc, c, a["L3_gnn_res_W"], a["L3_gnn_res_b"], a["L3_gnn_res_g"], a["L3_gnn_res_beta"], branch)
        add_and_norm(nc, c, "norm3", [c["x_t"], c["h_t"], branch])
    store_nodes(nc, c, out)


_INS = ['x', 'src', 'dst', 'edge_attr_128', 'edge_weight', 'L0_gnn_W1', 'L0_gnn_b1', 'L0_gnn_W2', 'L0_gnn_b2', 'L0_gnn_W3', 'L0_gnn_b3',
        'L1_gnn_weight_l', 'L1_gnn_weight_r', 'L1_gnn_att', 'L1_gnn_bias', 'L2_gnn_W_f', 'L2_gnn_b_f', 'L2_gnn_W_s', 'L2_gnn_b_s',
        'L3_gnn_conv_W', 'L3_gnn_conv_b', 'L3_gnn_ln_g', 'L3_gnn_ln_b', 'L3_gnn_res_W', 'L3_gnn_res_b', 'L3_gnn_res_g', 'L3_gnn_res_beta']


def kernel(**inputs):
    import numpy as _np
    import concourse.bacc as _bacc
    from concourse import mybir as _mybir
    from concourse.bass_utils import run_bass_kernel_spmd as _run

    nc = _bacc.Bacc("TRN2", target_bir_lowering=False, num_devices=1)
    arrays, args = {}, {}
    for name in _INS:
        a = _np.ascontiguousarray(inputs[name])
        if name == 'edge_attr_128':
            rows = _np.zeros((E + EB, D), a.dtype)
            rows[:E] = a
            a = rows
        arrays[f"in_{name}_dram"] = a
        args[name] = nc.dram_tensor(f"in_{name}_dram", a.shape, _mybir.dt.from_np(a.dtype), kind="ExternalInput").ap()
    out = nc.dram_tensor("out_dram", (N, D), F32, kind="ExternalOutput").ap()
    graph_network(nc, args, out)
    r = _run(nc, [arrays], core_ids=[0])
    return r.results[0]["out_dram"]
```
